# Optimizing a Trainium2 kernel written in Bass

```python
import numpy as np
import jax
import jax.numpy as jnp

def _softmax(x, axis=-1):
    return jax.nn.softmax(x, axis=axis)
def _gelu(x):
    return jax.nn.gelu(x, approximate=True)
def _silu(x):
    return jax.nn.silu(x)
def _sigmoid(x):
    return jax.nn.sigmoid(x)
def _layernorm(x, axis=-1, eps=1e-5):
    m = jnp.mean(x, axis=axis, keepdims=True)
    v = jnp.var(x, axis=axis, keepdims=True)
    return (x - m) / jnp.sqrt(v + eps)
def _scatter_add(tgt, idx, src, axis=0):
    return tgt.at[idx].add(src)
def _segment_sum(src, seg, n):
    return jax.ops.segment_sum(src, seg, n)

kernel_name = 'mk_conv_seq_d4_conv_nchw64_5036ca'

def setup_inputs(seed: int = 0):
    np.random.seed(seed)
    _w = jnp.asarray
    def _rec_inputs():
        import jax
        import jax.numpy as jnp
        _gk = jax.random.key(seed)
        x = -0.0002928 + 1 * jax.random.normal(jax.random.fold_in(_gk, 1), (4, 64, 128, 128), jnp.float32)
        return x
    x = _rec_inputs()
    def _L0_conv_setup():
        import jax, jax.numpy as jnp
        import numpy as np
        from jax import lax
        B, C, H, W = (4, 64, 128, 128)
        NUM_HEADS = 4
        D = C // NUM_HEADS
        SR1, SR2 = (8, 16)
        RED = 4
        EPS = 1e-05

        def _layernorm(x, gamma, beta):
            mu = jnp.mean(x, axis=-1, keepdims=True)
            var = jnp.var(x, axis=-1, keepdims=True)
            return (x - mu) * lax.rsqrt(var + EPS) * gamma + beta

        def _conv(x, w, stride, pad='VALID', groups=1):
            return lax.conv_general_dilated(x, w, (stride, stride), pad, dimension_numbers=('NCHW', 'OIHW', 'NCHW'), feature_group_count=groups)

        def _forward(x, fg_w1, fg_w2, q_w, q_b, sr1_w, sr1_b, ln1_g, ln1_b, kv1_w, kv1_b, sr2_w, sr2_b, ln2_g, ln2_b, kv2_w, kv2_b, dw_w, proj_w, proj_b):
            b, c, h, w = x.shape
            n = h * w
            spec = jnp.fft.rfft2(x, norm='ortho')
            mag = jnp.abs(spec)
            hid = jax.nn.gelu(jnp.einsum('bchw,oc->bohw', mag, fg_w1), approximate=False)
            gate = jax.nn.sigmoid(jnp.einsum('bchw,oc->bohw', hid, fg_w2))
            x_gated = jnp.fft.irfft2(spec * gate, s=(h, w), norm='ortho')
            xf = x + x_gated
            x_flat = xf.reshape(b, c, n).transpose(0, 2, 1)
            q = (x_flat @ q_w + q_b).reshape(b, n, NUM_HEADS, D).transpose(0, 2, 1, 3)

            def kv_path(sr_w, sr_b, ln_g, ln_b, kv_w, kv_b, stride):
                xs = _conv(xf, sr_w, stride) + sr_b[None, :, None, None]
                _, _, hs, ws = xs.shape
                xs_flat = _layernorm(xs.reshape(b, c, hs * ws).transpose(0, 2, 1), ln_g, ln_b)
                kv = xs_flat @ kv_w + kv_b
                k, v = (kv[..., :c], kv[..., c:])
                v_sp = v.transpose(0, 2, 1).reshape(b, c, hs, ws)
                v_sp = _conv(v_sp, dw_w, 1, pad=((1, 1), (1, 1)), groups=c)
                v = v_sp.reshape(b, c, hs * ws).transpose(0, 2, 1)
                return (k, v)
            k1, v1 = kv_path(sr1_w, sr1_b, ln1_g, ln1_b, kv1_w, kv1_b, SR1)
            k2, v2 = kv_path(sr2_w, sr2_b, ln2_g, ln2_b, kv2_w, kv2_b, SR2)
            k = jnp.concatenate([k1, k2], axis=1)
            v = jnp.concatenate([v1, v2], axis=1)
            nk = k.shape[1]
            k = k.reshape(b, nk, NUM_HEADS, D).transpose(0, 2, 1, 3)
            v = v.reshape(b, nk, NUM_HEADS, D).transpose(0, 2, 1, 3)
            scale = D ** (-0.5)
            attn = jax.nn.softmax(jnp.einsum('bhqd,bhkd->bhqk', q, k) * scale, axis=-1)
            out = jnp.einsum('bhqk,bhkd->bhqd', attn, v)
            out = out.transpose(0, 2, 1, 3).reshape(b, n, c)
            out = out @ proj_w + proj_b
            return out.transpose(0, 2, 1).reshape(b, c, h, w) + x
        key = jax.random.key(seed)
        ks = jax.random.split(key, 20)
        g = lambda i, shape, s=0.02: jax.random.normal(ks[i], shape, dtype=jnp.float32) * s
        inp = {'x': jax.random.normal(ks[0], (B, C, H, W), dtype=jnp.float32), 'fg_w1': g(1, (C // RED, C)), 'fg_w2': g(2, (C, C // RED)), 'q_w': g(3, (C, C)), 'q_b': g(4, (C,)), 'sr1_w': g(5, (C, C, SR1, SR1)), 'sr1_b': g(6, (C,)), 'ln1_g': 1.0 + g(7, (C,), 0.1), 'ln1_b': g(8, (C,), 0.1), 'kv1_w': g(9, (C, 2 * C)), 'kv1_b': g(10, (2 * C,)), 'sr2_w': g(11, (C, C, SR2, SR2)), 'sr2_b': g(12, (C,)), 'ln2_g': 1.0 + g(13, (C,), 0.1), 'ln2_b': g(14, (C,), 0.1), 'kv2_w': g(15, (C, 2 * C)), 'kv2_b': g(16, (2 * C,)), 'dw_w': g(17, (C, 1, 3, 3)), 'proj_w': g(18, (C, C)), 'proj_b': g(19, (C,))}
        return inp
    _L0_conv_all = _L0_conv_setup()
    _L0_conv_in = {k: v for k, v in _L0_conv_all.items() if k in ('fg_w1', 'fg_w2', 'q_w', 'q_b', 'sr1_w', 'sr1_b', 'ln1_g', 'ln1_b', 'kv1_w', 'kv1_b', 'sr2_w', 'sr2_b', 'ln2_g', 'ln2_b', 'kv2_w', 'kv2_b', 'dw_w', 'proj_w', 'proj_b', )}
    del _L0_conv_all

    def _L1_conv_setup():
        import jax, jax.numpy as jnp
        import numpy as np
        MODES = 32
        NUM_BLOCKS = 4
        NUM_EXPERTS = 16
        TOP_K = 4
        TEMPERATURE = 2.0

        def _gelu(t):
            return jax.nn.gelu(t, approximate=False)

        def _c1(x, w, b):
            return jnp.einsum('bchw,oc->bohw', x, w) + b[None, :, None, None]

        def _group_norm(x, w, b, groups=8, eps=1e-05):
            B, C, H, W = x.shape
            xg = x.reshape(B, groups, C // groups, H, W)
            mu = xg.mean(axis=(2, 3, 4), keepdims=True)
            var = xg.var(axis=(2, 3, 4), keepdims=True)
            xn = ((xg - mu) * jax.lax.rsqrt(var + eps)).reshape(B, C, H, W)
            return xn * w[None, :, None, None] + b[None, :, None, None]

        def _bn_eval(x, g, b, rm, rv, eps=1e-05):
            return (x - rm) * jax.lax.rsqrt(rv + eps) * g + b

        def _afno(x, w1, b1, w2, b2):
            B, C, H, W = x.shape
            bs = C // NUM_BLOCKS
            xp = x.transpose(0, 2, 3, 1)
            xf = jnp.fft.rfft2(xp, axes=(1, 2), norm='ortho')
            Wf = xf.shape[2]
            xf = xf.reshape(B, H, Wf, NUM_BLOCKS, bs)
            m = MODES
            xm = xf[:, :m, :m]
            xr, xi = (xm.real, xm.imag)
            o1r = _gelu(jnp.einsum('bhwni,nio->bhwno', xr, w1[0]) - jnp.einsum('bhwni,nio->bhwno', xi, w1[1]) + b1[0])
            o1i = _gelu(jnp.einsum('bhwni,nio->bhwno', xi, w1[0]) + jnp.einsum('bhwni,nio->bhwno', xr, w1[1]) + b1[1])
            o2r = jnp.einsum('bhwni,nio->bhwno', o1r, w2[0]) - jnp.einsum('bhwni,nio->bhwno', o1i, w2[1]) + b2[0]
            o2i = jnp.einsum('bhwni,nio->bhwno', o1i, w2[0]) + jnp.einsum('bhwni,nio->bhwno', o1r, w2[1]) + b2[1]
            of = jnp.zeros((B, H, Wf, NUM_BLOCKS, bs), dtype=xf.dtype)
            of = of.at[:, :m, :m].set(o2r + 1j * o2i)
            out = jnp.fft.irfft2(of.reshape(B, H, Wf, C), s=(H, W), axes=(1, 2), norm='ortho')
            out = out + xp
            return out.transpose(0, 3, 1, 2)

        def _forward(x, gn1_w, gn1_b, afno_w1, afno_b1, afno_w2, afno_b2, gn2_w, gn2_b, fe_w, fe_b, g1_w, g1_b, bn1_g, bn1_b, bn1_rm, bn1_rv, ca_w1, ca_b1, ca_w2, ca_b2, g2_w, g2_b, bn2_g, bn2_b, bn2_rm, bn2_rv, g3_w, g3_b, shared_w, shared_b, expert_w, expert_b):
            residual = x
            h = _group_norm(x, gn1_w, gn1_b)
            h = _afno(h, afno_w1, afno_b1, afno_w2, afno_b2)
            h = h + residual
            residual = h
            h = _group_norm(h, gn2_w, gn2_b)
            feats = _gelu(_c1(h, fe_w, fe_b))
            shared = jnp.zeros_like(h)
            for s in range(shared_w.shape[0]):
                shared = shared + _gelu(_c1(feats, shared_w[s], shared_b[s])) / shared_w.shape[0]
            gf = feats.mean(axis=(2, 3))
            h1 = _gelu(_bn_eval(gf @ g1_w.T + g1_b, bn1_g, bn1_b, bn1_rm, bn1_rv))
            a = _gelu(h1 @ ca_w1.T + ca_b1) @ ca_w2.T + ca_b2
            h1 = h1 * jax.nn.sigmoid(2.0 * a)
            h2 = _gelu(_bn_eval(h1 @ g2_w.T + g2_b, bn2_g, bn2_b, bn2_rm, bn2_rv))
            scores = h2 @ g3_w.T + g3_b
            vals, idx = jax.lax.top_k(scores, TOP_K)
            wts = jax.nn.softmax(vals / TEMPERATURE, axis=1)
            B = x.shape[0]
            gate_w = jnp.zeros((B, NUM_EXPERTS), x.dtype).at[jnp.arange(B)[:, None], idx].add(wts)
            out = shared
            for e in range(NUM_EXPERTS):
                out = out + _gelu(_c1(feats, expert_w[e], expert_b[e])) * gate_w[:, e][:, None, None, None]
            return out + residual
        key = jax.random.key(seed)
        ks = jax.random.split(key, 16)
        B, C, H, W = (8, 64, 192, 192)
        nb = NUM_BLOCKS
        bs = C // nb
        E = NUM_EXPERTS
        scale = 1.0 / (bs * bs)
        f32 = jnp.float32
        n = lambda k, shape: jax.random.normal(k, shape, f32) * 0.02
        return {'x': jax.random.normal(ks[0], (B, C, H, W), f32), 'gn1_w': jnp.ones((C,), f32), 'gn1_b': jnp.zeros((C,), f32), 'afno_w1': jax.random.uniform(ks[1], (2, nb, bs, bs), f32) * scale, 'afno_b1': jax.random.uniform(ks[2], (2, nb, bs), f32) * scale, 'afno_w2': jax.random.uniform(ks[3], (2, nb, bs, bs), f32) * scale, 'afno_b2': jax.random.uniform(ks[4], (2, nb, bs), f32) * scale, 'gn2_w': jnp.ones((C,), f32), 'gn2_b': jnp.zeros((C,), f32), 'fe_w': n(ks[5], (C, C)), 'fe_b': jnp.zeros((C,), f32), 'g1_w': n(ks[6], (2 * C, C)), 'g1_b': jnp.zeros((2 * C,), f32), 'bn1_g': jnp.ones((2 * C,), f32), 'bn1_b': jnp.zeros((2 * C,), f32), 'bn1_rm': jnp.zeros((2 * C,), f32), 'bn1_rv': jnp.ones((2 * C,), f32), 'ca_w1': n(ks[7], (2 * C // 16, 2 * C)), 'ca_b1': jnp.zeros((2 * C // 16,), f32), 'ca_w2': n(ks[8], (2 * C, 2 * C // 16)), 'ca_b2': jnp.zeros((2 * C,), f32), 'g2_w': n(ks[9], (C, 2 * C)), 'g2_b': jnp.zeros((C,), f32), 'bn2_g': jnp.ones((C,), f32), 'bn2_b': jnp.zeros((C,), f32), 'bn2_rm': jnp.zeros((C,), f32), 'bn2_rv': jnp.ones((C,), f32), 'g3_w': n(ks[10], (E, C)), 'g3_b': jnp.zeros((E,), f32), 'shared_w': n(ks[11], (2, C, C)), 'shared_b': jnp.zeros((2, C), f32), 'expert_w': n(ks[12], (E, C, C)), 'expert_b': jnp.zeros((E, C), f32)}
    _L1_conv_all = _L1_conv_setup()
    _L1_conv_in = {k: v for k, v in _L1_conv_all.items() if k in ('gn1_w', 'gn1_b', 'afno_w1', 'afno_b1', 'afno_w2', 'afno_b2', 'gn2_w', 'gn2_b', 'fe_w', 'fe_b', 'g1_w', 'g1_b', 'bn1_g', 'bn1_b', 'bn1_rm', 'bn1_rv', 'ca_w1', 'ca_b1', 'ca_w2', 'ca_b2', 'g2_w', 'g2_b', 'bn2_g', 'bn2_b', 'bn2_rm', 'bn2_rv', 'g3_w', 'g3_b', 'shared_w', 'shared_b', 'expert_w', 'expert_b', )}
    del _L1_conv_all

    def _L2_conv_setup():
        import jax, jax.numpy as jnp
        import numpy as np
        from jax import lax
        CUTOFF = 0.25
        SIGMA = 1.0
        RADIUS = 4

        def _gauss_kernel(sigma=SIGMA, radius=RADIUS):
            x = np.arange(-radius, radius + 1, dtype=np.float32)
            k = np.exp(-0.5 * (x / sigma) ** 2)
            return jnp.asarray(k / k.sum())

        def _blur_axis(x, axis, kernel):
            r = (kernel.shape[0] - 1) // 2
            pad = [(0, 0)] * x.ndim
            pad[axis] = (r, r)
            xp = jnp.pad(x, pad, mode='edge')
            out = jnp.zeros_like(x)
            for i in range(kernel.shape[0]):
                out = out + kernel[i] * lax.slice_in_dim(xp, i, i + x.shape[axis], axis=axis)
            return out

        def gaussian_smoothing_4d(x):
            k = _gauss_kernel().astype(x.dtype)
            for ax in range(4):
                x = _blur_axis(x, ax, k)
            return x

        def dht_2d(x):
            return (jnp.fft.fftn(x, axes=(2, 3)).real - jnp.fft.fftn(jnp.flip(x, axis=(2, 3)), axes=(2, 3)).imag).astype(x.dtype)

        def _neg_k(a):
            return jnp.roll(jnp.flip(a, axis=(-2, -1)), shift=(1, 1), axis=(-2, -1))

        def compl_mul2d(x1, x2):
            x1n, x2n = (_neg_k(x1), _neg_k(x2))
            e = lambda a, b: jnp.einsum('bixy,ioxy->boxy', a, b)
            return 0.5 * (e(x1, x2) - e(x1n, x2n) + e(x1, x2n) + e(x1n, x2))
        key = jax.random.key(seed)
        k1, k2 = jax.random.split(key)
        B, Cin, Cout, H, W, M1, M2 = (16, 64, 64, 128, 128, 20, 20)
        x = jax.random.normal(k1, (B, Cin, H, W), dtype=jnp.float32)
        scale = 1.0 / (Cin * Cout)
        w1 = scale * jax.random.uniform(k2, (Cin, Cout, M1, M2), dtype=jnp.float32)
        return {'x': x, 'w1': w1}
    _L2_conv_all = _L2_conv_setup()
    _L2_conv_in = {k: v for k, v in _L2_conv_all.items() if k in ('w1', )}
    del _L2_conv_all

    def _L3_conv_setup():
        import jax, jax.numpy as jnp
        from jax import lax
        import numpy as np
        D_STATE = 16
        D_CONV = 4
        GROUPS = 4
        TOKEN = 8

        def group_norm(x, w, b, groups, eps=1e-05):
            B, C, H, W = x.shape
            xg = x.reshape(B, groups, C // groups, H, W)
            mu = xg.mean(axis=(2, 3, 4), keepdims=True)
            var = ((xg - mu) ** 2).mean(axis=(2, 3, 4), keepdims=True)
            xg = (xg - mu) / jnp.sqrt(var + eps)
            return xg.reshape(B, C, H, W) * w[None, :, None, None] + b[None, :, None, None]

        def mamba_fwd(x, in_w, conv_w, conv_b, xproj_w, dt_w, dt_b, A_log, D, out_w):
            Bsz, L, _ = x.shape
            d_inner = in_w.shape[0] // 2
            dt_rank = dt_w.shape[1]
            xz = x @ in_w.T
            xi, z = jnp.split(xz, 2, axis=-1)
            xc = lax.conv_general_dilated(xi.transpose(0, 2, 1), conv_w, window_strides=(1,), padding=[(D_CONV - 1, 0)], dimension_numbers=('NCH', 'OIH', 'NCH'), feature_group_count=d_inner)
            xc = jax.nn.silu(xc + conv_b[None, :, None]).transpose(0, 2, 1)
            xdb = xc @ xproj_w.T
            dt, Bm, Cm = jnp.split(xdb, [dt_rank, dt_rank + D_STATE], axis=-1)
            dt = jax.nn.softplus(dt @ dt_w.T + dt_b)
            A = -jnp.exp(A_log)
            dA = jnp.exp(dt[..., None] * A)
            dBx = dt[..., None] * Bm[:, :, None, :] * xc[..., None]

            def step(h, inp):
                dA_t, dBx_t, C_t = inp
                h = dA_t * h + dBx_t
                y = jnp.einsum('bds,bs->bd', h, C_t)
                return (h, y)
            h0 = jnp.zeros((Bsz, d_inner, D_STATE), dtype=x.dtype)
            _, ys = lax.scan(step, h0, (dA.transpose(1, 0, 2, 3), dBx.transpose(1, 0, 2, 3), Cm.transpose(1, 0, 2)))
            y = ys.transpose(1, 0, 2) + xc * D
            y = y * jax.nn.silu(z)
            return y @ out_w.T
        key = jax.random.key(seed)
        ks = iter(jax.random.split(key, 48))

        def rn(shape, s=0.02):
            return jax.random.normal(next(ks), shape, dtype=jnp.float32) * s
        B, C, H, W = (4, 64, 64, 64)
        inp = {'x': jax.random.normal(next(ks), (B, C, H, W), dtype=jnp.float32)}

        def mamba_params(prefix, d_model):
            d_inner = 2 * d_model
            dt_rank = -(-d_model // 16)
            inp[prefix + '_in_w'] = rn((2 * d_inner, d_model))
            inp[prefix + '_conv_w'] = rn((d_inner, 1, D_CONV))
            inp[prefix + '_conv_b'] = rn((d_inner,))
            inp[prefix + '_xproj_w'] = rn((dt_rank + 2 * D_STATE, d_inner))
            inp[prefix + '_dt_w'] = rn((d_inner, dt_rank))
            inp[prefix + '_dt_b'] = rn((d_inner,)) + 0.5
            inp[prefix + '_A_log'] = jnp.log(jnp.tile(jnp.arange(1, D_STATE + 1, dtype=jnp.float32), (d_inner, 1)))
            inp[prefix + '_D'] = jnp.ones((d_inner,), jnp.float32)
            inp[prefix + '_out_w'] = rn((d_model, d_inner))
        mamba_params('spa', C)
        mamba_params('spe', -(-C // TOKEN))
        inp['spa_gn_w'] = jnp.ones((C,), jnp.float32)
        inp['spa_gn_b'] = jnp.zeros((C,), jnp.float32)
        inp['spe_gn_w'] = jnp.ones((C,), jnp.float32)
        inp['spe_gn_b'] = jnp.zeros((C,), jnp.float32)
        inp['att_w'] = jnp.full((2,), 0.5, jnp.float32)
        return inp
    _L3_conv_all = _L3_conv_setup()
    _L3_conv_in = {k: v for k, v in _L3_conv_all.items() if k in ('spa_in_w', 'spa_conv_w', 'spa_conv_b', 'spa_xproj_w', 'spa_dt_w', 'spa_dt_b', 'spa_A_log', 'spa_D', 'spa_out_w', 'spe_in_w', 'spe_conv_w', 'spe_conv_b', 'spe_xproj_w', 'spe_dt_w', 'spe_dt_b', 'spe_A_log', 'spe_D', 'spe_out_w', 'spa_gn_w', 'spa_gn_b', 'spe_gn_w', 'spe_gn_b', 'att_w', )}
    del _L3_conv_all

    return {
        "x": x,
        "L0_conv_fg_w1": _L0_conv_in["fg_w1"],
        "L0_conv_fg_w2": _L0_conv_in["fg_w2"],
        "L0_conv_q_w": _L0_conv_in["q_w"],
        "L0_conv_q_b": _L0_conv_in["q_b"],
        "L0_conv_sr1_w": _L0_conv_in["sr1_w"],
        "L0_conv_sr1_b": _L0_conv_in["sr1_b"],
        "L0_conv_ln1_g": _L0_conv_in["ln1_g"],
        "L0_conv_ln1_b": _L0_conv_in["ln1_b"],
        "L0_conv_kv1_w": _L0_conv_in["kv1_w"],
        "L0_conv_kv1_b": _L0_conv_in["kv1_b"],
        "L0_conv_sr2_w": _L0_conv_in["sr2_w"],
        "L0_conv_sr2_b": _L0_conv_in["sr2_b"],
        "L0_conv_ln2_g": _L0_conv_in["ln2_g"],
        "L0_conv_ln2_b": _L0_conv_in["ln2_b"],
        "L0_conv_kv2_w": _L0_conv_in["kv2_w"],
        "L0_conv_kv2_b": _L0_conv_in["kv2_b"],
        "L0_conv_dw_w": _L0_conv_in["dw_w"],
        "L0_conv_proj_w": _L0_conv_in["proj_w"],
        "L0_conv_proj_b": _L0_conv_in["proj_b"],
        "L1_conv_gn1_w": _L1_conv_in["gn1_w"],
        "L1_conv_gn1_b": _L1_conv_in["gn1_b"],
        "L1_conv_afno_w1": _L1_conv_in["afno_w1"],
        "L1_conv_afno_b1": _L1_conv_in["afno_b1"],
        "L1_conv_afno_w2": _L1_conv_in["afno_w2"],
        "L1_conv_afno_b2": _L1_conv_in["afno_b2"],
        "L1_conv_gn2_w": _L1_conv_in["gn2_w"],
        "L1_conv_gn2_b": _L1_conv_in["gn2_b"],
        "L1_conv_fe_w": _L1_conv_in["fe_w"],
        "L1_conv_fe_b": _L1_conv_in["fe_b"],
        "L1_conv_g1_w": _L1_conv_in["g1_w"],
        "L1_conv_g1_b": _L1_conv_in["g1_b"],
        "L1_conv_bn1_g": _L1_conv_in["bn1_g"],
        "L1_conv_bn1_b": _L1_conv_in["bn1_b"],
        "L1_conv_bn1_rm": _L1_conv_in["bn1_rm"],
        "L1_conv_bn1_rv": _L1_conv_in["bn1_rv"],
        "L1_conv_ca_w1": _L1_conv_in["ca_w1"],
        "L1_conv_ca_b1": _L1_conv_in["ca_b1"],
        "L1_conv_ca_w2": _L1_conv_in["ca_w2"],
        "L1_conv_ca_b2": _L1_conv_in["ca_b2"],
        "L1_conv_g2_w": _L1_conv_in["g2_w"],
        "L1_conv_g2_b": _L1_conv_in["g2_b"],
        "L1_conv_bn2_g": _L1_conv_in["bn2_g"],
        "L1_conv_bn2_b": _L1_conv_in["bn2_b"],
        "L1_conv_bn2_rm": _L1_conv_in["bn2_rm"],
        "L1_conv_bn2_rv": _L1_conv_in["bn2_rv"],
        "L1_conv_g3_w": _L1_conv_in["g3_w"],
        "L1_conv_g3_b": _L1_conv_in["g3_b"],
        "L1_conv_shared_w": _L1_conv_in["shared_w"],
        "L1_conv_shared_b": _L1_conv_in["shared_b"],
        "L1_conv_expert_w": _L1_conv_in["expert_w"],
        "L1_conv_expert_b": _L1_conv_in["expert_b"],
        "L2_conv_w1": _L2_conv_in["w1"],
        "L3_conv_spa_in_w": _L3_conv_in["spa_in_w"],
        "L3_conv_spa_conv_w": _L3_conv_in["spa_conv_w"],
        "L3_conv_spa_conv_b": _L3_conv_in["spa_conv_b"],
        "L3_conv_spa_xproj_w": _L3_conv_in["spa_xproj_w"],
        "L3_conv_spa_dt_w": _L3_conv_in["spa_dt_w"],
        "L3_conv_spa_dt_b": _L3_conv_in["spa_dt_b"],
        "L3_conv_spa_A_log": _L3_conv_in["spa_A_log"],
        "L3_conv_spa_D": _L3_conv_in["spa_D"],
        "L3_conv_spa_out_w": _L3_conv_in["spa_out_w"],
        "L3_conv_spe_in_w": _L3_conv_in["spe_in_w"],
        "L3_conv_spe_conv_w": _L3_conv_in["spe_conv_w"],
        "L3_conv_spe_conv_b": _L3_conv_in["spe_conv_b"],
        "L3_conv_spe_xproj_w": _L3_conv_in["spe_xproj_w"],
        "L3_conv_spe_dt_w": _L3_conv_in["spe_dt_w"],
        "L3_conv_spe_dt_b": _L3_conv_in["spe_dt_b"],
        "L3_conv_spe_A_log": _L3_conv_in["spe_A_log"],
        "L3_conv_spe_D": _L3_conv_in["spe_D"],
        "L3_conv_spe_out_w": _L3_conv_in["spe_out_w"],
        "L3_conv_spa_gn_w": _L3_conv_in["spa_gn_w"],
        "L3_conv_spa_gn_b": _L3_conv_in["spa_gn_b"],
        "L3_conv_spe_gn_w": _L3_conv_in["spe_gn_w"],
        "L3_conv_spe_gn_b": _L3_conv_in["spe_gn_b"],
        "L3_conv_att_w": _L3_conv_in["att_w"],
    }

def reference(x, L0_conv_fg_w1, L0_conv_fg_w2, L0_conv_q_w, L0_conv_q_b, L0_conv_sr1_w, L0_conv_sr1_b, L0_conv_ln1_g, L0_conv_ln1_b, L0_conv_kv1_w, L0_conv_kv1_b, L0_conv_sr2_w, L0_conv_sr2_b, L0_conv_ln2_g, L0_conv_ln2_b, L0_conv_kv2_w, L0_conv_kv2_b, L0_conv_dw_w, L0_conv_proj_w, L0_conv_proj_b, L1_conv_gn1_w, L1_conv_gn1_b, L1_conv_afno_w1, L1_conv_afno_b1, L1_conv_afno_w2, L1_conv_afno_b2, L1_conv_gn2_w, L1_conv_gn2_b, L1_conv_fe_w, L1_conv_fe_b, L1_conv_g1_w, L1_conv_g1_b, L1_conv_bn1_g, L1_conv_bn1_b, L1_conv_bn1_rm, L1_conv_bn1_rv, L1_conv_ca_w1, L1_conv_ca_b1, L1_conv_ca_w2, L1_conv_ca_b2, L1_conv_g2_w, L1_conv_g2_b, L1_conv_bn2_g, L1_conv_bn2_b, L1_conv_bn2_rm, L1_conv_bn2_rv, L1_conv_g3_w, L1_conv_g3_b, L1_conv_shared_w, L1_conv_shared_b, L1_conv_expert_w, L1_conv_expert_b, L2_conv_w1, L3_conv_spa_in_w, L3_conv_spa_conv_w, L3_conv_spa_conv_b, L3_conv_spa_xproj_w, L3_conv_spa_dt_w, L3_conv_spa_dt_b, L3_conv_spa_A_log, L3_conv_spa_D, L3_conv_spa_out_w, L3_conv_spe_in_w, L3_conv_spe_conv_w, L3_conv_spe_conv_b, L3_conv_spe_xproj_w, L3_conv_spe_dt_w, L3_conv_spe_dt_b, L3_conv_spe_A_log, L3_conv_spe_D, L3_conv_spe_out_w, L3_conv_spa_gn_w, L3_conv_spa_gn_b, L3_conv_spe_gn_w, L3_conv_spe_gn_b, L3_conv_att_w):
    import jax
    import jax.numpy as jnp
    def _L0_conv_ref(x, fg_w1, fg_w2, q_w, q_b, sr1_w, sr1_b, ln1_g, ln1_b, kv1_w, kv1_b, sr2_w, sr2_b, ln2_g, ln2_b, kv2_w, kv2_b, dw_w, proj_w, proj_b):
        import jax, jax.numpy as jnp
        import numpy as np
        from jax import lax
        B, C, H, W = (4, 64, 128, 128)
        NUM_HEADS = 4
        D = C // NUM_HEADS
        SR1, SR2 = (8, 16)
        RED = 4
        EPS = 1e-05

        def _layernorm(x, gamma, beta):
            mu = jnp.mean(x, axis=-1, keepdims=True)
            var = jnp.var(x, axis=-1, keepdims=True)
            return (x - mu) * lax.rsqrt(var + EPS) * gamma + beta

        def _conv(x, w, stride, pad='VALID', groups=1):
            return lax.conv_general_dilated(x, w, (stride, stride), pad, dimension_numbers=('NCHW', 'OIHW', 'NCHW'), feature_group_count=groups)

        def _forward(x, fg_w1, fg_w2, q_w, q_b, sr1_w, sr1_b, ln1_g, ln1_b, kv1_w, kv1_b, sr2_w, sr2_b, ln2_g, ln2_b, kv2_w, kv2_b, dw_w, proj_w, proj_b):
            b, c, h, w = x.shape
            n = h * w
            spec = jnp.fft.rfft2(x, norm='ortho')
            mag = jnp.abs(spec)
            hid = jax.nn.gelu(jnp.einsum('bchw,oc->bohw', mag, fg_w1), approximate=False)
            gate = jax.nn.sigmoid(jnp.einsum('bchw,oc->bohw', hid, fg_w2))
            x_gated = jnp.fft.irfft2(spec * gate, s=(h, w), norm='ortho')
            xf = x + x_gated
            x_flat = xf.reshape(b, c, n).transpose(0, 2, 1)
            q = (x_flat @ q_w + q_b).reshape(b, n, NUM_HEADS, D).transpose(0, 2, 1, 3)

            def kv_path(sr_w, sr_b, ln_g, ln_b, kv_w, kv_b, stride):
                xs = _conv(xf, sr_w, stride) + sr_b[None, :, None, None]
                _, _, hs, ws = xs.shape
                xs_flat = _layernorm(xs.reshape(b, c, hs * ws).transpose(0, 2, 1), ln_g, ln_b)
                kv = xs_flat @ kv_w + kv_b
                k, v = (kv[..., :c], kv[..., c:])
                v_sp = v.transpose(0, 2, 1).reshape(b, c, hs, ws)
                v_sp = _conv(v_sp, dw_w, 1, pad=((1, 1), (1, 1)), groups=c)
                v = v_sp.reshape(b, c, hs * ws).transpose(0, 2, 1)
                return (k, v)
            k1, v1 = kv_path(sr1_w, sr1_b, ln1_g, ln1_b, kv1_w, kv1_b, SR1)
            k2, v2 = kv_path(sr2_w, sr2_b, ln2_g, ln2_b, kv2_w, kv2_b, SR2)
            k = jnp.concatenate([k1, k2], axis=1)
            v = jnp.concatenate([v1, v2], axis=1)
            nk = k.shape[1]
            k = k.reshape(b, nk, NUM_HEADS, D).transpose(0, 2, 1, 3)
            v = v.reshape(b, nk, NUM_HEADS, D).transpose(0, 2, 1, 3)
            scale = D ** (-0.5)
            attn = jax.nn.softmax(jnp.einsum('bhqd,bhkd->bhqk', q, k) * scale, axis=-1)
            out = jnp.einsum('bhqk,bhkd->bhqd', attn, v)
            out = out.transpose(0, 2, 1, 3).reshape(b, n, c)
            out = out @ proj_w + proj_b
            return out.transpose(0, 2, 1).reshape(b, c, h, w) + x
        return _forward(x, fg_w1, fg_w2, q_w, q_b, sr1_w, sr1_b, ln1_g, ln1_b, kv1_w, kv1_b, sr2_w, sr2_b, ln2_g, ln2_b, kv2_w, kv2_b, dw_w, proj_w, proj_b)

    def _L1_conv_ref(x, gn1_w, gn1_b, afno_w1, afno_b1, afno_w2, afno_b2, gn2_w, gn2_b, fe_w, fe_b, g1_w, g1_b, bn1_g, bn1_b, bn1_rm, bn1_rv, ca_w1, ca_b1, ca_w2, ca_b2, g2_w, g2_b, bn2_g, bn2_b, bn2_rm, bn2_rv, g3_w, g3_b, shared_w, shared_b, expert_w, expert_b):
        import jax, jax.numpy as jnp
        import numpy as np
        MODES = 32
        NUM_BLOCKS = 4
        NUM_EXPERTS = 16
        TOP_K = 4
        TEMPERATURE = 2.0

        def _gelu(t):
            return jax.nn.gelu(t, approximate=False)

        def _c1(x, w, b):
            return jnp.einsum('bchw,oc->bohw', x, w) + b[None, :, None, None]

        def _group_norm(x, w, b, groups=8, eps=1e-05):
            B, C, H, W = x.shape
            xg = x.reshape(B, groups, C // groups, H, W)
            mu = xg.mean(axis=(2, 3, 4), keepdims=True)
            var = xg.var(axis=(2, 3, 4), keepdims=True)
            xn = ((xg - mu) * jax.lax.rsqrt(var + eps)).reshape(B, C, H, W)
            return xn * w[None, :, None, None] + b[None, :, None, None]

        def _bn_eval(x, g, b, rm, rv, eps=1e-05):
            return (x - rm) * jax.lax.rsqrt(rv + eps) * g + b

        def _afno(x, w1, b1, w2, b2):
            B, C, H, W = x.shape
            bs = C // NUM_BLOCKS
            xp = x.transpose(0, 2, 3, 1)
            xf = jnp.fft.rfft2(xp, axes=(1, 2), norm='ortho')
            Wf = xf.shape[2]
            xf = xf.reshape(B, H, Wf, NUM_BLOCKS, bs)
            m = MODES
            xm = xf[:, :m, :m]
            xr, xi = (xm.real, xm.imag)
            o1r = _gelu(jnp.einsum('bhwni,nio->bhwno', xr, w1[0]) - jnp.einsum('bhwni,nio->bhwno', xi, w1[1]) + b1[0])
            o1i = _gelu(jnp.einsum('bhwni,nio->bhwno', xi, w1[0]) + jnp.einsum('bhwni,nio->bhwno', xr, w1[1]) + b1[1])
            o2r = jnp.einsum('bhwni,nio->bhwno', o1r, w2[0]) - jnp.einsum('bhwni,nio->bhwno', o1i, w2[1]) + b2[0]
            o2i = jnp.einsum('bhwni,nio->bhwno', o1i, w2[0]) + jnp.einsum('bhwni,nio->bhwno', o1r, w2[1]) + b2[1]
            of = jnp.zeros((B, H, Wf, NUM_BLOCKS, bs), dtype=xf.dtype)
            of = of.at[:, :m, :m].set(o2r + 1j * o2i)
            out = jnp.fft.irfft2(of.reshape(B, H, Wf, C), s=(H, W), axes=(1, 2), norm='ortho')
            out = out + xp
            return out.transpose(0, 3, 1, 2)

        def _forward(x, gn1_w, gn1_b, afno_w1, afno_b1, afno_w2, afno_b2, gn2_w, gn2_b, fe_w, fe_b, g1_w, g1_b, bn1_g, bn1_b, bn1_rm, bn1_rv, ca_w1, ca_b1, ca_w2, ca_b2, g2_w, g2_b, bn2_g, bn2_b, bn2_rm, bn2_rv, g3_w, g3_b, shared_w, shared_b, expert_w, expert_b):
            residual = x
            h = _group_norm(x, gn1_w, gn1_b)
            h = _afno(h, afno_w1, afno_b1, afno_w2, afno_b2)
            h = h + residual
            residual = h
            h = _group_norm(h, gn2_w, gn2_b)
            feats = _gelu(_c1(h, fe_w, fe_b))
            shared = jnp.zeros_like(h)
            for s in range(shared_w.shape[0]):
                shared = shared + _gelu(_c1(feats, shared_w[s], shared_b[s])) / shared_w.shape[0]
            gf = feats.mean(axis=(2, 3))
            h1 = _gelu(_bn_eval(gf @ g1_w.T + g1_b, bn1_g, bn1_b, bn1_rm, bn1_rv))
            a = _gelu(h1 @ ca_w1.T + ca_b1) @ ca_w2.T + ca_b2
            h1 = h1 * jax.nn.sigmoid(2.0 * a)
            h2 = _gelu(_bn_eval(h1 @ g2_w.T + g2_b, bn2_g, bn2_b, bn2_rm, bn2_rv))
            scores = h2 @ g3_w.T + g3_b
            vals, idx = jax.lax.top_k(scores, TOP_K)
            wts = jax.nn.softmax(vals / TEMPERATURE, axis=1)
            B = x.shape[0]
            gate_w = jnp.zeros((B, NUM_EXPERTS), x.dtype).at[jnp.arange(B)[:, None], idx].add(wts)
            out = shared
            for e in range(NUM_EXPERTS):
                out = out + _gelu(_c1(feats, expert_w[e], expert_b[e])) * gate_w[:, e][:, None, None, None]
            return out + residual
        return _forward(x, gn1_w, gn1_b, afno_w1, afno_b1, afno_w2, afno_b2, gn2_w, gn2_b, fe_w, fe_b, g1_w, g1_b, bn1_g, bn1_b, bn1_rm, bn1_rv, ca_w1, ca_b1, ca_w2, ca_b2, g2_w, g2_b, bn2_g, bn2_b, bn2_rm, bn2_rv, g3_w, g3_b, shared_w, shared_b, expert_w, expert_b)

    def _L2_conv_ref(x, w1):
        import jax, jax.numpy as jnp
        import numpy as np
        from jax import lax
        CUTOFF = 0.25
        SIGMA = 1.0
        RADIUS = 4

        def _gauss_kernel(sigma=SIGMA, radius=RADIUS):
            x = np.arange(-radius, radius + 1, dtype=np.float32)
            k = np.exp(-0.5 * (x / sigma) ** 2)
            return jnp.asarray(k / k.sum())

        def _blur_axis(x, axis, kernel):
            r = (kernel.shape[0] - 1) // 2
            pad = [(0, 0)] * x.ndim
            pad[axis] = (r, r)
            xp = jnp.pad(x, pad, mode='edge')
            out = jnp.zeros_like(x)
            for i in range(kernel.shape[0]):
                out = out + kernel[i] * lax.slice_in_dim(xp, i, i + x.shape[axis], axis=axis)
            return out

        def gaussian_smoothing_4d(x):
            k = _gauss_kernel().astype(x.dtype)
            for ax in range(4):
                x = _blur_axis(x, ax, k)
            return x

        def dht_2d(x):
            return (jnp.fft.fftn(x, axes=(2, 3)).real - jnp.fft.fftn(jnp.flip(x, axis=(2, 3)), axes=(2, 3)).imag).astype(x.dtype)

        def _neg_k(a):
            return jnp.roll(jnp.flip(a, axis=(-2, -1)), shift=(1, 1), axis=(-2, -1))

        def compl_mul2d(x1, x2):
            x1n, x2n = (_neg_k(x1), _neg_k(x2))
            e = lambda a, b: jnp.einsum('bixy,ioxy->boxy', a, b)
            return 0.5 * (e(x1, x2) - e(x1n, x2n) + e(x1, x2n) + e(x1n, x2))
        B, _, H, W = x.shape
        Cout, M1, M2 = (w1.shape[1], w1.shape[2], w1.shape[3])
        x_ht = dht_2d(x)
        out_ht = jnp.zeros((B, Cout, H, W), dtype=x.dtype)
        out_ht = out_ht.at[:, :, :M1, :M2].set(compl_mul2d(x_ht[:, :, :M1, :M2], w1))
        y = dht_2d(out_ht) / (H * W)
        y = gaussian_smoothing_4d(y)
        freqs = jnp.fft.fftfreq(W)
        mask = (jnp.abs(freqs) <= CUTOFF).astype(y.dtype)
        return y * mask

    def _L3_conv_ref(x, spa_in_w, spa_conv_w, spa_conv_b, spa_xproj_w, spa_dt_w, spa_dt_b, spa_A_log, spa_D, spa_out_w, spe_in_w, spe_conv_w, spe_conv_b, spe_xproj_w, spe_dt_w, spe_dt_b, spe_A_log, spe_D, spe_out_w, spa_gn_w, spa_gn_b, spe_gn_w, spe_gn_b, att_w):
        import jax, jax.numpy as jnp
        from jax import lax
        import numpy as np
        D_STATE = 16
        D_CONV = 4
        GROUPS = 4
        TOKEN = 8

        def group_norm(x, w, b, groups, eps=1e-05):
            B, C, H, W = x.shape
            xg = x.reshape(B, groups, C // groups, H, W)
            mu = xg.mean(axis=(2, 3, 4), keepdims=True)
            var = ((xg - mu) ** 2).mean(axis=(2, 3, 4), keepdims=True)
            xg = (xg - mu) / jnp.sqrt(var + eps)
            return xg.reshape(B, C, H, W) * w[None, :, None, None] + b[None, :, None, None]

        def mamba_fwd(x, in_w, conv_w, conv_b, xproj_w, dt_w, dt_b, A_log, D, out_w):
            Bsz, L, _ = x.shape
            d_inner = in_w.shape[0] // 2
            dt_rank = dt_w.shape[1]
            xz = x @ in_w.T
            xi, z = jnp.split(xz, 2, axis=-1)
            xc = lax.conv_general_dilated(xi.transpose(0, 2, 1), conv_w, window_strides=(1,), padding=[(D_CONV - 1, 0)], dimension_numbers=('NCH', 'OIH', 'NCH'), feature_group_count=d_inner)
            xc = jax.nn.silu(xc + conv_b[None, :, None]).transpose(0, 2, 1)
            xdb = xc @ xproj_w.T
            dt, Bm, Cm = jnp.split(xdb, [dt_rank, dt_rank + D_STATE], axis=-1)
            dt = jax.nn.softplus(dt @ dt_w.T + dt_b)
            A = -jnp.exp(A_log)
            dA = jnp.exp(dt[..., None] * A)
            dBx = dt[..., None] * Bm[:, :, None, :] * xc[..., None]

            def step(h, inp):
                dA_t, dBx_t, C_t = inp
                h = dA_t * h + dBx_t
                y = jnp.einsum('bds,bs->bd', h, C_t)
                return (h, y)
            h0 = jnp.zeros((Bsz, d_inner, D_STATE), dtype=x.dtype)
            _, ys = lax.scan(step, h0, (dA.transpose(1, 0, 2, 3), dBx.transpose(1, 0, 2, 3), Cm.transpose(1, 0, 2)))
            y = ys.transpose(1, 0, 2) + xc * D
            y = y * jax.nn.silu(z)
            return y @ out_w.T
        B, C, H, W = x.shape
        gcn = -(-C // TOKEN)
        xs = x.transpose(0, 2, 3, 1).reshape(1, -1, C)
        ys = mamba_fwd(xs, spa_in_w, spa_conv_w, spa_conv_b, spa_xproj_w, spa_dt_w, spa_dt_b, spa_A_log, spa_D, spa_out_w)
        ys = ys.reshape(B, H, W, C).transpose(0, 3, 1, 2)
        spa = jax.nn.silu(group_norm(ys, spa_gn_w, spa_gn_b, GROUPS)) + x
        xe = x.transpose(0, 2, 3, 1).reshape(B * H * W, TOKEN, gcn)
        ye = mamba_fwd(xe, spe_in_w, spe_conv_w, spe_conv_b, spe_xproj_w, spe_dt_w, spe_dt_b, spe_A_log, spe_D, spe_out_w)
        ye = ye.reshape(B, H, W, C).transpose(0, 3, 1, 2)
        spe = x + jax.nn.silu(group_norm(ye, spe_gn_w, spe_gn_b, GROUPS))
        w = jax.nn.softmax(att_w)
        return spa * w[0] + spe * w[1] + x

    def _gn(v, G=32, eps=1e-5):
        B_, C_, H_, W_ = v.shape
        g = v.reshape(B_, G, C_ // G, H_, W_)
        m = jnp.mean(g, axis=(2, 3, 4), keepdims=True)
        s = jnp.var(g, axis=(2, 3, 4), keepdims=True)
        return ((g - m) / jnp.sqrt(s + eps)).reshape(v.shape)

    def _ln_c(v, eps=1e-6):
        m = jnp.mean(v, axis=1, keepdims=True)
        s = jnp.var(v, axis=1, keepdims=True)
        return (v - m) / jnp.sqrt(s + eps)

    def _ln_t(v, eps=1e-5):
        m = jnp.mean(v, axis=-1, keepdims=True)
        s = jnp.var(v, axis=-1, keepdims=True)
        return (v - m) / jnp.sqrt(s + eps)

    def _to_tokens(v):
        B_, C_, H_, W_ = v.shape
        return v.reshape(B_, C_, H_ * W_).transpose(0, 2, 1)
    def _from_tokens(t, like):
        B_, C_, H_, W_ = like.shape
        return t.transpose(0, 2, 1).reshape(B_, C_, H_, W_)

    x = _L0_conv_ref(x, L0_conv_fg_w1, L0_conv_fg_w2, L0_conv_q_w, L0_conv_q_b, L0_conv_sr1_w, L0_conv_sr1_b, L0_conv_ln1_g, L0_conv_ln1_b, L0_conv_kv1_w, L0_conv_kv1_b, L0_conv_sr2_w, L0_conv_sr2_b, L0_conv_ln2_g, L0_conv_ln2_b, L0_conv_kv2_w, L0_conv_kv2_b, L0_conv_dw_w, L0_conv_proj_w, L0_conv_proj_b)
    x = _L1_conv_ref(x, L1_conv_gn1_w, L1_conv_gn1_b, L1_conv_afno_w1, L1_conv_afno_b1, L1_conv_afno_w2, L1_conv_afno_b2, L1_conv_gn2_w, L1_conv_gn2_b, L1_conv_fe_w, L1_conv_fe_b, L1_conv_g1_w, L1_conv_g1_b, L1_conv_bn1_g, L1_conv_bn1_b, L1_conv_bn1_rm, L1_conv_bn1_rv, L1_conv_ca_w1, L1_conv_ca_b1, L1_conv_ca_w2, L1_conv_ca_b2, L1_conv_g2_w, L1_conv_g2_b, L1_conv_bn2_g, L1_conv_bn2_b, L1_conv_bn2_rm, L1_conv_bn2_rv, L1_conv_g3_w, L1_conv_g3_b, L1_conv_shared_w, L1_conv_shared_b, L1_conv_expert_w, L1_conv_expert_b)
    x = _L2_conv_ref(x, L2_conv_w1)
    x = _L3_conv_ref(x, L3_conv_spa_in_w, L3_conv_spa_conv_w, L3_conv_spa_conv_b, L3_conv_spa_xproj_w, L3_conv_spa_dt_w, L3_conv_spa_dt_b, L3_conv_spa_A_log, L3_conv_spa_D, L3_conv_spa_out_w, L3_conv_spe_in_w, L3_conv_spe_conv_w, L3_conv_spe_conv_b, L3_conv_spe_xproj_w, L3_conv_spe_dt_w, L3_conv_spe_dt_b, L3_conv_spe_A_log, L3_conv_spe_D, L3_conv_spe_out_w, L3_conv_spa_gn_w, L3_conv_spa_gn_b, L3_conv_spe_gn_w, L3_conv_spe_gn_b, L3_conv_att_w)
    return x


_drawn_inputs = setup_inputs


def setup_inputs(seed=0):
    import zlib

    import numpy as np

    out = dict(_drawn_inputs(seed))
    spreads = {'L1_conv_gn1_w': (1.0, 0.2),
     'L1_conv_gn1_b': (0.0, 0.1),
     'L1_conv_gn2_w': (1.0, 0.2),
     'L1_conv_gn2_b': (0.0, 0.1),
     'L1_conv_fe_b': (0.0, 0.1),
     'L1_conv_g1_b': (0.0, 0.1),
     'L1_conv_bn1_g': (1.0, 0.2),
     'L1_conv_bn1_b': (0.0, 0.1),
     'L1_conv_bn1_rm': (0.0, 0.1),
     'L1_conv_bn1_rv': (1.0, 0.2),
     'L1_conv_ca_b1': (0.0, 0.1),
     'L1_conv_ca_b2': (0.0, 0.1),
     'L1_conv_g2_b': (0.0, 0.1),
     'L1_conv_bn2_g': (1.0, 0.2),
     'L1_conv_bn2_b': (0.0, 0.1),
     'L1_conv_bn2_rm': (0.0, 0.1),
     'L1_conv_bn2_rv': (1.0, 0.2),
     'L1_conv_g3_b': (0.0, 0.1),
     'L1_conv_shared_b': (0.0, 0.1),
     'L1_conv_expert_b': (0.0, 0.1),
     'L3_conv_spa_D': (1.0, 0.2),
     'L3_conv_spe_D': (1.0, 0.2),
     'L3_conv_spa_gn_w': (1.0, 0.2),
     'L3_conv_spa_gn_b': (0.0, 0.1),
     'L3_conv_spe_gn_w': (1.0, 0.2),
     'L3_conv_spe_gn_b': (0.0, 0.1),
     'L3_conv_att_w': (0.5, 0.2)}
    factors = {}
    for name, (base, spread) in spreads.items():
        noise = np.random.default_rng([zlib.crc32(name.encode()), seed]).standard_normal(out[name].shape)
        drawn = base * np.exp(spread * noise) if base else spread * noise
        out[name] = jnp.asarray(drawn.astype(out[name].dtype))
    for name, factor in factors.items():
        out[name] = (out[name] * factor).astype(out[name].dtype)
    return out
```

```python
import math
from contextlib import ExitStack

import numpy as np
import concourse.bass as bass
from concourse import mybir

F32 = mybir.dt.float32
BF16 = mybir.dt.bfloat16
ALU = mybir.AluOpType
ACT = mybir.ActivationFunctionType
AX = mybir.AxisListType

B, C, H, W = 4, 64, 128, 128
WF = W // 2 + 1
HW = H * W
EPS = 1e-5
G4 = 4
NG = B * C // G4


class Stage:

    def __init__(self, nc, name):
        self.nc, self.name, self.ctx, self.sems = nc, name, ExitStack(), ExitStack()
        self.numbers = []

    def __enter__(self):
        return self

    def __exit__(self, *e):
        self.ctx.close()
        for sem in self.numbers:
            self.nc.gpsimd.sem_clear(sem)
        self.nc.all_engine_barrier()
        self.sems.close()

    def sb(self, name, shape, dt=F32):
        return self.ctx.enter_context(self.nc.sbuf_tensor(f"{self.name}_{name}", shape, dt))

    def ps(self, name, shape, dt=F32):
        return self.ctx.enter_context(self.nc.psum_tensor(f"{self.name}_{name}", shape, dt))

    def sem(self, name):
        sem = self.sems.enter_context(self.nc.semaphore(f"{self.name}_{name}"))
        self.numbers.append(sem)
        return sem

    def sem2(self, name):
        return [self.sem(f"{name}{s}") for s in range(2)]

    def block(self):
        return self.ctx.enter_context(self.nc.Block())


def turns(eng, n):
    def run(body):
        body(0)
        if n > 1:
            with eng.Fori(1, n) as j:
                body(j)
    return run


def spectrum(nc, x, c_h, c_w, spec, power):
    xv = x.rearrange("b c h w -> h (b c) w")
    sv = spec.rearrange("n k f -> k n f")
    mv = power.rearrange("n k f -> k n f")
    N = NG // 2
    with Stage(nc, "spectrum") as st:
        ch = st.sb("ch", [128, 256])
        cw = st.sb("cw", [128, 2, 2 * WF])
        xs = st.sb("xs", [128, 2, G4, W])
        rows = st.sb("rows", [128, 2, G4, 256])
        spc = st.sb("spc", [128, 2, G4, 2 * WF])
        sq = st.sb("sq", [128, 2, G4, 2 * WF])
        pw = st.sb("pw", [128, 2, G4, WF])
        p_rows = [st.ps(f"p_rows{s}", [128, G4, 256]) for s in range(2)]
        p_spec = [st.ps(f"p_spec{s}", [128, 2, 512]) for s in range(2)]
        consts_in = st.sem("consts_in")
        x_in, rows_done, rows_copied = st.sem2("x_in"), st.sem2("rows_done"), st.sem2("rows_copied")
        spec_done, spec_copied, squared = st.sem2("spec_done"), st.sem2("spec_copied"), st.sem2("squared")
        summed, stored = st.sem2("summed"), st.sem2("stored")

        def pv(s):
            return p_spec[s][:, :, 0:4 * WF].rearrange("p a (i f) -> p a i f", i=2)

        block = st.block()

        @block.sync
        def _(sp):
            def load(j, s):
                sp.dma_start(xs[:, s], xv[:, bass.ds((2 * j + s) * G4, G4), :]).then_inc(x_in[s], 16)

            def store(j, s):
                sp.wait_ge(spec_copied[s], j + 1)
                sp.dma_start(sv[:, bass.ds((2 * j + s) * G4, G4), :], spc[:, s]).then_inc(stored[s], 16)
                sp.wait_ge(summed[s], j + 1)
                sp.dma_start(mv[:, bass.ds((2 * j + s) * G4, G4), :], pw[:, s]).then_inc(stored[s], 16)

            sp.dma_start(ch[:, :], c_h).then_inc(consts_in, 16)
            sp.dma_start(cw[:, :, :], c_w).then_inc(consts_in, 16)
            for s in range(2):
                load(0, s)
            @turns(sp, N - 1)
            def _(j):
                for s in range(2):
                    sp.wait_ge(rows_done[s], j + 1)
                    load(j + 1, s)
                for s in range(2):
                    store(j, s)
            for s in range(2):
                store(N - 1, s)
            for s in range(2):
                sp.wait_ge(stored[s], 32 * N)

        @block.tensor
        def _(pe):
            pe.wait_ge(consts_in, 32)
            @turns(pe, N)
            def _(j):
                for s in range(2):
                    pe.wait_ge(x_in[s], 16 * j + 16)
                    pe.wait_ge(rows_copied[s], j)
                    for i in range(G4):
                        mm = nc.tensor.matmul(p_rows[s][:, i, :], xs[:, s, i, :], ch[:, :], start=True, stop=True)
                    mm.then_inc(rows_done[s], 1)
                for s in range(2):
                    pe.wait_ge(rows_copied[s], j + 1)
                    pe.wait_ge(spec_copied[s], j)
                    for i in range(G4):
                        o = pv(s)[:, i // 2, i % 2, :]
                        nc.tensor.matmul(o, rows[:, s, i, 0:128], cw[:, 0, :], start=True, stop=False)
                        mm = nc.tensor.matmul(o, rows[:, s, i, 128:256], cw[:, 1, :], start=False, stop=True)
                    mm.then_inc(spec_done[s], 1)

        @block.scalar
        def _(act):
            @turns(act, N)
            def _(j):
                for s in range(2):
                    act.wait_ge(rows_done[s], j + 1)
                    act.wait_ge(spec_done[s], j)
                    nc.scalar.activation(rows[:, s], p_rows[s][:, :, :], ACT.Copy).then_inc(rows_copied[s], 1)
                for s in range(2):
                    act.wait_ge(spec_copied[s], j + 1)
                    act.wait_ge(summed[s], j)
                    nc.scalar.activation(sq[:, s], spc[:, s], ACT.Square).then_inc(squared[s], 1)

        @block.vector
        def _(dve):
            @turns(dve, N)
            def _(j):
                for s in range(2):
                    dve.wait_ge(spec_done[s], j + 1)
                    dve.wait_ge(stored[s], 32 * j)
                    dve.wait_ge(squared[s], j)
                    nc.vector.tensor_copy(spc[:, s].rearrange("p (a i) f -> p a i f", a=2), pv(s)).then_inc(spec_copied[s], 1)
                for s in range(2):
                    dve.wait_ge(squared[s], j + 1)
                    nc.vector.scalar_tensor_tensor(pw[:, s], sq[:, s, :, 0:WF], 1e-34, sq[:, s, :, WF:2 * WF],
                                                   ALU.max, ALU.add).then_inc(summed[s], 1)


def frequency_gate(nc, power, w1, w2, gate):
    KF = H * WF
    CH = 416
    N = KF // CH
    pv = power.rearrange("(a p) k f -> p a (k f)", a=2)
    gv = gate.rearrange("(a p) k f -> p a (k f)", a=2)
    with Stage(nc, "gate") as st:
        w1s = st.sb("w1s", [128, 32])
        w2s = st.sb("w2s", [32, 128])
        mg = st.sb("mg", [128, 2, KF])
        hid = st.sb("hid", [32, 2, KF])
        p_hid = [st.ps(f"p_hid{s}", [32, 512]) for s in range(2)]
        p_gate = [st.ps(f"p_gate{s}", [128, 512]) for s in range(2)]
        w_in = st.sem("w_in")
        power_in = st.sem2("power_in")
        rooted, hid_done, hid_ready = st.sem2("rooted"), st.sem2("hid_done"), st.sem2("hid_ready")
        gate_done, gate_ready = st.sem2("gate_done"), st.sem2("gate_ready")
        stored = st.sem("stored")
        block = st.block()

        @block.sync
        def _(sp):
            sp.dma_start(w1s[:, :], w1).then_inc(w_in, 16)
            sp.dma_start(w2s[:, :], w2).then_inc(w_in, 16)
            for s in range(2):
                sp.dma_start(mg[:, s, :], pv[:, s, :]).then_inc(power_in[s], 16)
            for s in range(2):
                sp.wait_ge(gate_ready[s], N)
                sp.dma_start(gv[:, s, :], mg[:, s, :]).then_inc(stored, 16)
            sp.wait_ge(stored, 32)

        @block.tensor
        def _(pe):
            pe.wait_ge(w_in, 32)
            for s in range(2):
                pe.wait_ge(rooted[s], 1)
            @turns(pe, N)
            def _(j):
                for s in range(2):
                    pe.wait_ge(hid_ready[s], j)
                    nc.tensor.matmul(p_hid[s][:, 0:CH], w1s[:, :], mg[:, s, bass.ds(j * CH, CH)],
                                     start=True, stop=True).then_inc(hid_done[s], 1)
            for s in range(2):
                pe.wait_ge(hid_ready[s], N)
            @turns(pe, N)
            def _(j):
                for s in range(2):
                    pe.wait_ge(gate_ready[s], j)
                    nc.tensor.matmul(p_gate[s][:, 0:CH], w2s[:, :], hid[:, s, bass.ds(j * CH, CH)],
                                     start=True, stop=True).then_inc(gate_done[s], 1)

        @block.scalar
        def _(act):
            for s in range(2):
                act.wait_ge(power_in[s], 16)
                nc.scalar.activation(mg[:, s, :], mg[:, s, :], ACT.Sqrt).then_inc(rooted[s], 1)
            @turns(act, N)
            def _(j):
                for s in range(2):
                    act.wait_ge(hid_done[s], j + 1)
                    nc.scalar.activation(hid[:, s, bass.ds(j * CH, CH)], p_hid[s][:, 0:CH], ACT.Gelu).then_inc(hid_ready[s], 1)
            @turns(act, N)
            def _(j):
                for s in range(2):
                    act.wait_ge(gate_done[s], j + 1)
                    nc.scalar.activation(mg[:, s, bass.ds(j * CH, CH)], p_gate[s][:, 0:CH], ACT.Sigmoid).then_inc(gate_ready[s], 1)


def gated_inverse(nc, x, spec, gate, c_k, c_f, xf):
    xv = x.rearrange("b c h w -> h (b c) w")
    ov = xf.rearrange("b c h w -> h (b c) w")
    sv = spec.rearrange("n k f -> k n f")
    gv = gate.rearrange("n k f -> k n f")
    N = NG // 2
    with Stage(nc, "inverse") as st:
        ck = st.sb("ck", [128, 2, 256])
        cf = st.sb("cf", [WF, 2, W])
        xs = st.sb("xs", [128, 2, G4, W])
        sp_ = st.sb("spec", [128, 2, G4, 2 * WF])
        gt = st.sb("gate", [128, 2, G4, WF])
        gs = st.sb("gs", [128, 2, G4, 2 * WF])
        cols = st.sb("cols", [WF, 2, G4, 256])
        out = st.sb("out", [128, 2, G4, W])
        p_cols = [st.ps(f"p_cols{s}", [WF, G4, 256]) for s in range(2)]
        p_img = [st.ps(f"p_img{s}", [128, G4, W]) for s in range(2)]
        consts_in = st.sem("consts_in")
        spec_in, x_in, gated = st.sem2("spec_in"), st.sem2("x_in"), st.sem2("gated")
        cols_done, cols_copied, img_done = st.sem2("cols_done"), st.sem2("cols_copied"), st.sem2("img_done")
        added, stored = st.sem2("added"), st.sem2("stored")
        block = st.block()

        @block.sync
        def _(sp):
            def load(j, s):
                n = bass.ds((2 * j + s) * G4, G4)
                sp.dma_start(sp_[:, s], sv[:, n, :]).then_inc(spec_in[s], 16)
                sp.dma_start(gt[:, s], gv[:, n, :]).then_inc(spec_in[s], 16)

            def load_x(j, s):
                sp.dma_start(xs[:, s], xv[:, bass.ds((2 * j + s) * G4, G4), :]).then_inc(x_in[s], 16)

            def store(j, s):
                sp.wait_ge(added[s], j + 1)
                sp.dma_start(ov[:, bass.ds((2 * j + s) * G4, G4), :], out[:, s]).then_inc(stored[s], 16)

            sp.dma_start(ck[:, :, :], c_k).then_inc(consts_in, 16)
            sp.dma_start(cf[:, :, :], c_f).then_inc(consts_in, 16)
            for s in range(2):
                load(0, s)
                load_x(0, s)
            @turns(sp, N - 1)
            def _(j):
                for s in range(2):
                    sp.wait_ge(gated[s], 2 * j + 2)
                    load(j + 1, s)
                for s in range(2):
                    store(j, s)
                    load_x(j + 1, s)
            for s in range(2):
                store(N - 1, s)
            for s in range(2):
                sp.wait_ge(stored[s], 16 * N)

        @block.vector
        def _(dve):
            @turns(dve, N)
            def _(j):
                for s in range(2):
                    dve.wait_ge(spec_in[s], 32 * j + 32)
                    dve.wait_ge(cols_done[s], j)
                    for r in range(2):
                        nc.vector.tensor_tensor(gs[:, s, :, r * WF:(r + 1) * WF], sp_[:, s, :, r * WF:(r + 1) * WF],
                                                gt[:, s], ALU.mult).then_inc(gated[s], 1)
                for s in range(2):
                    dve.wait_ge(img_done[s], j + 1)
                    dve.wait_ge(x_in[s], 16 * j + 16)
                    dve.wait_ge(stored[s], 16 * j)
                    nc.vector.tensor_tensor(out[:, s], xs[:, s], p_img[s][:, :, :], ALU.add).then_inc(added[s], 1)

        @block.tensor
        def _(pe):
            pe.wait_ge(consts_in, 32)
            @turns(pe, N)
            def _(j):
                for s in range(2):
                    pe.wait_ge(gated[s], 2 * j + 2)
                    pe.wait_ge(cols_copied[s], j)
                    for i in range(G4):
                        nc.tensor.matmul(p_cols[s][:, i, :], gs[:, s, i, 0:WF], ck[:, 0, :], start=True, stop=False)
                        mm = nc.tensor.matmul(p_cols[s][:, i, :], gs[:, s, i, WF:2 * WF], ck[:, 1, :], start=False, stop=True)
                    mm.then_inc(cols_done[s], 1)
                for s in range(2):
                    pe.wait_ge(cols_copied[s], j + 1)
                    pe.wait_ge(added[s], j)
                    for i in range(G4):
                        nc.tensor.matmul(p_img[s][:, i, :], cols[:, s, i, 0:128], cf[:, 0, :], start=True, stop=False)
                        mm = nc.tensor.matmul(p_img[s][:, i, :], cols[:, s, i, 128:256], cf[:, 1, :], start=False, stop=True)
                    mm.then_inc(img_done[s], 1)

        @block.scalar
        def _(act):
            @turns(act, N)
            def _(j):
                for s in range(2):
                    act.wait_ge(cols_done[s], j + 1)
                    act.wait_ge(img_done[s], j)
                    nc.scalar.activation(cols[:, s], p_cols[s][:, :, :], ACT.Copy).then_inc(cols_copied[s], 1)


NK1, NK2 = 256, 64
NK = NK1 + NK2
NH, HD = 4, 16
NB = 6 * HD
NM = NB + 3
VM = 2 * NH + NH // 2
VC = 128 * VM


def keys_in_chunk(c):
    return min(128, NK - 128 * c)


def patch_convolutions(nc, xf, w1, w2, bias, xs):
    xv = xf.rearrange("(a p) c h w -> p c a (h w)", a=2)
    with Stage(nc, "conv") as st:
        xr = st.sb("x", [128, 2, HW])
        wb = st.sb("wb", [128, 2, 16, 128])
        zw = st.sb("zw", [128, 128])
        bs = st.sb("bs", [128, 2])
        res = st.sb("res", [128, 2, NK])
        acc = [st.ps("acc1", [128, 2, NK1]), st.ps("acc2", [128, 2, NK2])]
        x_in, b_in, zeroed = st.sem("x_in"), st.sem("b_in"), st.sem("zeroed")
        w_in, w_used = st.sem2("w_in"), st.sem2("w_used")
        summed, ready, stored = st.sem("summed"), st.sem("ready"), st.sem("stored")
        sizes = (8, 16)
        base = (0, 8 // 2)
        block = st.block()

        @block.sync
        def _(sp):
            sp.dma_start(bs[:, :], bias).then_inc(b_in, 16)
            for p in range(2):
                for a in range(2):
                    sp.dma_start(xr[64 * p:64 * p + 64, a, :], xv[p, :, a, :]).then_inc(x_in, 16)
            sp.wait_ge(zeroed, 2)
            for n, wv in enumerate((w1, w2)):
                q = sizes[n]
                @turns(sp, q // 2)
                def _(j):
                    for s in range(2):
                        sp.wait_ge(w_used[s], base[n] + j)
                        for p in range(2):
                            sp.dma_start(wb[64 * p:64 * p + 64, s, 0:q, 64 * p:64 * p + 64],
                                         wv[:, 2 * j + s, :, :]).then_inc(w_in[s], 16)
            sp.wait_ge(ready, 2)
            sp.dma_start(xs, res[:, :, :]).then_inc(stored, 16)
            sp.wait_ge(stored, 16)

        @block.gpsimd
        def _(pool):
            nc.gpsimd.memset(wb[:, :, :, :], 0.0).then_inc(zeroed, 1)
            nc.gpsimd.memset(zw[:, :], 0.0).then_inc(zeroed, 1)

        @block.tensor
        def _(pe):
            pe.wait_ge(zeroed, 2)
            pe.wait_ge(x_in, 64)
            for n in range(2):
                q = sizes[n]
                xq = xr[:, :, :].rearrange("p a (y i x k) -> p i k a y x", i=q, k=q, x=W // q)
                nc.tensor.matmul(acc[n][:, :, :], zw[:, :], xq[:, 0, 0], start=True, stop=False)
                @turns(pe, q // 2)
                def _(j):
                    for s in range(2):
                        pe.wait_ge(w_in[s], 32 * (base[n] + j) + 32)
                        for k in range(q):
                            mm = nc.tensor.matmul(acc[n][:, :, :], wb[:, s, k, :], xq[:, 2 * j + s, k],
                                                  start=False, stop=False)
                        mm.then_inc(w_used[s], 1)
                nc.tensor.matmul(acc[n][:, :, :], zw[:, :], xq[:, 0, 0], start=False, stop=True).then_inc(summed, 1)

        @block.scalar
        def _(act):
            act.wait_ge(b_in, 16)
            for n, (a, b) in enumerate(((0, NK1), (NK1, NK))):
                act.wait_ge(summed, n + 1)
                nc.scalar.activation(res[:, :, a:b], acc[n][:, :, :], ACT.Identity, bias=bs[:, n:n + 1]).then_inc(ready, 1)


def keys_and_values(nc, xs, ident, ln, wk, bk, part_rows, wv, dwv, k_out, v_out):
    PC, NCH = 80, 4
    with Stage(nc, "kv") as st:
        idn = st.sb("idn", [128, 128])
        x0 = st.sb("x0", [128, 2, NK])
        lns = st.sb("lns", [128, 4])
        wks = st.sb("wks", [128, 2, 2, NH, NB])
        bks = st.sb("bks", [NB, 2, NH])
        taken = st.sb("taken", [NB, 2])
        wvs = st.sb("wvs", [128, 2, 128])
        dws = st.sb("dws", [128, 11])
        xt = st.sb("xt", [PC, 8, 2, 64])
        xsq = st.sb("xsq", [PC, 8, 2, 64])
        mean = st.sb("mean", [PC, 8, 2])
        var = st.sb("var", [PC, 8, 2])
        std = st.sb("std", [PC, 8, 2])
        rstd = st.sb("rstd", [PC, 8, 2])
        xn = st.sb("xn", [128, 2, NK])
        kf = st.sb("kf", [NB, 4 * NH, NK])
        k1 = st.sb("k1", [NB, 4 * NH, NK], BF16)
        kr = st.sb("kr", [NB, 4 * NH, NK])
        kt = st.sb("kt", [NM, 4 * NH, NK], BF16)
        vp1 = st.sb("vp1", [128, 2, 18, 18])
        vp2 = st.sb("vp2", [128, 2, 10, 10])
        vd = st.sb("vd", [128, 2, NK + NK2])
        va = st.sb("va", [128, 4, VC])
        p_t = st.ps("p_t", [PC, 8, 128])
        p_b = st.ps("p_b", [128, 2, 512])
        p_k = [st.ps(f"p_k{s}", [NB, 512]) for s in range(2)]
        p_v = st.ps("p_v", [128, 2, 512])
        loaded, turned, step = st.sem("loaded"), st.sem("turned"), st.sem("step")
        normed, back, affine = st.sem("normed"), st.sem("back"), st.sem("affine")
        v_done, v_padded, k_done, k_ready = st.sem("v_done"), st.sem("v_padded"), st.sem("k_done"), st.sem("k_ready")
        var_ready, rooted, zeroed, convolved = st.sem("var_ready"), st.sem("rooted"), st.sem("zeroed"), st.sem("convolved")
        k_first, k_rest, k_split = st.sem("k_first"), st.sem("k_rest"), st.sem("k_split")
        vt_done, v_ready, stored = st.sem("vt_done"), st.sem("v_ready"), st.sem("stored")
        block = st.block()
        chunks = [(a, c) for a in range(2) for c in range(NCH)]

        @block.sync
        def _(sp):
            for dst, src in ((idn[:, :], ident), (x0[:, :, :], xs), (lns[:, :], ln), (wks[:, :, :, :], wk),
                             (bks[:, :, :], bk), (taken[:, :], part_rows), (wvs[:, :, :], wv), (dws[:, :], dwv)):
                sp.dma_start(dst, src).then_inc(loaded, 16)
            sp.wait_ge(k_split, 1)
            sp.wait_ge(zeroed, 10)
            sp.dma_start(k_out.rearrange("b p n -> p b n"), kt[:, :, :].rearrange("p (b h) n -> p b (h n)", b=4)).then_inc(stored, 16)
            sp.wait_ge(v_ready, 32)
            sp.dma_start(v_out.rearrange("b p n -> p b n"), va[:, :, :]).then_inc(stored, 16)
            sp.wait_ge(stored, 32)

        @block.gpsimd
        def _(pool):
            nc.gpsimd.memset(vp1[:, :, :, :], 0.0).then_inc(zeroed, 1)
            nc.gpsimd.memset(vp2[:, :, :, :], 0.0).then_inc(zeroed, 1)
            nc.gpsimd.memset(va[:, :, :], 0.0).then_inc(zeroed, 1)
            pool.wait_ge(zeroed, 3)
            for h in range(NH):
                o = 160 * h + HD
                nc.gpsimd.memset(va[:, :, o:512 + o + 1:512], 1.0).then_inc(zeroed, 1)
                pool.wait_ge(zeroed, 4 + h)
            for q in range(2):
                o = 1024 + 32 * q + HD
                nc.gpsimd.memset(va[64 * q:64 * q + 64, :, o:o + 193:192], 1.0).then_inc(zeroed, 1)
                pool.wait_ge(zeroed, 8 + q)
            nc.gpsimd.memset(kt[NB:NM, :, :], 1.0).then_inc(zeroed, 1)
            pool.wait_ge(zeroed, 10)

        @block.tensor
        def _(pe):
            pe.wait_ge(loaded, 128)
            for a, c in chunks:
                mm = nc.tensor.transpose(p_t[:, 4 * a + c, :], x0[:, a, c * PC:(c + 1) * PC], idn[:, :])
            mm.then_inc(turned, 1)
            pe.wait_ge(normed, 1)
            for a, c in chunks:
                mm = nc.tensor.transpose(p_b[:, a, c * PC:(c + 1) * PC], xt[:, 4 * a + c].rearrange("p b c -> p (b c)"),
                                         idn[0:PC, 0:PC])
            mm.then_inc(back, 1)
            pe.wait_ge(affine, 2)
            for a in range(2):
                nc.tensor.matmul(p_v[:, a, 0:NK1], wvs[:, 0, :], xn[:, a, 0:NK1], start=True, stop=True)
                mm = nc.tensor.matmul(p_v[:, a, NK1:NK], wvs[:, 1, :], xn[:, a, NK1:NK], start=True, stop=True)
            mm.then_inc(v_done, 1)
            for b in range(4):
                for h in range(NH):
                    n = NH * b + h
                    if n >= 2:
                        pe.wait_ge(k_ready, 2 * (n - 1))
                    o = p_k[n % 2]
                    nc.tensor.matmul(o[:, 0:NK1], wks[:, 0, b % 2, h, :], xn[:, b // 2, 0:NK1], start=True, stop=True)
                    nc.tensor.matmul(o[:, NK1:NK], wks[:, 1, b % 2, h, :], xn[:, b // 2, NK1:NK], start=True,
                                     stop=True).then_inc(k_done, 1)
            pe.wait_ge(convolved, 37)
            pe.wait_ge(v_padded, 4)
            for a in range(2):
                for c in range(3):
                    mm = nc.tensor.transpose(p_v[:, a, 128 * c:128 * c + 128], vd[:, a, 128 * c:128 * c + 128], idn[:, :])
            mm.then_inc(vt_done, 1)

        @block.vector
        def _(dve):
            seen = [0]

            def link(ins):
                seen[0] += 1
                ins.then_inc(step, 1)
                dve.wait_ge(step, seen[0])

            def wide(t):
                return t[:, :, :].unsqueeze(3).broadcast_to([PC, 8, 2, 64])

            dve.wait_ge(turned, 1)
            link(nc.vector.tensor_copy(xt[:, :, :, :], p_t[:, :, :].rearrange("p n (b c) -> p n b c", b=2)))
            link(nc.vector.tensor_reduce(mean[:, :, :], xt[:, :, :, :], AX.X, ALU.add))
            link(nc.vector.tensor_scalar(mean[:, :, :], mean[:, :, :], 1.0 / C, None, ALU.mult))
            link(nc.vector.tensor_tensor(xt[:, :, :, :], xt[:, :, :, :], wide(mean), ALU.subtract))
            link(nc.vector.tensor_tensor(xsq[:, :, :, :], xt[:, :, :, :], xt[:, :, :, :], ALU.mult))
            link(nc.vector.tensor_reduce(var[:, :, :], xsq[:, :, :, :], AX.X, ALU.add))
            nc.vector.tensor_scalar(var[:, :, :], var[:, :, :], 1.0 / C, EPS, ALU.mult, ALU.add).then_inc(var_ready, 1)
            dve.wait_ge(rooted, 1)
            link(nc.vector.reciprocal(rstd[:, :, :], std[:, :, :]))
            nc.vector.tensor_tensor(xt[:, :, :, :], xt[:, :, :, :], wide(rstd), ALU.mult).then_inc(normed, 1)
            dve.wait_ge(back, 1)
            for n, (a, b) in enumerate(((0, NK1), (NK1, NK))):
                nc.vector.tensor_scalar(xn[:, :, a:b], p_b[:, :, a:b], lns[:, 2 * n:2 * n + 1], lns[:, 2 * n + 1:2 * n + 2],
                                        ALU.mult, ALU.add).then_inc(affine, 1)
            dve.wait_ge(v_padded, 4)
            done = [0]
            for t in range(9):
                if t:
                    dve.wait_ge(convolved, 4 * t)
                for a in range(2):
                    for vp, q, o in ((vp1, 16, 0), (vp2, 8, NK1)):
                        src = vp[:, a, t // 3:t // 3 + q, t % 3:t % 3 + q]
                        dst = vd[:, a, o:o + q * q].rearrange("p (y x) -> p y x", y=q)
                        if t == 0:
                            nc.vector.tensor_scalar(dst, src, dws[:, 0:1], None, ALU.mult).then_inc(convolved, 1)
                        else:
                            nc.vector.scalar_tensor_tensor(dst, src, dws[:, t:t + 1], dst, ALU.mult, ALU.add).then_inc(convolved, 1)
            dve.wait_ge(convolved, 36)
            nc.vector.tensor_copy(vd[:, :, NK:NK + NK2], vd[:, :, NK1:NK]).then_inc(convolved, 1)
            dve.wait_ge(k_first, 1)
            nc.vector.scalar_tensor_tensor(kr[:, :, :], k1[:, :, :], taken[:, 0:1], kf[:, :, :], ALU.mult, ALU.add).then_inc(k_rest, 1)
            dve.wait_ge(k_rest, 2)
            nc.vector.scalar_tensor_tensor(kt[0:NB, :, :], k1[:, :, :], taken[:, 1:2], kr[:, :, :], ALU.mult, ALU.add).then_inc(k_split, 1)
            dve.wait_ge(vt_done, 1)
            dve.wait_ge(zeroed, 9)
            for b in range(4):
                src = p_v[:, b // 2, 0:384].rearrange("p (c q h d) -> p c q h d", c=3, q=2, h=NH)[:, :, b % 2]
                for h in range(NH):
                    o = 160 * h
                    dst = va[:, b, 0:1024].rearrange("p (c n) -> p c n", c=2)[:, :, o:o + HD]
                    nc.vector.tensor_copy(dst, src[:, 0:2, h]).then_inc(v_ready, 1)
                for h in range(NH):
                    r = slice(64 * (h % 2), 64 * (h % 2) + 64)
                    o = 1024 + 128 * (h // 2) + 32 * h
                    nc.vector.tensor_copy(va[r, b, o:o + HD], src[r, 2, h]).then_inc(v_ready, 1)

        @block.scalar
        def _(act):
            act.wait_ge(var_ready, 1)
            nc.scalar.activation(std[:, :, :], var[:, :, :], ACT.Sqrt).then_inc(rooted, 1)
            act.wait_ge(zeroed, 2)
            act.wait_ge(v_done, 1)
            for a in range(2):
                for vp, q, o, n in ((vp1, 16, 0, 0), (vp2, 8, NK1, 1)):
                    nc.scalar.activation(vp[:, a, 1:q + 1, 1:q + 1], p_v[:, a, o:o + q * q].rearrange("p (y x) -> p y x", y=q),
                                         ACT.Identity, bias=dws[:, 9 + n:10 + n]).then_inc(v_padded, 1)
            for n in range(4 * NH):
                act.wait_ge(k_done, n + 1)
                for m, (u, v) in enumerate(((0, NK1), (NK1, NK))):
                    nc.scalar.activation(kf[:, n, u:v], p_k[n % 2][:, u:v], ACT.Identity,
                                         bias=bks[:, m, n % NH:n % NH + 1]).then_inc(k_ready, 1)
            act.wait_ge(k_ready, 8 * NH)
            nc.scalar.activation(k1[:, :, :], kf[:, :, :], ACT.Copy).then_inc(k_first, 1)
            act.wait_ge(k_rest, 1)
            nc.scalar.activation(k1[:, :, :], kr[:, :, :], ACT.Copy).then_inc(k_rest, 1)


def query_parts(nc, xf, wq, bq, qp):
    N, QC = 2 * HW // 1024, 512
    xv = xf.rearrange("(a p) c h w -> (p c) a (h w)", a=2)
    with Stage(nc, "queries") as st:
        w = st.sb("w", [128, 128])
        bias = st.sb("bias", [128, 1])
        xs = st.sb("xs", [128, 2, 2, QC])
        qf = st.sb("qf", [128, 2, 2, QC])
        rest = st.sb("rest", [128, 2, 2, QC])
        parts = st.sb("parts", [128, 2, 3, 2, QC], BF16)
        p_q = [st.ps(f"p_q{s}", [128, 2, QC]) for s in range(2)]
        w_in, x_in, q_done, q_ready = st.sem("w_in"), st.sem2("x_in"), st.sem2("q_done"), st.sem2("q_ready")
        first, rested, second, third, stored = (st.sem2(n) for n in ("first", "rested", "second", "third", "stored"))
        block = st.block()
        half = HW // 1024

        def at(v, a, j):
            return v[:, a, bass.ds(j * 1024, 1024)]

        @block.sync
        def _(sp):
            sp.dma_start(w[:, :], wq).then_inc(w_in, 16)
            sp.dma_start(bias[:, :], bq).then_inc(w_in, 16)

            def load(j, s):
                sp.dma_start(xs[:, s].rearrange("p a n -> p (a n)"), at(xv, s, j)).then_inc(x_in[s], 16)

            def store(j, s):
                sp.wait_ge(first[s], j + 1)
                sp.wait_ge(second[s], j + 1)
                sp.wait_ge(third[s], j + 1)
                for k in range(3):
                    dst = qp[k].rearrange("(a p) c n -> (p c) a n", a=2)
                    sp.dma_start(at(dst, s, j), parts[:, s, k].rearrange("p a n -> p (a n)")).then_inc(stored[s], 16)

            for s in range(2):
                load(0, s)
            @turns(sp, half - 1)
            def _(j):
                for s in range(2):
                    sp.wait_ge(q_done[s], j + 1)
                    load(j + 1, s)
                for s in range(2):
                    store(j, s)
            for s in range(2):
                store(half - 1, s)
            for s in range(2):
                sp.wait_ge(stored[s], 48 * half)

        @block.tensor
        def _(pe):
            pe.wait_ge(w_in, 32)
            @turns(pe, half)
            def _(j):
                for s in range(2):
                    pe.wait_ge(x_in[s], 16 * j + 16)
                    pe.wait_ge(q_ready[s], j)
                    for a in range(2):
                        mm = nc.tensor.matmul(p_q[s][:, a, :], w[:, :], xs[:, s, a, :], start=True, stop=True)
                    mm.then_inc(q_done[s], 1)

        @block.scalar
        def _(act):
            act.wait_ge(w_in, 32)
            @turns(act, half)
            def _(j):
                for s in range(2):
                    act.wait_ge(q_done[s], j + 1)
                    act.wait_ge(rested[s], j)
                    nc.scalar.activation(qf[:, s], p_q[s][:, :, :], ACT.Identity, bias=bias[:, 0:1]).then_inc(q_ready[s], 1)
                    act.wait_ge(stored[s], 48 * j)
                    act.wait_ge(q_ready[s], j + 1)
                    nc.scalar.activation(parts[:, s, 0], qf[:, s], ACT.Copy).then_inc(first[s], 1)
                for s in range(2):
                    act.wait_ge(rested[s], j + 1)
                    nc.scalar.activation(parts[:, s, 1], rest[:, s], ACT.Copy).then_inc(second[s], 1)

        @block.vector
        def _(dve):
            @turns(dve, half)
            def _(j):
                for s in range(2):
                    dve.wait_ge(first[s], j + 1)
                    dve.wait_ge(third[s], j)
                    nc.vector.tensor_tensor(rest[:, s], qf[:, s], parts[:, s, 0], ALU.subtract).then_inc(rested[s], 1)
                for s in range(2):
                    dve.wait_ge(second[s], j + 1)
                    nc.vector.tensor_tensor(parts[:, s, 2], rest[:, s], parts[:, s, 1], ALU.subtract).then_inc(third[s], 1)


def attention(nc, x, qp, kd, vdr, ident, dsel, wp, bp, x1, st1):
    QC, T = 512, 4
    NCH = HW // QC
    U = 4
    NR = NCH // U
    UNITS = ((0,), (1,), (0, 1), (2,), (3,), (2, 3))
    with Stage(nc, "attention") as st:
        qs = st.sb("qs", [NM, U, NH, QC], BF16)
        ks = st.sb("ks", [NM, NH, NK], BF16)
        vs = st.sb("vs", [128, VC])
        idb = st.sb("idb", [128, 128], BF16)
        idf = st.sb("idf", [128, 128])
        sel = st.sb("sel", [128, 128])
        wps = st.sb("wps", [128, C])
        bps = st.sb("bps", [C, 1])
        xs = st.sb("xs", [C, U, QC])
        nm = st.sb("nm", [128, U, T, NH])
        nr = st.sb("nr", [128, U, T, NH])
        mp = st.sb("mp", [128, U, T, 3, NH], BF16)
        mr = st.sb("mr", [3 * NH, U, QC], BF16)
        pr = st.sb("pr", [128, 3, 2, QC])
        os = st.sb("os", [128, U, QC])
        rc = st.sb("rc", [128, U, QC])
        on = st.sb("on", [128, U, QC])
        out = st.sb("out", [C, U, QC])
        bn = st.sb("bn", [C, U, 6])
        p_s = [st.ps(f"p_s{s}", [128, 512]) for s in range(2)]
        p_t = [st.ps(f"p_t{s}", [128, 2, 512]) for s in range(2)]
        p_o = st.ps("p_o", [128, 512])
        p_m = st.ps("p_m", [128, 512])
        p_mb = p_m[:, :].bitcast(BF16)
        c_in, kv_in, casted = st.sem("c_in"), st.sem("kv_in"), st.sem("casted")
        q_in, x_in, m_in, out_stored = ([st.sem(f"{n}{u}") for u in range(U)] for n in ("q_in", "x_in", "m_in", "out_stored"))
        s_done, s_max, t_done = st.sem2("s_done"), st.sem2("s_max"), st.sem2("t_done")
        exp_done, pv_done = ([st.sem(f"{n}{p}") for p in range(3)] for n in ("exp_done", "pv_done"))
        m_split, m_turned, m_row = st.sem("m_split"), st.sem("m_turned"), st.sem("m_row")
        o_copied, d_done, d_taken, o_normed = st.sem("o_copied"), st.sem("d_done"), st.sem("d_taken"), st.sem("o_normed")
        p_done, out_ready, bn_ready = st.sem("p_done"), st.sem("out_ready"), st.sem("bn_ready")
        block = st.block()
        xv = x.rearrange("b c h w -> b c (h w)")
        ov = x1.rearrange("b c h w -> b c (h w)")


        def rounds(eng, before, one_round, after):
            @turns(eng, B)
            def _(b):
                before(b)
                one_round(b, 0, b * NR, True, False)
                with eng.Fori(1, NR - 1) as r:
                    one_round(b, r, b * NR + r, False, False)
                one_round(b, NR - 1, b * NR + (NR - 1), False, True)
                after(b)

        @block.sync
        def _(sp):
            def load_q(b, r, u):
                for k0, parts in ((0, (0, 0)), (32, (1, 1)), (64, (0, 2))):
                    for i, k in enumerate(parts):
                        src = qp[k, b].rearrange("(h d) n -> d h n", h=NH)[:, :, bass.ds((r * U + u) * QC, QC)]
                        sp.dma_start(qs[k0 + HD * i:k0 + HD * i + HD, u], src).then_inc(q_in[u], 16)

            def load_x(b, r, u):
                sp.dma_start(xs[:, u, :], xv[b][:, bass.ds((r * U + u) * QC, QC)]).then_inc(x_in[u], 16)

            def max_rows(n, u):
                sp.wait_ge(m_row, U * n + u + 1)
                for k in range(3):
                    sp.dma_start(qs[NB + k:NB + k + 1, u, :, :], mr[NH * k:NH * k + NH, u, :]).then_inc(m_in[u], 16)

            def store(b, r, n, u):
                sp.wait_ge(bn_ready, U * n + u + 1)
                sp.dma_start(ov[b][:, bass.ds((r * U + u) * QC, QC)], out[:, u, :]).then_inc(out_stored[u], 16)
                sp.dma_start(st1[b, :, r * U + u, :], bn[:, u, :]).then_inc(out_stored[u], 16)

            def before(b):
                sp.wait_ge(out_ready, NCH * b)
                sp.dma_start(ks[:, :, :].rearrange("p h n -> p (h n)"), kd[b]).then_inc(kv_in, 16)
                sp.dma_start(vs[:, :], vdr[b]).then_inc(kv_in, 16)
                for u in range(U):
                    load_q(b, 0, u)
                for u in range(U):
                    load_x(b, 0, u)
                for u in range(2):
                    max_rows(b * NR, u)

            def one_round(b, r, n, first, last):
                for u in range(U):
                    if u:
                        store(b, r, n, u - 1)
                        if not last:
                            load_x(b, r + 1, u - 1)
                    elif not first:
                        store(b, r - 1, n - 1, U - 1)
                        load_x(b, r, U - 1)
                    if u < 2:
                        max_rows(n, u + 2)
                    elif not last:
                        max_rows(n + 1, u - 2)
                    if not last:
                        sp.wait_ge(pv_done[2], 2 * (U * n + u) + 2)
                        load_q(b, r + 1, u)

            for dst, src in ((idf[:, :], ident), (sel[:, :], dsel), (wps[:, :], wp), (bps[:, :], bp)):
                sp.dma_start(dst, src).then_inc(c_in, 16)
            rounds(sp, before, one_round, lambda b: store(b, NR - 1, b * NR + (NR - 1), U - 1))
            for u in range(U):
                sp.wait_ge(out_stored[u], 32 * B * NR)

        @block.tensor
        def _(pe):
            def score(n, u, i):
                t, h = i // NH, i % NH
                pe.wait_ge(s_max[i % 2], 8 * (U * n + u) + i // 2)
                nc.tensor.matmul(p_s[i % 2][:, 0:NK], qs[0:NB, u, h, 128 * t:128 * t + 128], ks[0:NB, h, :],
                                 start=True, stop=True).then_inc(s_done[i % 2], 1)

            def turn_max(n, u, projected):
                pe.wait_ge(m_split, 4 * (U * n + u) + 4)
                pe.wait_ge(m_row, U * n + u)
                pe.wait_ge(out_ready, projected)
                for t in range(T):
                    mm = nc.tensor.transpose(p_mb[0:3 * NH, 128 * t:128 * t + 128],
                                             mp[:, u, t].rearrange("p k h -> p (k h)"), idb[:, :])
                mm.then_inc(m_turned, 1)

            def scores_t(n, u, v):
                m = U * n + u
                pe.wait_ge(exp_done[(v - 2) % 3], 2 * m + (v + 1) // 3 if v >= 2 else 2 * m)
                o = p_t[v % 2]
                if len(UNITS[v]) == 1:
                    h = UNITS[v][0]
                    for c in range(2):
                        mm = nc.tensor.matmul(o[:, c, :], ks[:, h, 128 * c:128 * c + 128], qs[:, u, h, :], start=True, stop=True)
                else:
                    for q, h in enumerate(UNITS[v]):
                        mm = nc.tensor.matmul(o[64 * q:64 * q + 64, 0, :], ks[:, h, NK1:NK], qs[:, u, h, :], start=True, stop=True)
                mm.then_inc(t_done[v % 2], 1)

            def product(n, u, v, c):
                h = UNITS[v][0]
                single = len(UNITS[v]) == 1
                if c == 0:
                    pe.wait_ge(exp_done[v % 3], 2 * (U * n + u) + v // 3 + 1)
                if single or c == 0:
                    o = 128 * (NH * c + h if single else 2 * NH + h // 2)
                    mm = nc.tensor.matmul(p_o[:, :], vs[:, o:o + 128], pr[:, v % 3, c, :],
                                          start=(v == 0 and c == 0), stop=(v == 5))
                    if c == 1 or not single:
                        mm.then_inc(pv_done[v % 3], 1)

            def denominators(n, u, rows_before):
                m = U * n + u
                pe.wait_ge(o_copied, m + 1)
                pe.wait_ge(m_row, rows_before)
                pe.wait_ge(out_ready, m)
                nc.tensor.matmul(p_m[:, :], sel[:, :], os[:, u, :], start=True, stop=True).then_inc(d_done, 1)

            def project(n, u):
                pe.wait_ge(o_normed, U * n + u + 1)
                nc.tensor.matmul(p_m[0:C, :], wps[:, :], on[:, u, :], start=True, stop=True).then_inc(p_done, 1)

            def before(b):
                n = b * NR
                pe.wait_ge(kv_in, 32 * b + 32)
                for u in range(2):
                    pe.wait_ge(q_in[u], 96 * n + 96)
                    for i in range(16):
                        score(n, u, i)
                    turn_max(n, u, NCH * b)

            def one_round(b, r, n, first, last):
                for u in range(U):
                    m = U * n + u
                    ahead = (n, u + 2) if u < 2 else None if last else (n + 1, u - 2)
                    prior = (n, u - 1) if u else None if first else (n - 1, U - 1)
                    pe.wait_ge(m_in[u], 48 * n + 48)
                    if ahead:
                        pe.wait_ge(q_in[ahead[1]], 96 * ahead[0] + 96)
                    for v in range(6):
                        scores_t(n, u, v)
                        if ahead:
                            score(*ahead, 3 * v)
                        if v == 1 and prior:
                            denominators(*prior, m + 1 if last and u == 3 else m + 2)
                        if v == 4 and prior:
                            project(*prior)
                        if v == 1:
                            pe.wait_ge(o_copied, m)
                        for c in range(2):
                            if v:
                                product(n, u, v - 1, c)
                            if ahead and 3 * v + c + 1 < 16:
                                score(*ahead, 3 * v + c + 1)
                    for c in range(2):
                        product(n, u, 5, c)
                    if ahead:
                        turn_max(*ahead, m if prior else NCH * b)

            def after(b):
                n = b * NR + (NR - 1)
                denominators(n, U - 1, NCH * b + NCH)
                project(n, U - 1)

            pe.wait_ge(c_in, 64)
            pe.wait_ge(casted, 1)
            rounds(pe, before, one_round, after)

        @block.scalar
        def _(act):
            def exponentials(n, u, v):
                m = U * n + u
                act.wait_ge(t_done[v % 2], 3 * m + v // 2 + 1)
                act.wait_ge(pv_done[v % 3], 2 * m + v // 3)
                c = 2 if len(UNITS[v]) == 1 else 1
                nc.scalar.activation(pr[:, v % 3, 0:c], p_t[v % 2][:, 0:c, :], ACT.Exp, scale=HD ** -0.5).then_inc(exp_done[v % 3], 1)

            def copy_rows(n, u):
                act.wait_ge(m_turned, U * n + u + 1)
                act.wait_ge(m_in[u], 48 * n)
                nc.scalar.activation(mr[:, u, :], p_mb[0:3 * NH, 0:QC], ACT.Copy).then_inc(m_row, 1)

            def copy_out(n, u):
                m = U * n + u
                act.wait_ge(pv_done[2], 2 * m + 2)
                act.wait_ge(o_normed, U * n)
                nc.scalar.activation(os[:, u, :], p_o[:, :], ACT.Copy).then_inc(o_copied, 1)

            def before(b):
                for u in range(2):
                    copy_rows(b * NR, u)

            def one_round(b, r, n, first, last):
                for u in range(U):
                    if u:
                        copy_out(n, u - 1)
                    elif not first:
                        copy_out(n - 1, U - 1)
                    for v in range(6):
                        exponentials(n, u, v)
                    if u < 2:
                        copy_rows(n, u + 2)
                    elif not last:
                        copy_rows(n + 1, u - 2)

            act.wait_ge(c_in, 64)
            nc.scalar.activation(idb[:, :], idf[:, :], ACT.Copy).then_inc(casted, 1)
            rounds(act, before, one_round, lambda b: copy_out(b * NR + (NR - 1), U - 1))

        @block.vector
        def _(dve):
            def maximum(n, u, i):
                m = U * n + u
                dve.wait_ge(s_done[i % 2], 8 * m + i // 2 + 1)
                nc.vector.tensor_reduce(nm[:, u, i // NH, i % NH:i % NH + 1], p_s[i % 2][:, 0:NK], AX.X, ALU.max,
                                        negate=True).then_inc(s_max[i % 2], 1)

            def split_max(n, u):
                m = U * n + u
                dve.wait_ge(s_max[0], 8 * m + 8)
                dve.wait_ge(s_max[1], 8 * m + 8)
                dve.wait_ge(m_turned, U * n)
                nc.vector.tensor_copy(mp[:, u, :, 0, :], nm[:, u]).then_inc(m_split, 1)
                dve.wait_ge(m_split, 4 * m + 1)
                nc.vector.tensor_tensor(nr[:, u], nm[:, u], mp[:, u, :, 0, :], ALU.subtract).then_inc(m_split, 1)
                dve.wait_ge(m_split, 4 * m + 2)
                nc.vector.tensor_copy(mp[:, u, :, 1, :], nr[:, u]).then_inc(m_split, 1)
                dve.wait_ge(m_split, 4 * m + 3)
                nc.vector.tensor_tensor(mp[:, u, :, 2, :], nr[:, u], mp[:, u, :, 1, :], ALU.subtract).then_inc(m_split, 1)

            def invert(n, u, k):
                m = U * n + u
                dve.wait_ge(d_done, m + 1)
                cols = slice(128 * k, 128 * k + 128)
                nc.vector.reciprocal(rc[:, u, cols], p_m[:, cols]).then_inc(d_taken, 1)

            def norm(n, u):
                m = U * n + u
                dve.wait_ge(d_taken, 4 * m + 4)
                dve.wait_ge(p_done, U * n)
                nc.vector.tensor_tensor(on[:, u, :], os[:, u, :], rc[:, u, :], ALU.mult).then_inc(o_normed, 1)

            def finish(n, u):
                m = U * n + u
                dve.wait_ge(p_done, m + 1)
                dve.wait_ge(x_in[u], 16 * n + 16)
                dve.wait_ge(out_stored[u], 32 * n)
                nc.vector.scalar_tensor_tensor(out[:, u, :], p_m[0:C, :], bps[:, 0:1], xs[:, u, :], ALU.add,
                                               ALU.add).then_inc(out_ready, 1)
                dve.wait_ge(out_ready, m + 1)
                nc.vector.bn_stats(bn[:, u, :], out[:, u, :]).then_inc(bn_ready, 1)

            def before(b):
                for u in range(2):
                    for i in range(16):
                        maximum(b * NR, u, i)
                    split_max(b * NR, u)

            def one_round(b, r, n, first, last):
                for u in range(U):
                    ahead = (n, u + 2) if u < 2 else None if last else (n + 1, u - 2)
                    prior = (n, u - 1) if u else None if first else (n - 1, U - 1)
                    for i in range(16):
                        if prior and i in (3, 5, 7, 9):
                            invert(*prior, i // 2 - 1)
                        if i == 11 and prior:
                            norm(*prior)
                        if i == 15 and prior:
                            finish(*prior)
                        if ahead:
                            maximum(*ahead, i)
                    if ahead:
                        split_max(*ahead)

            dve.wait_ge(c_in, 64)

            def after(b):
                for k in range(4):
                    invert(b * NR + (NR - 1), U - 1, k)
                norm(b * NR + (NR - 1), U - 1)
                finish(b * NR + (NR - 1), U - 1)

            rounds(dve, before, one_round, after)


MD = 32
G8 = 8


def low_spectrum(nc, name, src, c_h, c_w, low):
    xv = src.rearrange("b c h w -> h (b c) w")
    N = B * C // G8 // 2
    with Stage(nc, name) as st:
        ch = st.sb("ch", [128, 2 * MD])
        cw = st.sb("cw", [128, 2, 2 * MD])
        xs = st.sb("xs", [128, 2, G8, W])
        rows = st.sb("rows", [128, 2, 2, G8, MD])
        res = st.sb("res", [2 * MD, 2, G8, MD])
        p_rows = [st.ps(f"p_rows{s}", [128, G8, 2 * MD]) for s in range(2)]
        p_low = [st.ps(f"p_low{s}", [2 * MD, 512]) for s in range(2)]
        consts_in = st.sem("consts_in")
        x_in, rows_done, rows_copied = st.sem2("x_in"), st.sem2("rows_done"), st.sem2("rows_copied")
        low_done, low_copied, stored = st.sem2("low_done"), st.sem2("low_copied"), st.sem2("stored")
        block = st.block()

        @block.sync
        def _(sp):
            def load(j, s):
                sp.dma_start(xs[:, s], xv[:, bass.ds((2 * j + s) * G8, G8), :]).then_inc(x_in[s], 16)

            def store(j, s):
                sp.wait_ge(low_copied[s], j + 1)
                sp.dma_start(low[:, bass.ds((2 * j + s) * G8, G8), :], res[:, s]).then_inc(stored[s], 16)

            sp.dma_start(ch[:, :], c_h).then_inc(consts_in, 16)
            sp.dma_start(cw[:, :, :], c_w).then_inc(consts_in, 16)
            for s in range(2):
                load(0, s)
            @turns(sp, N - 1)
            def _(j):
                for s in range(2):
                    sp.wait_ge(rows_done[s], j + 1)
                    load(j + 1, s)
                for s in range(2):
                    store(j, s)
            for s in range(2):
                store(N - 1, s)
            for s in range(2):
                sp.wait_ge(stored[s], 16 * N)

        @block.tensor
        def _(pe):
            pe.wait_ge(consts_in, 32)
            @turns(pe, N)
            def _(j):
                for s in range(2):
                    pe.wait_ge(x_in[s], 16 * j + 16)
                    pe.wait_ge(rows_copied[s], j)
                    for i in range(G8):
                        mm = nc.tensor.matmul(p_rows[s][:, i, :], xs[:, s, i, :], ch[:, :], start=True, stop=True)
                    mm.then_inc(rows_done[s], 1)
                for s in range(2):
                    pe.wait_ge(rows_copied[s], j + 1)
                    pe.wait_ge(low_copied[s], j)
                    o = p_low[s][:, 0:G8 * MD]
                    for r in range(2):
                        mm = nc.tensor.matmul(o, cw[:, r, :], rows[:, s, r].rearrange("p i k -> p (i k)"),
                                              start=(r == 0), stop=(r == 1))
                    mm.then_inc(low_done[s], 1)

        @block.scalar
        def _(act):
            @turns(act, N)
            def _(j):
                for s in range(2):
                    act.wait_ge(rows_done[s], j + 1)
                    act.wait_ge(low_done[s], j)
                    nc.scalar.activation(rows[:, s].rearrange("p r i k -> p i r k"),
                                         p_rows[s][:, :, :].rearrange("p i (r k) -> p i r k", r=2), ACT.Copy)\
                        .then_inc(rows_copied[s], 1)

        @block.vector
        def _(dve):
            @turns(dve, N)
            def _(j):
                for s in range(2):
                    dve.wait_ge(low_done[s], j + 1)
                    dve.wait_ge(stored[s], 16 * j)
                    nc.vector.tensor_copy(res[:, s], p_low[s][:, 0:G8 * MD].rearrange("p (i k) -> p i k", i=G8)).then_inc(low_copied[s], 1)


def fourier_mlp(nc, low, st1, gmat, gwb, sign, w1, w2, bias, modes, gn_out):
    K2 = MD * MD
    with Stage(nc, "mlp") as st:
        stt = st.sb("stt", [128, B, 32, 6])
        mv = st.sb("mv", [128, B, 2])
        g = st.sb("g", [128, 2, B])
        gm = st.sb("gm", [128, 128])
        gw = st.sb("gw", [128, 2])
        grp = st.sb("grp", [128, 2, B])
        var = st.sb("var", [128, B])
        std = st.sb("std", [128, B])
        ab = st.sb("ab", [128, 2, B])
        dc = st.sb("dc", [C, B])
        sg = st.sb("sg", [128, 128])
        ws = st.sb("ws", [128, 2, 128])
        wm = st.sb("wm", [128, 2, 128])
        bs = st.sb("bs", [128, 2])
        xs = st.sb("xs", [128, B, K2])
        hid = st.sb("hid", [128, B, K2])
        os = st.sb("os", [128, B, MD, MD])
        p_g = st.ps("p_g", [128, 2 * B])
        p_h = [st.ps(f"p_h{s}", [128, 512]) for s in range(2)]
        p_o = [st.ps(f"p_o{s}", [128, 512]) for s in range(2)]
        loaded, x_in, step = st.sem("loaded"), st.sem("x_in"), st.sem("step")
        sums_ready, grouped, var_ready, rooted = st.sem("sums_ready"), st.sem("grouped"), st.sem("var_ready"), st.sem("rooted")
        ab_ready, x_ready, w_ready = st.sem("ab_ready"), st.sem("x_ready"), st.sem("w_ready")
        h_done, h_ready, o_done, o_ready = st.sem2("h_done"), st.sem2("h_ready"), st.sem2("o_done"), st.sem2("o_ready")
        stored = st.sem("stored")
        NCK = B * K2 // 512
        block = st.block()

        @block.sync
        def _(sp):
            for q in range(2):
                sp.dma_start(stt[64 * q:64 * q + 64].rearrange("c b m s -> c b (m s)"),
                             st1.rearrange("b c m s -> c b (m s)")).then_inc(loaded, 16)
            for dst, src in ((gm[:, :], gmat), (gw[:, :], gwb), (sg[:, :], sign), (ws[:, 0, :], w1), (ws[:, 1, :], w2), (bs[:, :], bias)):
                sp.dma_start(dst, src).then_inc(loaded, 16)
            lv = low.rearrange("(r k) (b c) m -> r b c k m", r=2, b=B)
            for r in range(2):
                for b in range(B):
                    sp.dma_start(xs[64 * r:64 * r + 64, b].rearrange("c (k m) -> c k m", k=MD), lv[r, b]).then_inc(x_in, 16)
            sp.wait_ge(ab_ready, 2)
            sp.dma_start(gn_out, ab[0:C, :, :]).then_inc(stored, 16)
            for s in range(2):
                sp.wait_ge(o_ready[s], NCK // 2)
            for r in range(2):
                sp.dma_start(modes[r].rearrange("b c k m -> c b (k m)"), os[r * C:(r + 1) * C].rearrange("p b k m -> p b (k m)")).then_inc(stored, 16)
            sp.wait_ge(stored, 48)

        @block.vector
        def _(dve):
            seen = [0]

            def link(ins):
                seen[0] += 1
                ins.then_inc(step, 1)
                dve.wait_ge(step, seen[0])

            dve.wait_ge(loaded, 128)
            for i in range(2):
                nc.vector.tensor_tensor(wm[:, i, :], ws[:, i, :], sg[:, :], ALU.mult).then_inc(w_ready, 1)
            for b in range(B):
                last = nc.vector.bn_aggr(mv[:, b, :], stt[:, b].rearrange("p m s -> p (m s)"))
            link(last)
            link(nc.vector.tensor_copy(g[:, 0, :], mv[:, :, 0]))
            link(nc.vector.tensor_tensor(g[:, 1, :], mv[:, :, 0], mv[:, :, 0], ALU.mult))
            nc.vector.tensor_tensor(g[:, 1, :], g[:, 1, :], mv[:, :, 1], ALU.add).then_inc(sums_ready, 1)
            dve.wait_ge(grouped, 1)
            link(nc.vector.tensor_copy(grp[:, :, :], p_g[:, :].rearrange("p (a b) -> p a b", a=2)))
            link(nc.vector.tensor_tensor(var[:, :], grp[:, 0, :], grp[:, 0, :], ALU.mult))
            link(nc.vector.tensor_tensor(var[:, :], grp[:, 1, :], var[:, :], ALU.subtract))
            nc.vector.tensor_scalar(var[:, :], var[:, :], 0.0, EPS, ALU.max, ALU.add).then_inc(var_ready, 1)
            dve.wait_ge(rooted, 1)
            link(nc.vector.reciprocal(var[:, :], std[:, :]))
            nc.vector.tensor_scalar(ab[:, 0, :], var[:, :], gw[:, 0:1], None, ALU.mult).then_inc(ab_ready, 1)
            dve.wait_ge(ab_ready, 1)
            link(nc.vector.tensor_tensor(ab[:, 1, :], grp[:, 0, :], ab[:, 0, :], ALU.mult))
            nc.vector.tensor_scalar(ab[:, 1, :], ab[:, 1, :], -1.0, gw[:, 1:2], ALU.mult, ALU.add).then_inc(ab_ready, 1)
            dve.wait_ge(ab_ready, 2)
            link(nc.vector.tensor_scalar(dc[:, :], ab[0:C, 1, :], float(H), None, ALU.mult))
            dve.wait_ge(x_in, 128)
            for b in range(B):
                last = nc.vector.tensor_scalar(xs[:, b, :], xs[:, b, :], ab[:, 0, b:b + 1], None, ALU.mult)
            link(last)
            nc.vector.tensor_tensor(xs[0:C, :, 0], xs[0:C, :, 0], dc[:, :], ALU.add).then_inc(x_ready, 1)

        @block.tensor
        def _(pe):
            pe.wait_ge(sums_ready, 1)
            pe.wait_ge(loaded, 128)
            nc.tensor.matmul(p_g[:, :], gm[:, :], g[:, :, :].rearrange("p a b -> p (a b)"), start=True, stop=True).then_inc(grouped, 1)
            pe.wait_ge(w_ready, 2)
            pe.wait_ge(x_ready, 1)
            xv, hv = xs[:, :, :].rearrange("p b n -> p (b n)"), hid[:, :, :].rearrange("p b n -> p (b n)")
            for j in range(NCK // 2):
                for s in range(2):
                    if j:
                        pe.wait_ge(h_ready[s], j)
                    o = (2 * j + s) * 512
                    nc.tensor.matmul(p_h[s][:, :], wm[:, 0, :], xv[:, o:o + 512], start=True, stop=True).then_inc(h_done[s], 1)
            for j in range(NCK // 2):
                for s in range(2):
                    pe.wait_ge(h_ready[s], j + 1)
                    if j:
                        pe.wait_ge(o_ready[s], j)
                    o = (2 * j + s) * 512
                    nc.tensor.matmul(p_o[s][:, :], wm[:, 1, :], hv[:, o:o + 512], start=True, stop=True).then_inc(o_done[s], 1)

        @block.scalar
        def _(act):
            act.wait_ge(var_ready, 1)
            nc.scalar.activation(std[:, :], var[:, :], ACT.Sqrt).then_inc(rooted, 1)
            hv = hid[:, :, :].rearrange("p b n -> p (b n)")
            for j in range(NCK // 2):
                for s in range(2):
                    act.wait_ge(h_done[s], j + 1)
                    o = (2 * j + s) * 512
                    nc.scalar.activation(hv[:, o:o + 512], p_h[s][:, :], ACT.Gelu, bias=bs[:, 0:1]).then_inc(h_ready[s], 1)
            for j in range(NCK // 2):
                for s in range(2):
                    act.wait_ge(o_done[s], j + 1)
                    dst = os[:, j, :, 16 * s:16 * s + 16].rearrange("p k m -> p m k")
                    nc.scalar.activation(dst, p_o[s][:, :].rearrange("p (m k) -> p m k", m=16), ACT.Identity,
                                         bias=bs[:, 1:2]).then_inc(o_ready[s], 1)


def low_inverse(nc, name, modes, used, c_k, c_m, out):
    WO = out.shape[3]
    N = B * C // G8 // 2
    PB = G8 // 2
    with Stage(nc, name) as st:
        ck = st.sb("ck", [2 * MD, 2, H])
        cm = st.sb("cm", [128, 2, WO])
        ms = st.sb("ms", [2 * MD, 2, G8, MD])
        cols = st.sb("cols", [128, 2, G8 // 2, H])
        res = st.sb("res", [128, 2, G8, WO])
        p_cols = [st.ps(f"p_cols{s}", [128, G8 // 2, H]) for s in range(2)]
        p_img = [st.ps(f"p_img{s}", [128, 2, 512]) for s in range(2)]
        consts_in, zeroed = st.sem("consts_in"), st.sem("zeroed")
        m_in, cols_done, cols_copied = st.sem2("m_in"), st.sem2("cols_done"), st.sem2("cols_copied")
        img_done, img_copied, stored = st.sem2("img_done"), st.sem2("img_copied"), st.sem2("stored")
        block = st.block()

        def pv(s):
            return p_img[s][:, :, 0:PB * WO].rearrange("p a (i w) -> p a i w", i=PB)

        @block.gpsimd
        def _(pool):
            nc.gpsimd.memset(ms[:, :, :, :], 0.0).then_inc(zeroed, 1)

        @block.sync
        def _(sp):
            R = C // G8 // 2

            def load(j, s):
                for r in range(2):
                    src = modes[r, :, :, 0:used, 0:used].rearrange("b c k m -> k (b c) m")
                    sp.dma_start(ms[MD * r:MD * r + used, s, :, 0:used], src[:, bass.ds((2 * j + s) * G8, G8), :]).then_inc(m_in[s], 16)

            def store(b, g, s):
                sp.wait_ge(img_copied[s], b * R + g + 1)
                sp.dma_start(out[:, b, bass.ds((2 * g + s) * G8, G8), :], res[:, s]).then_inc(stored[s], 16)

            def both(b, g):
                for s in range(2):
                    sp.wait_ge(cols_done[s], b * R + g + 1)
                    load(b * R + g + 1, s)
                for s in range(2):
                    store(b, g, s)

            sp.dma_start(ck[:, :, :], c_k).then_inc(consts_in, 16)
            sp.dma_start(cm[:, :, :], c_m).then_inc(consts_in, 16)
            sp.wait_ge(zeroed, 1)
            for s in range(2):
                load(0, s)
            for b in range(B):
                with sp.Fori(0, R - (b == B - 1)) as g:
                    both(b, g)
            for s in range(2):
                store(B - 1, R - 1, s)
            for s in range(2):
                sp.wait_ge(stored[s], 16 * N)

        @block.tensor
        def _(pe):
            pe.wait_ge(consts_in, 32)
            @turns(pe, N)
            def _(j):
                for s in range(2):
                    pe.wait_ge(m_in[s], 32 * j + 32)
                    pe.wait_ge(cols_copied[s], j)
                    nc.tensor.matmul(p_cols[s][:, 0, 0:2], ck[:, 0, :], ck[:, 0, 0:2], start=True, stop=True)
                    for r in range(2):
                        for i in range(G8 // 2):
                            mm = nc.tensor.matmul(p_cols[s][64 * r:64 * r + 64, i, :], ms[:, s, 2 * i:2 * i + 2, :].rearrange("p i k -> p (i k)"),
                                                  ck[:, r, :], start=True, stop=True)
                    mm.then_inc(cols_done[s], 1)
                for s in range(2):
                    pe.wait_ge(cols_copied[s], j + 1)
                    pe.wait_ge(img_copied[s], j)
                    for i in range(0, G8, 2):
                        mm = nc.tensor.matmul(pv(s)[:, i // PB, i % PB:i % PB + 2, :].rearrange("p i w -> p (i w)"), cols[:, s, i // 2, :],
                                              cm[:, :, :].rearrange("p i w -> p (i w)"), start=True, stop=True)
                    mm.then_inc(img_done[s], 1)

        @block.scalar
        def _(act):
            @turns(act, N)
            def _(j):
                for s in range(2):
                    act.wait_ge(cols_done[s], j + 1)
                    act.wait_ge(img_done[s], j)
                    nc.scalar.activation(cols[:, s], p_cols[s][:, :, :], ACT.Copy).then_inc(cols_copied[s], 1)

        @block.vector
        def _(dve):
            @turns(dve, N)
            def _(j):
                for s in range(2):
                    dve.wait_ge(img_done[s], j + 1)
                    dve.wait_ge(stored[s], 16 * j)
                    nc.vector.tensor_copy(res[:, s].rearrange("p (a i) w -> p a i w", a=2), pv(s)).then_inc(img_copied[s], 1)


CH = 2048
NCK1 = HW // CH


def second_residual(nc, x1, y, gn1, hr, st2):
    xv = x1.rearrange("(a p) c h w -> (p c) a (h w)", a=2)
    yv = y.rearrange("(a p c) h w -> (p c) a (h w)", a=2, p=2)
    with Stage(nc, "resid") as st:
        ab = st.sb("ab", [128, 2, 2])
        a1 = st.sb("a1", [128, 2])
        xs = st.sb("xs", [128, 2, CH])
        ys = st.sb("ys", [128, 2, CH])
        ts = st.sb("ts", [128, 2, CH])
        ab_in, a1_ready = st.sem("ab_in"), st.sem("a1_ready")
        x_in, y_in, scaled, added, counted = (st.sem2(n) for n in ("x_in", "y_in", "scaled", "added", "counted"))
        block = st.block()

        @block.sync
        def _(sp):
            with nc.allow_non_contiguous_dma(reason="scale and shift of one batch per partition half"):
                gv = gn1.rearrange("c s (a p) -> p c s a", p=2)
                for p in range(2):
                    for s in range(2):
                        sp.dma_start(ab[64 * p:64 * p + 64, s, :], gv[p, :, s, :]).then_inc(ab_in, 16)
            for a in range(2):
                @turns(sp, NCK1 // 2)
                def _(j):
                    for s in range(2):
                        n = bass.ds((2 * j + s) * CH, CH)
                        sp.wait_ge(scaled[s], a * NCK1 // 2 + j)
                        sp.dma_start(xs[:, s, :], xv[:, a, n]).then_inc(x_in[s], 16)
                        sp.wait_ge(added[s], a * NCK1 // 2 + j)
                        sp.dma_start(ys[:, s, :], yv[:, a, n]).then_inc(y_in[s], 16)

        @block.scalar
        def _(act):
            act.wait_ge(a1_ready, 1)
            for a in range(2):
                @turns(act, NCK1 // 2)
                def _(j):
                    for s in range(2):
                        act.wait_ge(x_in[s], 16 * (a * NCK1 // 2) + 16 * j + 16)
                        act.wait_ge(added[s], a * NCK1 // 2 + j)
                        nc.scalar.activation(ts[:, s, :], xs[:, s, :], ACT.Identity, scale=a1[:, a:a + 1],
                                             bias=ab[:, 1, a:a + 1]).then_inc(scaled[s], 1)

        @block.gpsimd
        def _(pool):
            for a in range(2):
                @turns(pool, NCK1 // 2)
                def _(j):
                    for s in range(2):
                        pool.wait_ge(scaled[s], a * NCK1 // 2 + j + 1)
                        pool.wait_ge(y_in[s], 16 * (a * NCK1 // 2) + 16 * j + 16)
                        nc.gpsimd.tensor_tensor(hr[:, a, bass.ds((2 * j + s) * CH, CH)], ts[:, s, :], ys[:, s, :],
                                                ALU.add).then_inc(added[s], 1)

        @block.vector
        def _(dve):
            dve.wait_ge(ab_in, 64)
            nc.vector.tensor_scalar(a1[:, :], ab[:, 0, :], 1.0, None, ALU.add).then_inc(a1_ready, 1)
            for a in range(2):
                @turns(dve, NCK1 // 2)
                def _(j):
                    for s in range(2):
                        dve.wait_ge(added[s], a * NCK1 // 2 + j + 1)
                        for q in range(CH // 512):
                            nc.vector.bn_stats(st2[:, a, bass.ds((2 * j + s) * (CH // 512) + q, 1), :].rearrange("p m s -> p (m s)"),
                                               hr[:, a, bass.ds((2 * j + s) * CH + q * 512, 512)]).then_inc(counted[s], 1)
            for s in range(2):
                dve.wait_ge(counted[s], 2 * (NCK1 // 2) * (CH // 512))


def features(nc, hr, st2, gmat, gwb, fe_w, fe_b, feats, mean_out):
    NF = HW // 512
    with Stage(nc, "feats") as st:
        gm = st.sb("gm", [128, 128])
        gw = st.sb("gw", [128, 2])
        fw = st.sb("fw", [128, 128])
        fb = st.sb("fb", [128, 1])
        wa = st.sb("wa", [128, 2, 128])
        bb = st.sb("bb", [128, 2])
        mv = st.sb("mv", [128, 2, 2])
        g = st.sb("g", [128, 2, 2])
        grp = st.sb("grp", [128, 2, 2])
        var = st.sb("var", [128, 2])
        std = st.sb("std", [128, 2])
        ab = st.sb("ab", [128, 2, 2])
        fs = st.sb("fs", [128, 2, 2, 512])
        sums = st.sb("sums", [128, 2, NF])
        mean = st.sb("mean", [128, 2])
        p_g = st.ps("p_g", [128, 8])
        p_f = [st.ps(f"p_f{s}", [128, 2, 512]) for s in range(2)]
        loaded, step = st.sem("loaded"), st.sem("step")
        sums_ready, grouped, var_ready, rooted = st.sem("sums_ready"), st.sem("grouped"), st.sem("var_ready"), st.sem("rooted")
        ab_ready, shifted, w_ready = st.sem("ab_ready"), st.sem("shifted"), st.sem("w_ready")
        f_done, f_ready, stored = st.sem2("f_done"), st.sem2("f_ready"), st.sem2("stored")
        mean_ready, mean_out_done = st.sem("mean_ready"), st.sem("mean_out_done")
        fv = feats
        N = NF // 4
        block = st.block()

        @block.sync
        def _(sp):
            for dst, src in ((gm[:, :], gmat), (gw[:, :], gwb), (fw[:, :], fe_w), (fb[:, :], fe_b)):
                sp.dma_start(dst, src).then_inc(loaded, 16)
            for a in range(2):
                @turns(sp, N)
                def _(j):
                    for s in range(2):
                        sp.wait_ge(f_ready[s], 2 * a * N + 2 * j + 2)
                        sp.dma_start(fv[:, a, bass.ds((2 * j + s) * 1024, 1024)], fs[:, s].rearrange("p a n -> p (a n)"))\
                            .then_inc(stored[s], 16)
            sp.wait_ge(mean_ready, 1)
            sp.dma_start(mean_out, mean[:, :]).then_inc(mean_out_done, 16)
            sp.wait_ge(mean_out_done, 16)
            for s in range(2):
                sp.wait_ge(stored[s], 32 * N)

        @block.vector
        def _(dve):
            seen = [0]

            def link(ins):
                seen[0] += 1
                ins.then_inc(step, 1)
                dve.wait_ge(step, seen[0])

            for a in range(2):
                last = nc.vector.bn_aggr(mv[:, a, :], st2[:, a].rearrange("p m s -> p (m s)"))
            link(last)
            link(nc.vector.tensor_copy(g[:, 0, :], mv[:, :, 0]))
            link(nc.vector.tensor_tensor(g[:, 1, :], mv[:, :, 0], mv[:, :, 0], ALU.mult))
            nc.vector.tensor_tensor(g[:, 1, :], g[:, 1, :], mv[:, :, 1], ALU.add).then_inc(sums_ready, 1)
            dve.wait_ge(grouped, 1)
            link(nc.vector.tensor_copy(grp[:, :, :], p_g[:, 0:4].rearrange("p (a b) -> p a b", a=2)))
            link(nc.vector.tensor_tensor(var[:, :], grp[:, 0, :], grp[:, 0, :], ALU.mult))
            link(nc.vector.tensor_tensor(var[:, :], grp[:, 1, :], var[:, :], ALU.subtract))
            nc.vector.tensor_scalar(var[:, :], var[:, :], 0.0, EPS, ALU.max, ALU.add).then_inc(var_ready, 1)
            dve.wait_ge(rooted, 1)
            link(nc.vector.reciprocal(var[:, :], std[:, :]))
            link(nc.vector.tensor_scalar(ab[:, 0, :], var[:, :], gw[:, 0:1], None, ALU.mult))
            link(nc.vector.tensor_tensor(ab[:, 1, :], grp[:, 0, :], ab[:, 0, :], ALU.mult))
            nc.vector.tensor_scalar(ab[:, 1, :], ab[:, 1, :], -1.0, gw[:, 1:2], ALU.mult, ALU.add).then_inc(ab_ready, 1)
            for a in range(2):
                nc.vector.tensor_scalar(wa[:, a, :], fw[:, :], ab[:, 0, a:a + 1], None, ALU.mult).then_inc(w_ready, 1)
            dve.wait_ge(shifted, 1)
            nc.vector.tensor_scalar(bb[:, :], p_g[:, 4:6], fb[:, 0:1], None, ALU.add).then_inc(w_ready, 1)
            for s in range(2):
                dve.wait_ge(f_ready[s], 4 * N)
            link(nc.vector.tensor_reduce(mean[:, :], sums[:, :, :], AX.X, ALU.add))
            nc.vector.tensor_scalar(mean[:, :], mean[:, :], 1.0 / HW, None, ALU.mult).then_inc(mean_ready, 1)

        @block.tensor
        def _(pe):
            pe.wait_ge(loaded, 64)
            pe.wait_ge(sums_ready, 1)
            nc.tensor.matmul(p_g[:, 0:4], gm[:, :], g[:, :, :].rearrange("p a b -> p (a b)"), start=True, stop=True).then_inc(grouped, 1)
            pe.wait_ge(ab_ready, 1)
            nc.tensor.matmul(p_g[:, 4:6], fw[:, :], ab[:, 1, :], start=True, stop=True).then_inc(shifted, 1)
            pe.wait_ge(w_ready, 3)
            for a in range(2):
                @turns(pe, N)
                def _(j):
                    for s in range(2):
                        pe.wait_ge(f_ready[s], 2 * a * N + 2 * j)
                        for q in range(2):
                            mm = nc.tensor.matmul(p_f[s][:, q, :], wa[:, a, :], hr[:, a, bass.ds((2 * j + s) * 1024 + q * 512, 512)],
                                                  start=True, stop=True)
                        mm.then_inc(f_done[s], 1)

        @block.scalar
        def _(act):
            act.wait_ge(var_ready, 1)
            nc.scalar.activation(std[:, :], var[:, :], ACT.Sqrt).then_inc(rooted, 1)
            act.wait_ge(w_ready, 3)
            for a in range(2):
                @turns(act, N)
                def _(j):
                    for s in range(2):
                        act.wait_ge(f_done[s], a * N + j + 1)
                        act.wait_ge(stored[s], 16 * a * N + 16 * j)
                        for q in range(2):
                            nc.scalar.activation(fs[:, s, q, :], p_f[s][:, q, :], ACT.Gelu, bias=bb[:, a:a + 1],
                                                 accum_out=sums[:, a, bass.ds((2 * j + s) * 2 + q, 1)]).then_inc(f_ready[s], 1)


NE, TOP, NSH = 16, 4, 2
NX = NSH + TOP


def routing(nc, mean, g1w, bn1, ca1, ca1b, ca2, ca2b, g2w, bn2, g3w, g3b, before, sel_out, wts_out):
    with Stage(nc, "route") as st:
        mn = st.sb("mn", [128, 2])
        w1 = st.sb("w1", [128, 2, 128])
        b1 = st.sb("b1", [128, 5])
        w2 = st.sb("w2", [128, 64])
        b2 = st.sb("b2", [64, 5])
        c1 = st.sb("c1", [128, 8])
        c1b = st.sb("c1b", [8, 1])
        c2 = st.sb("c2", [8, 128])
        c2b = st.sb("c2b", [128, 1])
        w3 = st.sb("w3", [64, NE])
        b3 = st.sb("b3", [B, NE])
        bf = st.sb("bf", [B, NE, NE])
        s1 = st.sb("s1", [128, 2])
        s2 = st.sb("s2", [64, 2])
        h1 = st.sb("h1", [128, B])
        ca = st.sb("ca", [8, B])
        sg = st.sb("sg", [128, B])
        h2 = st.sb("h2", [64, B])
        sc = st.sb("sc", [B, NE])
        gt = st.sb("gt", [B, NE, NE])
        eq = st.sb("eq", [B, NE, NE])
        rank = st.sb("rank", [B, NE])
        hot = st.sb("hot", [B, TOP, NE])
        hv = st.sb("hv", [B, TOP, NE])
        val = st.sb("val", [B, TOP])
        nb = st.sb("nb", [B, 1])
        ex = st.sb("ex", [B, TOP])
        tot = st.sb("tot", [B, 1])
        wt = st.sb("wt", [B, TOP])
        p = [st.ps(f"p{i}", [128, 16]) for i in range(5)]
        loaded, step, stored = st.sem("loaded"), st.sem("step"), st.sem("stored")
        norm_ready, rooted = st.sem("norm_ready"), st.sem("rooted")
        product, active, ready = st.sem("product"), st.sem("active"), st.sem("ready")
        scaled, raised, hot_ready, wt_ready = st.sem("scaled"), st.sem("raised"), st.sem("hot_ready"), st.sem("wt_ready")
        block = st.block()

        @block.sync
        def _(sp):
            for dst, src in ((mn[:, :], mean), (w1[:, :, :], g1w), (b1[:, :], bn1), (w2[:, :], g2w), (b2[:, :], bn2),
                             (c1[:, :], ca1), (c1b[:, :], ca1b), (c2[:, :], ca2), (c2b[:, :], ca2b), (w3[:, :], g3w),
                             (b3[:, :], g3b), (bf[:, :, :], before)):
                sp.dma_start(dst, src).then_inc(loaded, 16)
            sp.wait_ge(hot_ready, TOP)
            sp.dma_start(sel_out, hot[:, :, :]).then_inc(stored, 16)
            sp.wait_ge(wt_ready, 1)
            sp.dma_start(wts_out, wt[:, :]).then_inc(stored, 16)
            sp.wait_ge(stored, 32)

        @block.vector
        def _(dve):
            seen = [0]

            def link(ins):
                seen[0] += 1
                ins.then_inc(step, 1)
                dve.wait_ge(step, seen[0])

            dve.wait_ge(loaded, 192)
            link(nc.vector.tensor_scalar(s1[:, 0:1], b1[:, 2:3], EPS, None, ALU.add))
            nc.vector.tensor_scalar(s2[:, 0:1], b2[:, 2:3], EPS, None, ALU.add).then_inc(norm_ready, 1)
            dve.wait_ge(rooted, 2)
            for s, b in ((s1, b1), (s2, b2)):
                link(nc.vector.reciprocal(s[:, 0:1], s[:, 1:2]))
                link(nc.vector.tensor_tensor(s[:, 0:1], s[:, 0:1], b[:, 3:4], ALU.mult))
                link(nc.vector.tensor_tensor(s[:, 1:2], b[:, 0:1], b[:, 1:2], ALU.subtract))
                link(nc.vector.tensor_tensor(s[:, 1:2], s[:, 1:2], s[:, 0:1], ALU.mult))
                link(nc.vector.tensor_tensor(s[:, 1:2], s[:, 1:2], b[:, 4:5], ALU.add))
            nc.vector.tensor_scalar(c2b[:, :], c2b[:, :], 2.0, None, ALU.mult).then_inc(ready, 1)
            dve.wait_ge(active, 3)
            nc.vector.tensor_tensor(h1[:, :], h1[:, :], sg[:, :], ALU.mult).then_inc(scaled, 1)
            dve.wait_ge(product, 5)
            link(nc.vector.tensor_tensor(sc[:, :], p[4][0:B, 0:NE], b3[:, :], ALU.add))
            row = sc[:, :].unsqueeze(1).broadcast_to([B, NE, NE])
            col = sc[:, :].unsqueeze(2).broadcast_to([B, NE, NE])
            link(nc.vector.tensor_tensor(gt[:, :, :], row, col, ALU.is_gt))
            link(nc.vector.tensor_tensor(eq[:, :, :], row, col, ALU.is_equal))
            link(nc.vector.tensor_tensor(eq[:, :, :], eq[:, :, :], bf[:, :, :], ALU.mult))
            link(nc.vector.tensor_tensor(gt[:, :, :], gt[:, :, :], eq[:, :, :], ALU.add))
            link(nc.vector.tensor_reduce(rank[:, :], gt[:, :, :], AX.X, ALU.add))
            for k in range(TOP):
                nc.vector.tensor_scalar(hot[:, k, :], rank[:, :], float(k), None, ALU.is_equal).then_inc(hot_ready, 1)
            dve.wait_ge(hot_ready, TOP)
            link(nc.vector.tensor_tensor(hv[:, :, :], hot[:, :, :], sc[:, :].unsqueeze(1).broadcast_to([B, TOP, NE]), ALU.mult))
            link(nc.vector.tensor_reduce(val[:, :], hv[:, :, :], AX.X, ALU.add))
            nc.vector.tensor_scalar(nb[:, :], val[:, 0:1], -0.5, None, ALU.mult).then_inc(ready, 1)
            dve.wait_ge(raised, 1)
            link(nc.vector.tensor_reduce(tot[:, :], ex[:, :], AX.X, ALU.add))
            link(nc.vector.reciprocal(tot[:, :], tot[:, :]))
            nc.vector.tensor_scalar(wt[:, :], ex[:, :], tot[:, 0:1], None, ALU.mult).then_inc(wt_ready, 1)

        @block.tensor
        def _(pe):
            pe.wait_ge(loaded, 192)
            for q in range(2):
                mm = nc.tensor.matmul(p[0][:, 2 * q:2 * q + 2], w1[:, q, :], mn[:, :], start=True, stop=True)
            mm.then_inc(product, 1)
            pe.wait_ge(active, 1)
            nc.tensor.matmul(p[1][0:8, 0:B], c1[:, :], h1[:, :], start=True, stop=True).then_inc(product, 1)
            pe.wait_ge(active, 2)
            nc.tensor.matmul(p[2][:, 0:B], c2[:, :], ca[:, :], start=True, stop=True).then_inc(product, 1)
            pe.wait_ge(scaled, 1)
            nc.tensor.matmul(p[3][0:64, 0:B], w2[:, :], h1[:, :], start=True, stop=True).then_inc(product, 1)
            pe.wait_ge(active, 4)
            nc.tensor.matmul(p[4][0:B, 0:NE], h2[:, :], w3[:, :], start=True, stop=True).then_inc(product, 1)

        @block.scalar
        def _(act):
            act.wait_ge(norm_ready, 1)
            for s in (s1, s2):
                nc.scalar.activation(s[:, 1:2], s[:, 0:1], ACT.Sqrt).then_inc(rooted, 1)
            act.wait_ge(ready, 1)
            act.wait_ge(product, 1)
            nc.scalar.activation(h1[:, :], p[0][:, 0:B], ACT.Gelu, scale=s1[:, 0:1], bias=s1[:, 1:2]).then_inc(active, 1)
            act.wait_ge(product, 2)
            nc.scalar.activation(ca[:, :], p[1][0:8, 0:B], ACT.Gelu, bias=c1b[:, 0:1]).then_inc(active, 1)
            act.wait_ge(product, 3)
            nc.scalar.activation(sg[:, :], p[2][:, 0:B], ACT.Sigmoid, scale=2.0, bias=c2b[:, 0:1]).then_inc(active, 1)
            act.wait_ge(product, 4)
            nc.scalar.activation(h2[:, :], p[3][0:64, 0:B], ACT.Gelu, scale=s2[:, 0:1], bias=s2[:, 1:2]).then_inc(active, 1)
            act.wait_ge(ready, 2)
            nc.scalar.activation(ex[:, :], val[:, :], ACT.Exp, scale=0.5, bias=nb[:, 0:1]).then_inc(raised, 1)


def experts(nc, hr, feats, sel, wts, we, be, ws, bs, out1):
    NF = HW // 512
    ov = out1.rearrange("(a p) c h w -> (p c) a (h w)", a=2)
    fv = feats.rearrange("p a n -> p (a n)")
    with Stage(nc, "experts") as st:
        wes = st.sb("wes", [128, C, NE])
        bes = st.sb("bes", [128, NE])
        hot = st.sb("hot", [128, 2, TOP, NE])
        pk = st.sb("pk", [128, C, NE])
        pb = st.sb("pb", [128, 2, TOP, NE])
        wx = st.sb("wx", [128, 2, NX, 128])
        bx = st.sb("bx", [128, 2, NX])
        gx = st.sb("gx", [128, 2, NX])
        fs = st.sb("fs", [128, 2, 512])
        os = st.sb("os", [128, 2, 512])
        p_x = [st.ps(f"p_x{k}", [128, 512]) for k in range(NX)]
        loaded, zeroed, step, w_ready = st.sem("loaded"), st.sem("zeroed"), st.sem("step"), st.sem("w_ready")
        f_in, x_done, x_ready = st.sem2("f_in"), st.sem("x_done"), st.sem("x_ready")
        summed = [st.sem(f"summed{k}") for k in range(NX)]
        stored = st.sem2("stored")
        N = NF // 2
        block = st.block()

        @block.gpsimd
        def _(pool):
            nc.gpsimd.memset(wx[:, :, NSH:NX, :], 0.0).then_inc(zeroed, 1)
            nc.gpsimd.memset(gx[:, :, 0:NSH], 1.0 / NSH).then_inc(zeroed, 1)

        @block.sync
        def _(sp):
            for dst, src in ((wes[:, :, :], we), (bes[:, :], be)):
                sp.dma_start(dst, src).then_inc(loaded, 16)
            for a in range(2):
                sp.dma_start(wx[:, a, 0:NSH, :], ws).then_inc(loaded, 16)
                sp.dma_start(bx[:, a, 0:NSH], bs).then_inc(loaded, 16)
            for q in range(2):
                for a in range(2):
                    b = 2 * q + a
                    r = slice(64 * q, 64 * q + 64)
                    sp.dma_start(hot[r, a].rearrange("p k e -> p (k e)"),
                                 sel.rearrange("b k e -> b (k e)")[b:b + 1, :].broadcast_to([64, TOP * NE])).then_inc(loaded, 16)
                    sp.dma_start(gx[r, a, NSH:NX], wts[b:b + 1, :].broadcast_to([64, TOP])).then_inc(loaded, 16)
            def load(n, s):
                sp.dma_start(fs[:, s, :], fv[:, bass.ds(n * 512, 512)]).then_inc(f_in[s], 16)

            def store(a, j, s):
                sp.wait_ge(summed[NX - 1], a * N * 2 + 2 * j + s + 1)
                sp.dma_start(ov[:, a, bass.ds((2 * j + s) * 512, 512)], os[:, s, :]).then_inc(stored[s], 16)

            for s in range(2):
                load(s, s)
            for a in range(2):
                @turns(sp, N - a)
                def _(j):
                    for s in range(2):
                        n = a * N * 2 + 2 * j + s
                        sp.wait_ge(x_done, n * NX + NX)
                        load(n + 2, s)
                    for s in range(2):
                        store(a, j, s)
            for s in range(2):
                store(1, N - 1, s)
            for s in range(2):
                sp.wait_ge(stored[s], 32 * N)

        @block.scalar
        def _(act):
            act.wait_ge(w_ready, 1)
            for a in range(2):
                @turns(act, N)
                def _(j):
                    for s in range(2):
                        n = a * N * 2 + 2 * j + s
                        for k in range(NX):
                            act.wait_ge(x_done, n * NX + k + 1)
                            nc.scalar.activation(p_x[k][:, :], p_x[k][:, :], ACT.Gelu, bias=bx[:, a, k:k + 1]).then_inc(x_ready, 1)

        @block.tensor
        def _(pe):
            pe.wait_ge(w_ready, 1)
            for a in range(2):
                @turns(pe, N)
                def _(j):
                    for s in range(2):
                        n = a * N * 2 + 2 * j + s
                        pe.wait_ge(f_in[s], 16 * (a * N + j) + 16)
                        for k in range(NX):
                            pe.wait_ge(summed[k], n)
                            mm = nc.tensor.matmul(p_x[k][:, :], wx[:, a, k, :], fs[:, s, :], start=True, stop=True)
                            mm.then_inc(x_done, 1)

        @block.vector
        def _(dve):
            seen = [0]

            def link(ins):
                seen[0] += 1
                ins.then_inc(step, 1)
                dve.wait_ge(step, seen[0])

            dve.wait_ge(loaded, 16 * 14)
            dve.wait_ge(zeroed, 2)
            for a in range(2):
                for k in range(TOP):
                    link(nc.vector.tensor_tensor(pk[:, :, :], wes[:, :, :], hot[:, a, k, :].unsqueeze(1).broadcast_to([128, C, NE]), ALU.mult))
                    for q in range(2):
                        r = slice(64 * q, 64 * q + 64)
                        last = nc.vector.tensor_reduce(wx[r, a, NSH + k, 64 * q:64 * q + 64], pk[r], AX.X, ALU.add)
                        link(last)
            link(nc.vector.tensor_tensor(pb[:, :, :, :].rearrange("p a k e -> p (a k) e"),
                                         hot[:, :, :, :].rearrange("p a k e -> p (a k) e"),
                                         bes[:, :].unsqueeze(1).broadcast_to([128, 2 * TOP, NE]), ALU.mult))
            for a in range(2):
                last = nc.vector.tensor_reduce(bx[:, a, NSH:NX], pb[:, a], AX.X, ALU.add)
                if a == 0:
                    link(last)
            last.then_inc(w_ready, 1)
            for a in range(2):
                @turns(dve, N)
                def _(j):
                    for s in range(2):
                        n = a * N * 2 + 2 * j + s
                        dve.wait_ge(stored[s], 16 * (a * N + j))
                        for k in range(NX):
                            dve.wait_ge(x_ready, n * NX + k + 1)
                            if k:
                                dve.wait_ge(summed[k - 1], n + 1)
                            part = os[:, s, :] if k else hr[:, a, bass.ds((2 * j + s) * 512, 512)]
                            nc.vector.scalar_tensor_tensor(os[:, s, :], p_x[k][:, :], gx[:, a, k:k + 1], part,
                                                           ALU.mult, ALU.add).then_inc(summed[k], 1)


M2 = 20
KEPT = 69
PADX = 4


def hartley_modes(nc, low, t_re, t_im, half, wm, mixc, modes, x2):
    M3 = M2 + 1
    with Stage(nc, "modes2") as st:
        re = st.sb("re", [128, B, M2, M2])
        im = st.sb("im", [128, B, M2, M2])
        tr = st.sb("tr", [128, M2, M2])
        ti = st.sb("ti", [128, M2, M2])
        hf = st.sb("hf", [128, 2])
        neg = st.sb("neg", [128, B, M2, M2])
        uv = st.sb("uv", [128, M2 * M2, B])
        wt = st.sb("wt", [128, 2, M2, C])
        o = st.sb("o", [C, B, M2, M2])
        mx = st.sb("mx", [C, B * B, 128])
        res = st.sb("res", [128, B, M3, M3])
        zero = st.sb("zero", [C, PADX])
        p_o = [st.ps(f"p_o{s}", [C, 512]) for s in range(2)]
        p_m = [st.ps(f"p_m{s}", [128, 512]) for s in range(B)]
        loaded, step, zeroed = st.sem("loaded"), st.sem("step"), st.sem("zeroed")
        uv_ready, mixed, res_ready, stored = st.sem("uv_ready"), st.sem("mixed"), st.sem("res_ready"), st.sem("stored")
        w_in, o_done, o_copied = st.sem2("w_in"), st.sem2("o_done"), st.sem2("o_copied")
        block = st.block()

        @block.gpsimd
        def _(pool):
            nc.gpsimd.memset(zero[:, :], 0.0).then_inc(zeroed, 1)
            nc.gpsimd.memset(res[:, :, :, :], 0.0).then_inc(zeroed, 1)

        @block.sync
        def _(sp):
            def load(j, s):
                sp.dma_start(wt[:, s], wm[:, bass.ds(2 * j + s, 1)].rearrange("p o k c -> p (o k) c")).then_inc(w_in[s], 16)

            for r, dst in ((0, re), (1, im)):
                for b in range(B):
                    src = low[r * MD:r * MD + M2, b * C:(b + 1) * C, 0:M2].rearrange("k c m -> c k m")
                    for q in range(2):
                        sp.dma_start(dst[q * C:(q + 1) * C, b], src).then_inc(loaded, 16)
            for dst, src in ((tr[:, :, :], t_re), (ti[:, :, :], t_im), (hf[:, :], half), (mx[:, :, :], mixc)):
                sp.dma_start(dst, src).then_inc(loaded, 16)
            for s in range(2):
                load(0, s)
            @turns(sp, M2 // 2 - 1)
            def _(j):
                for s in range(2):
                    sp.wait_ge(o_done[s], j + 1)
                    load(j + 1, s)
            sp.wait_ge(zeroed, 1)
            sp.dma_start(x2[:, 0:PADX], zero[:, :]).then_inc(stored, 16)
            sp.wait_ge(res_ready, 2 * B)
            for r in range(2):
                sp.dma_start(modes[r].rearrange("b c k m -> c b (k m)"), res[r * C:(r + 1) * C].rearrange("p b k m -> p b (k m)")).then_inc(stored, 16)
            sp.wait_ge(stored, 48)

        @block.vector
        def _(dve):
            seen = [0]

            def link(ins):
                seen[0] += 1
                ins.then_inc(step, 1)
                dve.wait_ge(step, seen[0])

            dve.wait_ge(loaded, 16 * (4 * B + 4))
            for v, t in ((re, tr), (im, ti)):
                for b in range(B):
                    link(nc.vector.tensor_tensor(v[:, b], v[:, b], t[:, :, :], ALU.mult))
            link(nc.vector.tensor_tensor(re[:, :, :, :], re[:, :, :, :], im[:, :, :, :], ALU.add))
            F = M2 - 1
            for b in range(B):
                link(nc.vector.tensor_copy(neg[:, b, 0, 0:1], re[:, b, 0, 0:1]))
                link(nc.vector.tensor_copy(neg[:, b, 0, 1:], re[:, b, 0, F:0:-1]))
                link(nc.vector.tensor_copy(neg[:, b, 1:, 0], re[:, b, F:0:-1, 0]))
                link(nc.vector.tensor_copy(neg[:, b, 1:, 1:], re[:, b, F:0:-1, F:0:-1]))
            nc.vector.scalar_tensor_tensor(uv[:, :, :].rearrange("p k b -> p b k"), neg[:, :, :, :].rearrange("p b k m -> p b (k m)"),
                                           hf[:, 0:1], re[:, :, :, :].rearrange("p b k m -> p b (k m)"), ALU.mult, ALU.add)\
                .then_inc(uv_ready, 1)
            dve.wait_ge(mixed, 1)
            dve.wait_ge(zeroed, 2)
            for b in range(B):
                for q in range(2):
                    r = slice(q * C, q * C + C)
                    nc.vector.tensor_scalar(res[r, b, q:q + M2, q:q + M2], p_m[b][r, 0:M2 * M2].rearrange("p (k m) -> p k m", k=M2),
                                            hf[r, 1:2], None, ALU.mult).then_inc(res_ready, 1)

        @block.tensor
        def _(pe):
            pe.wait_ge(loaded, 16 * (4 * B + 4))
            pe.wait_ge(uv_ready, 1)
            @turns(pe, M2 // 2)
            def _(j):
                for s in range(2):
                    pe.wait_ge(w_in[s], 16 * j + 16)
                    pe.wait_ge(o_copied[s], j)
                    nc.tensor.matmul(p_m[0][:, 0:4], mx[:, 0, :], mx[:, 0, 0:4], start=True, stop=True)
                    for k in range(M2):
                        mm = nc.tensor.matmul(p_o[s][:, k * B:k * B + B], wt[:, s, k, :], uv[:, bass.ds((2 * j + s) * M2 + k, 1), :],
                                              start=True, stop=True)
                    mm.then_inc(o_done[s], 1)
            for s in range(2):
                pe.wait_ge(o_copied[s], M2 // 2)
            for b in range(B):
                for a in range(B):
                    mm = nc.tensor.matmul(p_m[b][:, 0:M2 * M2], mx[:, b * B + a, :], o[:, a].rearrange("p k m -> p (k m)"),
                                          start=(a == 0), stop=(a == B - 1))
            mm.then_inc(mixed, 1)

        @block.scalar
        def _(act):
            @turns(act, M2 // 2)
            def _(j):
                for s in range(2):
                    act.wait_ge(o_done[s], j + 1)
                    nc.scalar.activation(o[:, :, :, bass.ds(2 * j + s, 1)].rearrange("p b k m -> p b (k m)"),
                                         p_o[s][:, 0:M2 * B].rearrange("p (k b) -> p b k", b=B), ACT.Copy).then_inc(o_copied[s], 1)


LX = B * H * KEPT
ST = 16
TK, CG, DE = 8, 8, 16
TD = TK * DE
PE_CH = 128
UE = 6


def after(eng, sem, n):
    if not (isinstance(n, int) and n <= 0):
        eng.wait_ge(sem, n)


def pipeline(eng, n, unroll, tail, *parts):
    def fixed(i):
        for lag, part in parts:
            c = i - lag
            if 0 <= c < n:
                part(c, c % unroll, c // unroll)

    for i in range(unroll):
        fixed(i)
    with eng.Fori(1, n // unroll) as j:
        for s in range(unroll):
            for lag, part in parts:
                back = 1 if lag > s else 0
                part(j * unroll + (s - lag), (s - lag) % unroll, j - back if back else j)
    for i in range(n, n + tail):
        fixed(i)


def spectral_mamba(nc, x2, w_in, w_conv, w_xd, w_dt, w_bc, row, skip_d, a_log, w_out, ident, ye):
    NC = LX // PE_CH
    with Stage(nc, "spe") as st:
        wi = st.sb("wi", [65, 2 * TD])
        wc = st.sb("wc", [65, 2 * TD])
        wxd = st.sb("wxd", [TK, TD])
        wdt = st.sb("wdt", [TK, TD])
        xw = st.sb("xw", [TD, 3 * TD])
        rw = st.sb("rw", [1, TD])
        one = st.sb("one", [1, PE_CH])
        dd = st.sb("dd", [TD, 1])
        dg = st.sb("dg", [TD, TD])
        av = st.sb("av", [128, DE, ST])
        wo = st.sb("wo", [TD, C])
        idt = st.sb("idt", [128, 128])
        xt = st.sb("xt", [65, UE, PE_CH])
        sg = st.sb("sg", [128, 2, 2 * TD])
        xz = st.sb("xz", [128, UE, 2, TD])
        xct = st.sb("xct", [TD, UE, 2, PE_CH])
        soft = st.sb("soft", [128, 2, TD])
        relu = st.sb("relu", [128, 2, TD])
        dt = st.sb("dt", [128, 2, DE, TK])
        u = st.sb("u", [128, 3, DE, TK])
        da = st.sb("da", [128, 3, DE * ST, TK])
        bx = st.sb("bx", [128, 3, DE, ST, TK])
        hs = st.sb("hs", [128, DE, ST, TK])
        hh = st.sb("hh", [128, 2, ST // 2, DE, TK])
        y2 = st.sb("y2", [TD, 2, PE_CH])
        res = st.sb("res", [C, UE, PE_CH])
        p_xz = [st.ps(f"p_xz{s}", [128, 512]) for s in range(2)]
        p_t = st.ps("p_t", [128, 512])
        p_y = st.ps("p_y", [128, 512])
        p_o = st.ps("p_o", [C, 512])
        p_bc = [st.ps(f"p_bc{s}", [128, 512]) for s in range(3)]
        loaded, step, product, w_ready, zeroed = (st.sem(n) for n in ("loaded", "step", "product", "w_ready", "zeroed"))
        x_in, stored = [st.sem(f"x_in{s}") for s in range(UE)], [st.sem(f"stored{s}") for s in range(UE)]
        (projected, sig_step, sig_ready, activated, turned, turned_copied, bc_done, soft_step, soft_ready, dt_step, u_ready, dta_ready, decay_ready,
         bx_ready, scanned, weighted, halved, summed, y_ready, out_done, out_copied) = (
            st.sem(n) for n in ("projected", "sig_step", "sig_ready", "activated", "turned", "turned_copied", "bc_done", "soft_step", "soft_ready",
                                "dt_step", "u_ready", "dta_ready", "decay_ready", "bx_ready", "scanned", "weighted", "halved", "summed",
                                "y_ready", "out_done", "out_copied"))
        block = st.block()

        @block.sync
        def _(sp):
            def load(c, s):
                sp.dma_start(xt[0:64, s, :], x2[:, bass.ds(c * PE_CH + PADX, PE_CH)]).then_inc(x_in[s], 16)

            def next_load(c, s, r):
                sp.wait_ge(projected, c + 1)
                load(c + UE, s)

            def store(c, s, r):
                sp.wait_ge(out_copied, c + 1)
                sp.dma_start(ye[:, bass.ds(c * PE_CH, PE_CH)], res[:, s, :]).then_inc(stored[s], 16)

            for dst, src in ((wi[:, :], w_in), (wc[:, :], w_conv), (wxd[:, :], w_xd), (wdt[:, :], w_dt),
                             (xw[:, TD:3 * TD], w_bc), (rw[:, :], row), (dd[:, :], skip_d),
                             (av[:, :, :], a_log), (wo[:, :], w_out), (idt[:, :], ident)):
                sp.dma_start(dst, src).then_inc(loaded, 16)
            for s in range(UE):
                load(s, s)
            @turns(sp, NC // UE - 1)
            def _(j):
                for s in range(UE):
                    next_load(j * UE + s, s, j)
                    store(j * UE + s, s, j)
            for s in range(UE):
                store(NC - UE + s, s, NC // UE - 1)
            for s in range(UE):
                sp.wait_ge(stored[s], 16 * (NC // UE))

        @block.gpsimd
        def _(pool):
            nc.gpsimd.memset(xt[64:65, :, :], 1.0).then_inc(zeroed, 1)
            pool.wait_ge(zeroed, 1)
            nc.gpsimd.memset(one[:, :], 1.0).then_inc(zeroed, 1)
            pool.wait_ge(zeroed, 2)
            nc.gpsimd.memset(da[:, :, :, 0:1], 0.0).then_inc(zeroed, 1)
            pool.wait_ge(w_ready, 5)

            def silu(c, s, r):
                pool.wait_ge(sig_ready, c + 1)
                v = xz[:, s].rearrange("p q n -> p (q n)")
                nc.gpsimd.tensor_tensor(v, v, sg[:, s % 2, :], ALU.mult).then_inc(activated, 1)

            def step_sizes(c, s, r):
                pool.wait_ge(soft_ready, c + 1)
                d = dt[:, s % 2].rearrange("p d t -> p (d t)")
                nc.gpsimd.tensor_tensor(d, soft[:, s % 2, :], relu[:, s % 2, :], ALU.add).then_inc(dt_step, 1)
                pool.wait_ge(activated, c + 1)
                after(pool, bx_ready, c - 2)
                pool.wait_ge(dt_step, c + 1)
                nc.gpsimd.tensor_tensor(u[:, s % 3].rearrange("p d t -> p (d t)"), d, xz[:, s, 0, :], ALU.mult).then_inc(u_ready, 1)
                after(pool, scanned, c - 2)
                nc.gpsimd.tensor_tensor(da[:, s % 3, :, 1:].rearrange("p (d s) t -> p d s t", s=ST),
                                        dt[:, s % 2, :, 1:].unsqueeze(2).broadcast_to([128, DE, ST, TK - 1]),
                                        av[:, :, :].unsqueeze(3).broadcast_to([128, DE, ST, TK - 1]), ALU.mult).then_inc(dta_ready, 1)

            def halve(c, s, r):
                pool.wait_ge(weighted, c + 1)
                after(pool, summed, c - 1)
                v = bx[:, s % 3]
                nc.gpsimd.tensor_tensor(hh[:, s % 2].rearrange("p s d t -> p d s t"), v[:, :, 0:ST // 2], v[:, :, ST // 2:], ALU.add)\
                    .then_inc(halved, 1)

            pipeline(pool, NC, UE, 4, (0, silu), (4, halve), (1, step_sizes))

        @block.tensor
        def _(pe):
            pe.wait_ge(loaded, 160)
            nc.tensor.matmul(p_t[:, 0:TD], wxd[:, :], wdt[:, :], start=True, stop=True).then_inc(product, 1)
            pe.wait_ge(w_ready, 5)
            pe.wait_ge(zeroed, 3)

            def project(c, s, r):
                pe.wait_ge(x_in[s], 16 * r + 16)
                after(pe, activated, c - 1)
                nc.tensor.matmul(p_xz[s % 2][:, 0:2 * TD], xt[:, s, :], wi[:, :], start=True, stop=True).then_inc(projected, 1)

            def turn(c, s, r):
                pe.wait_ge(activated, c + 1)
                after(pe, turned_copied, c)
                for q in range(2):
                    mm = nc.tensor.matmul(p_t[:, q * PE_CH:(q + 1) * PE_CH], xz[:, s, q, :], idt[:, :], start=True, stop=True)
                mm.then_inc(turned, 1)

            def dt_b_c(c, s, r):
                pe.wait_ge(turned_copied, c + 1)
                after(pe, weighted, c - 2)
                nc.tensor.matmul(p_bc[s % 3][:, 0:3 * TD], xct[:, s, 0, :], xw[:, :], start=True, stop=False)
                nc.tensor.matmul(p_bc[s % 3][:, 0:TD], one[:, :], rw[:, :], start=False, stop=True).then_inc(bc_done, 1)

            def sum_y(c, s, r):
                pe.wait_ge(halved, c + 1)
                after(pe, y_ready, c)
                nc.tensor.matmul(p_y[:, 0:PE_CH], dg[:, :], xct[:, s, 0, :], start=True, stop=False)
                for k in range(ST // 2):
                    mm = nc.tensor.matmul(p_y[:, 0:PE_CH], hh[:, s % 2, k].rearrange("p d t -> p (d t)"), idt[:, :], start=False, stop=(k == ST // 2 - 1))
                mm.then_inc(summed, 1)

            def project_out(c, s, r):
                pe.wait_ge(y_ready, c + 1)
                after(pe, out_copied, c)
                nc.tensor.matmul(p_o[:, 0:PE_CH], wo[:, :], y2[:, s % 2, :], start=True, stop=True).then_inc(out_done, 1)

            pipeline(pe, NC, UE, 6, (1, turn), (1, dt_b_c), (0, project), (5, sum_y), (6, project_out))

        @block.scalar
        def _(act):
            act.wait_ge(loaded, 160)
            act.preload_act_table_set("natural_log_exp_and_others")
            nc.scalar.activation(av[:, :, :], av[:, :, :], ACT.Exp).then_inc(w_ready, 1)
            act.wait_ge(w_ready, 5)

            def sigmoid(c, s, r):
                act.wait_ge(projected, c + 1)
                after(act, activated, c - 1)
                t = sg[:, s % 2, :]
                after(act, turned, c - UE + 1)
                after(act, u_ready, c - UE + 1)
                nc.scalar.activation(xz[:, s].rearrange("p q n -> p (q n)"), p_xz[s % 2][:, 0:2 * TD], ACT.Copy)
                nc.scalar.activation(t, p_xz[s % 2][:, 0:2 * TD], ACT.Exp, scale=-1.0).then_inc(sig_step, 1)
                act.wait_ge(sig_step, 2 * c + 1)
                nc.scalar.activation(t, t, ACT.Ln, bias=1.0).then_inc(sig_step, 1)
                act.wait_ge(sig_step, 2 * c + 2)
                nc.scalar.activation(t, t, ACT.Exp, scale=-1.0).then_inc(sig_ready, 1)

            def copy_turned(c, s, r):
                act.wait_ge(turned, c + 1)
                after(act, y_ready, c - UE + 1)
                nc.scalar.activation(xct[:, s].rearrange("p q n -> p (q n)"), p_t[:, 0:2 * PE_CH], ACT.Copy).then_inc(turned_copied, 1)

            def softplus(c, s, r):
                act.wait_ge(bc_done, c + 1)
                after(act, dt_step, c - 1)
                t = soft[:, s % 2, :]
                nc.scalar.activation(t, p_bc[s % 3][:, 0:TD], ACT.Abs).then_inc(soft_step, 1)
                nc.scalar.activation(relu[:, s % 2, :], p_bc[s % 3][:, 0:TD], ACT.Relu)
                act.wait_ge(soft_step, 2 * c + 1)
                nc.scalar.activation(t, t, ACT.Exp, scale=-1.0).then_inc(soft_step, 1)
                act.wait_ge(soft_step, 2 * c + 2)
                nc.scalar.activation(t, t, ACT.Ln, bias=1.0).then_inc(soft_ready, 1)

            def decay(c, s, r):
                act.wait_ge(dta_ready, c + 1)
                nc.scalar.activation(da[:, s % 3, :, 1:], da[:, s % 3, :, 1:], ACT.Exp).then_inc(decay_ready, 1)

            def copy_out(c, s, r):
                act.wait_ge(out_done, c + 1)
                after(act, stored[s], 16 * r)
                nc.scalar.activation(res[:, s, :], p_o[:, 0:PE_CH], ACT.Copy).then_inc(out_copied, 1)

            pipeline(act, NC, UE, 6, (1, copy_turned), (1, softplus), (0, sigmoid), (6, copy_out), (2, decay))

        @block.vector
        def _(dve):
            dve.wait_ge(loaded, 160)
            nc.vector.tensor_tensor(wi[:, :], wi[:, :], wc[:, :], ALU.mult).then_inc(w_ready, 1)
            nc.vector.tensor_scalar(dg[:, :], idt[:, :], dd[:, 0:1], None, ALU.mult).then_inc(w_ready, 1)
            dve.wait_ge(product, 1)
            nc.vector.tensor_copy(xw[:, 0:TD], p_t[:, 0:TD]).then_inc(w_ready, 1)
            dve.wait_ge(w_ready, 4)
            nc.vector.tensor_scalar(av[:, :, :], av[:, :, :], -1.0, None, ALU.mult).then_inc(w_ready, 1)
            dve.wait_ge(zeroed, 3)

            def flat(t):
                return t.rearrange("p d s t -> p (d s t)")

            def over_d(s, q):
                return p_bc[s % 3][:, q * TD:(q + 1) * TD].rearrange("p (s t) -> p s t", t=TK).unsqueeze(1)\
                    .broadcast_to([128, DE, ST, TK])

            def feed(c, s, r):
                dve.wait_ge(u_ready, c + 1)
                after(dve, halved, c - 2)
                nc.vector.tensor_tensor(bx[:, s % 3], u[:, s % 3].unsqueeze(2).broadcast_to([128, DE, ST, TK]), over_d(s, 1),
                                        ALU.mult).then_inc(bx_ready, 1)

            def scan(c, s, r):
                dve.wait_ge(decay_ready, c + 1)
                dve.wait_ge(bx_ready, c + 1)
                nc.vector.tensor_tensor_scan(flat(hs[:, :, :, :]), da[:, s % 3].rearrange("p n t -> p (n t)"), flat(bx[:, s % 3]), 0.0,
                                             ALU.mult, ALU.add).then_inc(scanned, 1)

            def weight(c, s, r):
                dve.wait_ge(scanned, c + 1)
                nc.vector.tensor_tensor(bx[:, s % 3], hs[:, :, :, :], over_d(s, 2), ALU.mult).then_inc(weighted, 1)

            def gate(c, s, r):
                dve.wait_ge(summed, c + 1)
                after(dve, out_done, c - 1)
                nc.vector.tensor_tensor(y2[:, s % 2, :], p_y[:, 0:PE_CH], xct[:, s, 1, :], ALU.mult).then_inc(y_ready, 1)

            pipeline(dve, NC, UE, 5, (3, feed), (3, scan), (3, weight), (5, gate))


RA = 4
NA = RA * KEPT
UA = 8
JUMP = 36
STEADY = W // 2 - 4
SG = 4
SPREAD = [(0, 0), (0, 1), (1, 0), (0, 2), (1, 1), (0, 3), (1, 2), (1, 3)]


def spatial_mamba(nc, x2, w_in, w_conv, w_z, conv_b, conv_row, w_xd, w_dt, dt_b, w_bc3, w_b, a_log, skip_d, w_out, split_rows, pick, ident, ys):
    NC = LX // NA
    with Stage(nc, "spa") as st:
        wi = st.sb("wi", [128, 2, 128])
        wc = st.sb("wc", [128, 2, 128])
        wz = st.sb("wz", [C, 128])
        cb = st.sb("cb", [128, 2])
        cr = st.sb("cr", [1, 128])
        one = st.sb("one", [1, NA])
        wxd = st.sb("wxd", [4, 128])
        wdt = st.sb("wdt", [4, 128])
        wd = st.sb("wd", [128, 128])
        db = st.sb("db", [128, 2])
        w96 = st.sb("w96", [128, 96])
        wb = st.sb("wb", [128, ST])
        av = st.sb("av", [128, ST])
        dd = st.sb("dd", [128, 1])
        dg = st.sb("dg", [128, 128])
        wo = st.sb("wo", [128, C])
        sr = st.sb("sr", [96, 2])
        pk = st.sb("pk", [96, 2 * ST])
        sel = st.sb("sel", [96, 2 * ST, 128], BF16)
        idt = st.sb("idt", [128, 128])
        c0 = st.sb("c0", [128, 8])
        xrep = st.sb("xrep", [128, 128])
        a0 = st.sb("a0", [128, ST])
        b0 = st.sb("b0", [128, ST])
        a60 = st.sb("a60", [128, ST, STEADY])
        b60 = st.sb("b60", [128, ST, STEADY])
        jump = st.sb("jump", [128, ST])
        xt = st.sb("xt", [128, UA, NA + 4])
        fold60 = st.sb("fold60", [128, RA])
        sg = st.sb("sg", [128, 2, 2, NA])
        xz = st.sb("xz", [128, UA, 2, NA])
        soft = st.sb("soft", [128, 2, NA])
        relu = st.sb("relu", [128, 2, NA])
        dt = st.sb("dt", [128, 2, NA])
        u = st.sb("u", [128, 4, NA])
        hi = st.sb("hi", [96, 2, NA], BF16)
        rest = st.sb("rest", [96, 2, NA])
        parts = st.sb("parts", [96, 4, NA], BF16)
        da = st.sb("da", [128, 2, ST, NA])
        bx = st.sb("bx", [128, 2 * SG, NA])
        hs = st.sb("hs", [128, 2, ST, NA])
        hc = st.sb("hc", [128, 2, ST, NA])
        hh = st.sb("hh", [128, ST // 2, NA])
        hq = st.sb("hq", [128, 2, ST // 4, NA])
        y2 = st.sb("y2", [128, 2, NA])
        res = st.sb("res", [C, 4, NA])
        p_x = st.ps("p_x", [128, 2, 512])
        p_y = st.ps("p_y", [128, 512])
        p_o = st.ps("p_o", [C, 512])
        p_s = [st.ps(f"p_s{i}", [128, 2, 512]) for i in range(2)]
        x_in, stored = [st.sem(f"x_in{s}") for s in range(UA)], [st.sem(f"stored{s}") for s in range(4)]
        (loaded, step, setup_act, setup_pe, w_ready, zeroed, projected, sig_step, sig_ready, activated, derived, soft_step, soft_ready,
         hi_ready, rest_ready, mid_ready, parts_ready, dt_step, u_ready, decay_ready, spread, taken, fixed, scanned, halved,
         quartered, y_done, y_ready, out_done, out_copied) = (
            st.sem(n) for n in ("loaded", "step", "setup_act", "setup_pe", "w_ready", "zeroed", "projected", "sig_step", "sig_ready",
                                "activated", "derived", "soft_step", "soft_ready", "hi_ready", "rest_ready", "mid_ready", "parts_ready",
                                "dt_step", "u_ready", "decay_ready", "spread", "taken", "fixed", "scanned", "halved", "quartered",
                                "y_done", "y_ready", "out_done", "out_copied"))
        LOADS = 16 * 16
        block = st.block()

        def jumps(t):
            return t.rearrange("p (r w) -> p r w", w=KEPT)[:, :, JUMP]

        @block.sync
        def _(sp):
            def load(c, s):
                for q in range(2):
                    sp.dma_start(xt[q * C:(q + 1) * C, s, 0:NA + 3], x2[:, bass.ds(c * NA + (PADX - 3 - q), NA + 3)]).then_inc(x_in[s], 16)

            def next_load(c, s, r):
                sp.wait_ge(projected, c + 1)
                load(c + UA, s)

            def store(c, s, r):
                sp.wait_ge(out_copied, c + 1)
                sp.dma_start(ys[:, bass.ds(c * NA, NA)], res[:, s % 4, :]).then_inc(stored[s % 4], 16)

            for dst, src in ((wi[:, :, :], w_in), (wc[:, :, :], w_conv), (wz[:, :], w_z), (cb[:, 0:1], conv_b), (cr[:, :], conv_row), (wxd[:, :], w_xd),
                             (wdt[:, :], w_dt), (db[:, 0:1], dt_b), (w96[:, :], w_bc3), (wb[:, :], w_b), (av[:, :], a_log),
                             (dd[:, :], skip_d), (wo[:, :], w_out), (sr[:, :], split_rows), (pk[:, :], pick), (idt[:, :], ident)):
                sp.dma_start(dst, src).then_inc(loaded, 16)
            for s in range(UA):
                load(s, s)
            @turns(sp, NC // UA - 1)
            def _(j):
                for s in range(UA):
                    next_load(j * UA + s, s, j)
                    store(j * UA + s, s, j)
            for s in range(UA):
                store(NC - UA + s, s, NC // UA - 1)
            for s in range(4):
                sp.wait_ge(stored[s], 16 * (NC // 4))

        @block.gpsimd
        def _(pool):
            nc.gpsimd.memset(hs[:, 1, :, NA - 1:NA], 0.0).then_inc(zeroed, 1)
            pool.wait_ge(zeroed, 1)
            nc.gpsimd.memset(fold60[:, :], float(STEADY)).then_inc(zeroed, 1)
            pool.wait_ge(zeroed, 2)
            nc.gpsimd.memset(one[:, :], 1.0).then_inc(zeroed, 1)
            pool.wait_ge(zeroed, 3)
            pool.wait_ge(w_ready, 1)

            def silu(c, s, r):
                pool.wait_ge(sig_ready, c + 1)
                nc.gpsimd.tensor_tensor(xz[:, s], xz[:, s], sg[:, s % 2], ALU.mult).then_inc(activated, 1)

            def step_sizes(c, s, r):
                pool.wait_ge(soft_ready, c + 1)
                after(pool, decay_ready, (c - 1) * ST)
                d = dt[:, s % 2, :]
                nc.gpsimd.tensor_tensor(d, soft[:, s % 2, :], relu[:, s % 2, :], ALU.add).then_inc(dt_step, 1)
                after(pool, scanned, (c - 3) * ST)
                pool.wait_ge(dt_step, 2 * c + 1)
                pool.wait_ge(activated, c + 1)
                nc.gpsimd.tensor_tensor(u[:, s % 4, :], d, xz[:, s, 0, :], ALU.mult).then_inc(u_ready, 1)
                pool.wait_ge(u_ready, c + 1)
                nc.gpsimd.tensor_tensor(jumps(d), jumps(d), fold60[:, :], ALU.mult).then_inc(dt_step, 1)

            def remainder(c, s, r):
                pool.wait_ge(hi_ready, c + 1)
                nc.gpsimd.tensor_tensor(rest[:, s % 2, :], hi[:, s % 2, :], rest[:, s % 2, :], ALU.add).then_inc(rest_ready, 1)

            def split(c, s, r):
                pool.wait_ge(mid_ready, c + 1)
                after(pool, spread, (c - 3) * 16)
                nc.gpsimd.tensor_tensor(parts[:, s % 4, :], hi[:, s % 2, :], rest[:, s % 2, :], ALU.add).then_inc(parts_ready, 1)

            def fold(c, s, r):
                pool.wait_ge(taken, (c + 1) * 16)
                after(pool, quartered, c)
                nc.gpsimd.tensor_tensor(hh[:, :, :], hc[:, s % 2, 0:ST // 2, :], hc[:, s % 2, ST // 2:, :], ALU.add).then_inc(halved, 1)
                pool.wait_ge(halved, c + 1)
                after(pool, y_done, c - 1)
                nc.gpsimd.tensor_tensor(hq[:, s % 2], hh[:, 0:ST // 4, :], hh[:, ST // 4:, :], ALU.add).then_inc(quartered, 1)

            pipeline(pool, NC, UA, 4, (1, step_sizes), (1, remainder), (1, split), (0, silu), (4, fold))

        @block.tensor
        def _(pe):
            pe.wait_ge(loaded, LOADS)
            nc.tensor.matmul(p_s[0][:, 0, 0:128], wxd[:, :], wdt[:, :], start=True, stop=True).then_inc(setup_pe, 1)
            pe.wait_ge(step, 4)
            nc.tensor.matmul(p_s[1][:, 0, 0:2], wd[:, :], c0[:, 0:2], start=True, stop=True).then_inc(setup_pe, 1)
            nc.tensor.matmul(p_s[1][:, 1, 0:ST], xrep[:, :], wb[:, :], start=True, stop=True).then_inc(setup_pe, 1)
            pe.wait_ge(w_ready, 1)
            pe.wait_ge(zeroed, 3)

            def project(part):
                def run(c, s, r):
                    if part == 0:
                        pe.wait_ge(x_in[s], 32 * r + 32)
                        after(pe, hi_ready, c)
                        after(pe, soft_ready, c)
                        nc.tensor.matmul(p_x[:, 0, 0:NA], wi[:, 0, :], xt[:, s, 3:3 + NA], start=True, stop=False)
                    elif part == 1:
                        nc.tensor.matmul(p_x[:, 0, 0:NA], wi[:, 1, :], xt[:, s, 1:1 + NA], start=False, stop=False)
                    elif part == 2:
                        nc.tensor.matmul(p_x[:, 0, 0:NA], cr[:, :], one[:, :], start=False, stop=True)
                    else:
                        nc.tensor.matmul(p_x[:, 1, 0:NA], wz[:, :], xt[0:C, s, 3:3 + NA], start=True, stop=True).then_inc(projected, 1)
                return run

            def derive(c, s, r):
                pe.wait_ge(activated, c + 1)
                nc.tensor.matmul(p_x[:, 1, 0:NA], wd[:, :], xz[:, s, 0, :], start=True, stop=True).then_inc(derived, 1)
                nc.tensor.matmul(p_x[0:96, 0, 0:NA], w96[:, :], xz[:, s, 0, :], start=True, stop=True).then_inc(derived, 1)

            def spread_part(p, pair):
                q, g = SPREAD[p]

                def run(c, s, r):
                    if p == 0 and pair == 0:
                        pe.wait_ge(parts_ready, c + 1)
                    after(pe, taken, c * 16 + (2 * p + pair - 1))
                    for k in range(2):
                        mm = nc.tensor.matmul(p_s[pair][:, k, 0:NA], sel[:, q * ST + g * SG + 2 * pair + k, :], parts[:, s % 4, :],
                                              start=True, stop=True)
                    mm.then_inc(spread, 1)
                return run

            def total(part):
                def run(c, s, r):
                    if part == 0:
                        pe.wait_ge(quartered, c + 1)
                        after(pe, y_ready, c)
                        nc.tensor.matmul(p_y[:, 0:NA], dg[:, :], xz[:, s, 0, :], start=True, stop=False)
                        return
                    mm = nc.tensor.matmul(p_y[:, 0:NA], idt[:, :], hq[:, s % 2, part - 1, :], start=False, stop=(part == ST // 4))
                    if part == ST // 4:
                        mm.then_inc(y_done, 1)
                return run

            def project_out(c, s, r):
                pe.wait_ge(y_ready, c + 1)
                after(pe, out_copied, c)
                nc.tensor.matmul(p_o[:, 0:NA], wo[:, :], y2[:, s % 2, :], start=True, stop=True).then_inc(out_done, 1)

            after_pair = {
                       1: [(6, project_out)],
                       3: [(0, project(0)), (0, project(1))],
                       5: [(0, project(2))],
                       7: [(0, project(3)), (5, total(0))],
                       9: [(5, total(1))],
                       11: [(5, total(2)), (5, total(3))],
                       13: [(5, total(4))],
            }
            order = [(1, derive)]
            for i in range(16):
                order.append((3, spread_part(i // 2, i % 2)))
                order += after_pair.get(i, [])
            pipeline(pe, NC, UA, 6, *order)

        @block.scalar
        def _(act):
            act.wait_ge(loaded, LOADS)
            act.preload_act_table_set("natural_log_exp_and_others")
            seen = [0]

            def link(ins):
                seen[0] += 1
                ins.then_inc(setup_act, 1)
                act.wait_ge(setup_act, seen[0])

            link(nc.scalar.activation(av[:, :], av[:, :], ACT.Exp))
            act.wait_ge(step, 1)
            link(nc.scalar.activation(c0[:, 2:3], cb[:, 1:2], ACT.Exp))
            link(nc.scalar.activation(c0[:, 2:3], c0[:, 2:3], ACT.Ln, bias=1.0))
            link(nc.scalar.activation(c0[:, 2:3], c0[:, 2:3], ACT.Exp, scale=-1.0))
            act.wait_ge(setup_pe, 2)
            nc.scalar.activation(c0[:, 4:5], p_s[1][:, 0, 0:1], ACT.Relu, bias=db[:, 0:1])
            link(nc.scalar.activation(c0[:, 5:6], p_s[1][:, 0, 0:1], ACT.Abs, bias=db[:, 0:1]))
            link(nc.scalar.activation(c0[:, 5:6], c0[:, 5:6], ACT.Exp, scale=-1.0))
            link(nc.scalar.activation(c0[:, 5:6], c0[:, 5:6], ACT.Ln, bias=1.0))
            act.wait_ge(step, 6)
            link(nc.scalar.activation(a0[:, :], av[:, :], ACT.Exp, scale=c0[:, 6:7]))
            act.wait_ge(w_ready, 1)

            def sigmoid(c, s, r):
                act.wait_ge(projected, c + 1)
                after(act, activated, c - 1)
                t = sg[:, s % 2].rearrange("p q n -> p (q n)")
                after(act, y_ready, c - UA + 1)
                nc.scalar.activation(xz[:, s], p_x[:, :, 0:NA], ACT.Copy)
                nc.scalar.activation(sg[:, s % 2], p_x[:, :, 0:NA], ACT.Exp, scale=-1.0).then_inc(sig_step, 1)
                act.wait_ge(sig_step, 2 * c + 1)
                nc.scalar.activation(t, t, ACT.Ln, bias=1.0).then_inc(sig_step, 1)
                act.wait_ge(sig_step, 2 * c + 2)
                nc.scalar.activation(t, t, ACT.Exp, scale=-1.0).then_inc(sig_ready, 1)

            def softplus(c, s, r):
                act.wait_ge(derived, 2 * c + 1)
                after(act, dt_step, 2 * (c - 1))
                t = soft[:, s % 2, :]
                nc.scalar.activation(t, p_x[:, 1, 0:NA], ACT.Abs, bias=db[:, 0:1]).then_inc(soft_step, 1)
                nc.scalar.activation(relu[:, s % 2, :], p_x[:, 1, 0:NA], ACT.Relu, bias=db[:, 0:1])
                act.wait_ge(soft_step, 2 * c + 1)
                nc.scalar.activation(t, t, ACT.Exp, scale=-1.0).then_inc(soft_step, 1)
                act.wait_ge(soft_step, 2 * c + 2)
                nc.scalar.activation(t, t, ACT.Ln, bias=1.0).then_inc(soft_ready, 1)

            def first_part(c, s, r):
                act.wait_ge(derived, 2 * c + 2)
                after(act, parts_ready, c - 1)
                nc.scalar.activation(rest[:, s % 2, :], p_x[0:96, 0, 0:NA], ACT.Copy)
                nc.scalar.activation(hi[:, s % 2, :], p_x[0:96, 0, 0:NA], ACT.Identity, scale=sr[:, 0:1]).then_inc(hi_ready, 1)

            def second_part(c, s, r):
                act.wait_ge(rest_ready, c + 1)
                nc.scalar.activation(hi[:, s % 2, :], rest[:, s % 2, :], ACT.Identity, scale=sr[:, 1:2]).then_inc(mid_ready, 1)

            def decay(c, s, r):
                act.wait_ge(dt_step, 2 * c + 2)
                after(act, scanned, (c - 1) * ST)
                for k in range(ST):
                    nc.scalar.activation(da[:, s % 2, k, :], dt[:, s % 2, :], ACT.Exp, scale=av[:, k:k + 1]).then_inc(decay_ready, 1)

            def copy_out(c, s, r):
                act.wait_ge(out_done, c + 1)
                if isinstance(r, int):
                    after(act, stored[s % 4], 16 * (c // 4))
                else:
                    act.wait_ge(stored[s % 4], 32 * r + 16 * (s // 4))
                nc.scalar.activation(res[:, s % 4, :], p_o[:, 0:NA], ACT.Copy).then_inc(out_copied, 1)

            pipeline(act, NC, UA, 6, (1, softplus), (1, first_part), (6, copy_out), (1, second_part), (0, sigmoid), (2, decay))

        @block.vector
        def _(dve):
            seen = [0]

            def link(ins):
                seen[0] += 1
                ins.then_inc(step, 1)
                dve.wait_ge(step, seen[0])

            dve.wait_ge(loaded, LOADS)
            link(nc.vector.tensor_scalar(cb[:, 1:2], cb[:, 0:1], -1.0, None, ALU.mult))
            dve.wait_ge(setup_act, 4)
            link(nc.vector.tensor_tensor(c0[:, 0:2], cb[:, 0:1].broadcast_to([128, 2]), c0[:, 2:3].broadcast_to([128, 2]), ALU.mult))
            link(nc.vector.tensor_copy(xrep[:, :], c0[:, 0:1].broadcast_to([128, 128])))
            dve.wait_ge(setup_pe, 1)
            link(nc.vector.tensor_copy(wd[:, :], p_s[0][:, 0, 0:128]))
            link(nc.vector.tensor_scalar(av[:, :], av[:, :], -1.0, None, ALU.mult))
            dve.wait_ge(setup_act, 7)
            link(nc.vector.tensor_tensor(c0[:, 6:7], c0[:, 4:5], c0[:, 5:6], ALU.add))
            link(nc.vector.tensor_tensor(c0[:, 7:8], c0[:, 6:7], c0[:, 0:1], ALU.mult))
            dve.wait_ge(setup_pe, 3)
            link(nc.vector.tensor_scalar(b0[:, :], p_s[1][:, 1, 0:ST], c0[:, 7:8], None, ALU.mult))
            dve.wait_ge(setup_act, 8)
            link(nc.vector.tensor_copy(a60[:, :, :], a0[:, :].unsqueeze(2).broadcast_to([128, ST, STEADY])))
            link(nc.vector.tensor_copy(b60[:, :, :], b0[:, :].unsqueeze(2).broadcast_to([128, ST, STEADY])))
            link(nc.vector.memset(a60[:, :, 0:1], 0.0))
            link(nc.vector.tensor_tensor_scan(b60[:, :, :].rearrange("p s n -> p (s n)"), a60[:, :, :].rearrange("p s n -> p (s n)"),
                                              b60[:, :, :].rearrange("p s n -> p (s n)"), 0.0, ALU.mult, ALU.add))
            link(nc.vector.tensor_copy(jump[:, :], b60[:, :, STEADY - 1]))
            link(nc.vector.tensor_tensor(wi[:, :, :], wi[:, :, :], wc[:, :, :], ALU.mult))
            link(nc.vector.tensor_scalar(dg[:, :], idt[:, :], dd[:, 0:1], None, ALU.mult))
            nc.vector.tensor_copy(sel[:, :, :], pk[:, :].unsqueeze(2).broadcast_to([96, 2 * ST, 128])).then_inc(w_ready, 1)
            dve.wait_ge(w_ready, 1)
            dve.wait_ge(zeroed, 3)

            def main(c, s, r):
                dve.wait_ge(u_ready, c + 1)
                after(dve, halved, c - 1)
                n = c * 16
                for p, (q, g) in enumerate(SPREAD):
                    for pair in range(2):
                        dve.wait_ge(spread, n + 2 * p + pair + 1)
                        rows = p_s[pair][:, :, 0:NA]
                        i, k = g * SG + 2 * pair, g % 2 * SG + 2 * pair
                        if q == 0:
                            nc.vector.tensor_tensor(bx[:, k:k + 2, :], u[:, s % 4, :].unsqueeze(1).broadcast_to([128, 2, NA]), rows,
                                                    ALU.mult).then_inc(taken, 1)
                        else:
                            dve.wait_ge(scanned, c * ST + i + 2)
                            nc.vector.tensor_tensor(hc[:, s % 2, i:i + 2, :], hs[:, s % 2, i:i + 2, :], rows, ALU.mult).then_inc(taken, 1)
                    due = {0: 0, 2: 1, 4: 2, 6: 3}.get(p)
                    if due is not None:
                        b = bx[:, due % 2 * SG:(due % 2 + 1) * SG, :]
                        dve.wait_ge(taken, n + 2 * (SPREAD.index((0, due)) + 1))
                        nc.vector.tensor_copy(b.rearrange("p k (r w) -> p k r w", w=KEPT)[:, :, :, JUMP],
                                              jump[:, due * SG:(due + 1) * SG].unsqueeze(2).broadcast_to([128, SG, RA])).then_inc(fixed, 1)
                        dve.wait_ge(fixed, c * 4 + due + 1)
                        if due == 0:
                            dve.wait_ge(decay_ready, (c + 1) * ST)
                        for k in range(SG):
                            i = due * SG + k
                            nc.vector.tensor_tensor_scan(hs[:, s % 2, i, :], da[:, s % 2, i, :], b[:, k, :],
                                                         hs[:, (s + 1) % 2, i, NA - 1:NA], ALU.mult, ALU.add).then_inc(scanned, 1)

            def gate(c, s, r):
                dve.wait_ge(y_done, c + 1)
                after(dve, out_done, c - 1)
                nc.vector.tensor_tensor(y2[:, s % 2, :], p_y[:, 0:NA], xz[:, s, 1, :], ALU.mult).then_inc(y_ready, 1)

            pipeline(dve, NC, UA, 5, (3, main), (5, gate))


NR = 16
BN = 368


def merge_branches(nc, ys, ye, x2, gmat, gwb, att, out):
    K = H * KEPT
    NS = H // NR // 2
    N = NR * KEPT
    L, LR = JUMP + 1, KEPT - JUMP - 1
    with Stage(nc, "merge") as st:
        v = [st.sb(f"v{q}", [128, 2, K]) for q in range(2)]
        xs = st.sb("xs", [128, 2, N])
        t1 = st.sb("t1", [128, 2, N])
        t2 = st.sb("t2", [128, 2, N])
        tx = st.sb("tx", [128, N])
        os = st.sb("os", [128, 2, NR, W])
        gm = st.sb("gm", [128, 128])
        gw = st.sb("gw", [128, 2, 2])
        at = st.sb("at", [128, 8])
        bs = st.sb("bs", [128, 4, K // BN, 6])
        mv = st.sb("mv", [128, 4, 2])
        g = st.sb("g", [128, 2, 4])
        grp = st.sb("grp", [128, 2, 4])
        var = st.sb("var", [128, 4])
        std = st.sb("std", [128, 4])
        sh = st.sb("sh", [128, 2, 2, 2])
        zs = st.sb("zs", [128, 2, 2])
        zv = st.sb("zv", [128, 2])
        p_g = st.ps("p_g", [128, 8])
        loaded, step, sums_ready, grouped, ab_ready, const_ready = (
            st.sem(n) for n in ("loaded", "step", "sums_ready", "grouped", "ab_ready", "const_ready"))
        max_ready, raised, var_ready, rooted, zero_act = (st.sem(n) for n in ("max_ready", "raised", "var_ready", "rooted", "zero_act"))
        counted = st.sem("counted")
        v_in = [st.sem(f"v_in{i}") for i in range(4)]
        x_in, filled, silu_ready, x_scaled, added, merged, stored = (st.sem2(n) for n in (
            "x_in", "filled", "silu_ready", "x_scaled", "added", "merged", "stored"))
        ov = out.rearrange("(a p) c h w -> (p c) a h w", a=2)
        block = st.block()

        @block.sync
        def _(sp):
            for dst, src in ((gm[:, :], gmat), (gw[:, :, :], gwb), (at[:, 0:2], att)):
                sp.dma_start(dst, src).then_inc(loaded, 16)
            for q, src in enumerate((ys, ye)):
                for a in range(2):
                    for p in range(2):
                        sp.dma_start(v[q][64 * p:64 * p + 64, a, :], src[:, (2 * a + p) * K:(2 * a + p + 1) * K]).then_inc(v_in[2 * q + a], 16)
            for a in range(2):
                @turns(sp, NS)
                def _(j):
                    for s in range(2):
                        sp.wait_ge(x_scaled[s], a * NS + j)
                        for p in range(2):
                            sp.dma_start(xs[64 * p:64 * p + 64, s, :], x2[:, bass.ds((2 * j + s) * N + (PADX + (2 * a + p) * K), N)])\
                                .then_inc(x_in[s], 16)
                    for s in range(2):
                        sp.wait_ge(merged[s], a * NS + j + 1)
                        sp.wait_ge(filled[s], a * NS + j + 1)
                        sp.dma_start(ov[:, a, bass.ds((2 * j + s) * NR, NR), :], os[:, s]).then_inc(stored[s], 16)
            for s in range(2):
                sp.wait_ge(stored[s], 32 * NS)

        @block.scalar
        def _(act):
            act.wait_ge(max_ready, 1)
            nc.scalar.activation(at[:, 3:5], at[:, 0:2], ACT.Exp, bias=at[:, 2:3]).then_inc(raised, 1)
            act.wait_ge(var_ready, 1)
            nc.scalar.activation(std[:, :], var[:, :], ACT.Sqrt).then_inc(rooted, 1)
            act.wait_ge(ab_ready, 1)
            nc.scalar.activation(zs[:, :, :], sh[:, 1], ACT.Silu).then_inc(zero_act, 1)
            act.wait_ge(const_ready, 1)
            for a in range(2):
                @turns(act, NS)
                def _(j):
                    for s in range(2):
                        act.wait_ge(merged[s], a * NS + j)
                        for q, t in enumerate((t1, t2)):
                            nc.scalar.activation(t[:, s, :], v[q][:, a, bass.ds((2 * j + s) * N, N)], ACT.Silu,
                                                 scale=sh[:, 0, q, a:a + 1], bias=sh[:, 1, q, a:a + 1]).then_inc(silu_ready[s], 1)
                        act.wait_ge(stored[s], 16 * (a * NS) + 16 * j)
                        nc.scalar.activation(os[:, s, :, L:W - LR], zv[:, a:a + 1].unsqueeze(2).broadcast_to([128, NR, W - LR - L]),
                                             ACT.Copy).then_inc(filled[s], 1)

        @block.tensor
        def _(pe):
            pe.wait_ge(loaded, 48)
            pe.wait_ge(sums_ready, 1)
            nc.tensor.matmul(p_g[:, 0:8], gm[:, :], g[:, :, :].rearrange("p a b -> p (a b)"), start=True, stop=True).then_inc(grouped, 1)

        @block.vector
        def _(dve):
            seen = [0]

            def link(ins):
                seen[0] += 1
                ins.then_inc(step, 1)
                dve.wait_ge(step, seen[0])

            dve.wait_ge(loaded, 48)
            link(nc.vector.tensor_reduce(at[:, 2:3], at[:, 0:2], AX.X, ALU.max))
            nc.vector.tensor_scalar(at[:, 2:3], at[:, 2:3], -1.0, None, ALU.mult).then_inc(max_ready, 1)
            dve.wait_ge(raised, 1)
            link(nc.vector.tensor_reduce(at[:, 5:6], at[:, 3:5], AX.X, ALU.add))
            link(nc.vector.reciprocal(at[:, 5:6], at[:, 5:6]))
            link(nc.vector.tensor_scalar(at[:, 3:5], at[:, 3:5], at[:, 5:6], None, ALU.mult))
            link(nc.vector.tensor_reduce(at[:, 6:7], at[:, 3:5], AX.X, ALU.add))
            link(nc.vector.tensor_scalar(at[:, 6:7], at[:, 6:7], 1.0, None, ALU.add))
            for i in range(4):
                dve.wait_ge(v_in[i], 32)
                @turns(dve, K // BN)
                def _(j):
                    nc.vector.bn_stats(bs[:, i, bass.ds(j, 1), :].rearrange("p m s -> p (m s)"), v[i // 2][:, i % 2, bass.ds(j * BN, BN)])\
                        .then_inc(counted, 1)
            dve.wait_ge(counted, 4 * (K // BN))
            for i in range(4):
                last = nc.vector.bn_aggr(mv[:, i, :], bs[:, i].rearrange("p m s -> p (m s)"))
            link(last)
            r = K / HW
            link(nc.vector.tensor_tensor(g[:, 1, :], mv[:, :, 0], mv[:, :, 0], ALU.mult))
            link(nc.vector.tensor_tensor(g[:, 1, :], g[:, 1, :], mv[:, :, 1], ALU.add))
            link(nc.vector.tensor_scalar(g[:, 1, :], g[:, 1, :], r, None, ALU.mult))
            nc.vector.tensor_scalar(g[:, 0, :], mv[:, :, 0], r, None, ALU.mult).then_inc(sums_ready, 1)
            dve.wait_ge(grouped, 1)
            link(nc.vector.tensor_copy(grp[:, :, :], p_g[:, 0:8].rearrange("p (a b) -> p a b", a=2)))
            link(nc.vector.tensor_tensor(var[:, :], grp[:, 0, :], grp[:, 0, :], ALU.mult))
            link(nc.vector.tensor_tensor(var[:, :], grp[:, 1, :], var[:, :], ALU.subtract))
            nc.vector.tensor_scalar(var[:, :], var[:, :], 0.0, EPS, ALU.max, ALU.add).then_inc(var_ready, 1)
            dve.wait_ge(rooted, 1)
            link(nc.vector.reciprocal(var[:, :], std[:, :]))
            for q in range(2):
                link(nc.vector.tensor_scalar(sh[:, 0, q, :], var[:, 2 * q:2 * q + 2], gw[:, q, 0:1], None, ALU.mult))
                link(nc.vector.tensor_tensor(sh[:, 1, q, :], grp[:, 0, 2 * q:2 * q + 2], sh[:, 0, q, :], ALU.mult))
                link(nc.vector.tensor_scalar(sh[:, 1, q, :], sh[:, 1, q, :], -1.0, gw[:, q, 1:2], ALU.mult, ALU.add))
            dve.sem_inc(ab_ready, 1)
            dve.wait_ge(zero_act, 1)
            link(nc.vector.tensor_scalar(zv[:, :], zs[:, 0, :], at[:, 3:4], None, ALU.mult))
            nc.vector.scalar_tensor_tensor(zv[:, :], zs[:, 1, :], at[:, 4:5], zv[:, :], ALU.mult, ALU.add).then_inc(const_ready, 1)
            for a in range(2):
                @turns(dve, NS)
                def _(j):
                    for s in range(2):
                        dve.wait_ge(x_in[s], 32 * (a * NS) + 32 * j + 32)
                        dve.wait_ge(merged[1 - s], a * NS + j + s)
                        nc.vector.tensor_scalar(tx[:, :], xs[:, s, :], at[:, 6:7], None, ALU.mult).then_inc(x_scaled[s], 1)
                        dve.wait_ge(silu_ready[s], 2 * (a * NS) + 2 * j + 2)
                        dve.wait_ge(x_scaled[s], a * NS + j + 1)
                        nc.vector.scalar_tensor_tensor(tx[:, :], t1[:, s, :], at[:, 3:4], tx[:, :], ALU.mult, ALU.add).then_inc(added[s], 1)
                        dve.wait_ge(added[s], a * NS + j + 1)
                        dve.wait_ge(stored[s], 16 * (a * NS) + 16 * j)
                        tv = tx[:, :].rearrange("p (r w) -> p r w", w=KEPT)
                        sv = t2[:, s, :].rearrange("p (r w) -> p r w", w=KEPT)
                        nc.vector.scalar_tensor_tensor(os[:, s, :, 0:L], sv[:, :, 0:L], at[:, 4:5], tv[:, :, 0:L], ALU.mult, ALU.add)
                        nc.vector.scalar_tensor_tensor(os[:, s, :, W - LR:W], sv[:, :, L:KEPT], at[:, 4:5], tv[:, :, L:KEPT], ALU.mult,
                                                       ALU.add).then_inc(merged[s], 1)


def twice(a):
    r, c = a.shape
    out = np.zeros((2 * r, 2 * c), a.dtype)
    out[:r, :c] = a
    out[r:, c:] = a
    return out


def layer0_layouts(i):
    k = {}
    p = lambda n: np.asarray(i["L0_conv_" + n])
    dup = lambda a: np.concatenate([a, a], 0)
    k["fg1"], k["fg2"] = twice(p("fg_w1").T), twice(p("fg_w2").T)
    k["sr1"], k["sr2"] = p("sr1_w").transpose(1, 2, 3, 0), p("sr2_w").transpose(1, 2, 3, 0)
    k["srb"] = dup(np.stack([p("sr1_b"), p("sr2_b")], 1))
    k["ln"] = dup(np.stack([p("ln1_g"), p("ln1_b"), p("ln2_g"), p("ln2_b")], 1))
    wk = np.zeros((2, 64, 2, 2, NH, 6, HD), np.float32)
    bk = np.zeros((6, HD, 2, NH), np.float32)
    for n in range(2):
        for q in range(2):
            wk[q, :, n, q] = p(f"kv{n + 1}_w")[:, :C].reshape(C, NH, 1, HD)
        bk[:, :, n] = p(f"kv{n + 1}_b")[:C].reshape(NH, HD).T
    k["wk"] = wk.reshape(128, 2, 2, NH, NB)
    k["bk"] = bk.reshape(NB, 2, NH)
    k["wq"] = twice(p("q_w"))
    k["bq"] = dup(p("q_b")[:, None])
    wp = np.zeros((NH, 32, C), np.float32)
    wp[:, :HD] = p("proj_w").reshape(NH, HD, C)
    k["wp"] = wp.reshape(128, C)
    k["bp"] = p("proj_b")[:, None]
    k["wv"] = np.stack([twice(p(f"kv{n}_w")[:, C:]) for n in (1, 2)], 1)
    k["dwv"] = dup(np.concatenate([p("dw_w").reshape(C, 9), p("kv1_b")[C:, None], p("kv2_b")[C:, None]], 1))
    return {n: np.ascontiguousarray(v) for n, v in k.items()}


def layer1_layouts(i):
    k = {}
    p = lambda n: np.asarray(i["L1_conv_" + n])
    dup = lambda a: np.concatenate([a, a], 0)
    for n in (1, 2):
        k[f"gn{n}"] = dup(np.stack([p(f"gn{n}_w"), p(f"gn{n}_b")], 1))
        w = p(f"afno_w{n}")
        m = np.zeros((2, 4, 16, 2, 4, 16), np.float32)
        for q in range(4):
            m[0, q, :, 0, q] = m[1, q, :, 1, q] = w[0, q]
            m[0, q, :, 1, q] = m[1, q, :, 0, q] = w[1, q]
        k[f"afno{n}"] = m.reshape(128, 128)
    k["afnob"] = np.stack([p("afno_b1").reshape(128), p("afno_b2").reshape(128)], 1)
    g1 = np.zeros((2, 64, 2, 128), np.float32)
    g1[0, :, 0] = g1[1, :, 1] = p("g1_w").T
    k["g1"] = g1.reshape(128, 2, 128)
    for n in (1, 2):
        k[f"bn{n}"] = np.stack([p(f"g{n}_b"), p(f"bn{n}_rm"), p(f"bn{n}_rv"), p(f"bn{n}_g"), p(f"bn{n}_b")], 1)
    k["ca1"], k["ca1b"], k["ca2"], k["ca2b"] = p("ca_w1").T, p("ca_b1")[:, None], p("ca_w2").T, p("ca_b2")[:, None]
    k["g2"], k["g3"], k["g3b"] = p("g2_w").T, p("g3_w").T, np.tile(p("g3_b"), (B, 1))
    k["ew"] = dup(p("expert_w").transpose(2, 1, 0))
    k["eb"] = dup(p("expert_b").T)
    k["sw"] = np.stack([twice(w.T) for w in p("shared_w")], 1)
    k["sb"] = dup(p("shared_b").T)
    k["few"], k["feb"] = twice(p("fe_w").T), dup(p("fe_b")[:, None])
    return {n: np.ascontiguousarray(v) for n, v in k.items()}


def layer2_layouts(i):
    w = np.asarray(i["L2_conv_w1"]).transpose(0, 3, 2, 1)
    n = -np.arange(M2) % M2
    return {"wm": np.ascontiguousarray(np.concatenate([w, w[:, n][:, :, n]], 0))}


def spectral_layouts(i):
    k = {}
    p = lambda n: np.asarray(i["L3_conv_spe_" + n])
    win, conv, xp, tok = p("in_w"), p("conv_w")[:, 0], p("xproj_w"), np.arange(TK)
    wi, wc = np.zeros((65, 2, DE, TK), np.float32), np.zeros((65, 2, DE, TK), np.float32)
    vi, vc = wi[:64].reshape(TK, CG, 2, DE, TK), wc[:64].reshape(TK, CG, 2, DE, TK)
    for t in range(TK):
        for tap in range(4):
            if t + tap - 3 >= 0:
                vi[t + tap - 3, :, 0, :, t] = win[:DE].T
                vc[t + tap - 3, :, 0, :, t] = conv[:, tap]
        vi[t, :, 1, :, t], vc[t, :, 1, :, t] = win[DE:].T, 1
    wi[64, 0], wc[64] = p("conv_b")[:, None], 1
    k["e_in"], k["e_conv"] = wi.reshape(65, -1), wc.reshape(65, -1)
    xd, dt = np.zeros((TK, DE, TK), np.float32), np.zeros((TK, DE, TK), np.float32)
    xd[tok, :, tok], dt[tok, :, tok] = xp[0], p("dt_w")[:, 0]
    k["e_xd"], k["e_dt"] = xd.reshape(TK, TD), dt.reshape(TK, TD)
    bc = np.zeros((DE, TK, 2, ST, TK), np.float32)
    for t in range(TK):
        bc[:, t, :, :, t] = xp[1:].T.reshape(DE, 2, ST)
    k["e_bc"] = bc.reshape(TD, 2 * TD)
    k["e_row"] = np.repeat(p("dt_b"), TK)[None]
    k["e_d"] = np.repeat(p("D"), TK)[:, None]
    k["e_alog"] = np.tile(p("A_log"), (128, 1, 1))
    wo = np.zeros((DE, TK, TK, CG), np.float32)
    for t in range(TK):
        wo[:, t, t] = p("out_w").T
    k["e_out"] = wo.reshape(TD, C)
    return {n: np.ascontiguousarray(v) for n, v in k.items()}


def spatial_layouts(i):
    k = {}
    p = lambda n: np.asarray(i["L3_conv_spa_" + n])
    win, conv, xp = p("in_w"), p("conv_w")[:, 0], p("xproj_w")
    wi, wc = np.zeros((2, C, 2, 128), np.float32), np.zeros((2, C, 2, 128), np.float32)
    for q in range(2):
        for m in range(2):
            wi[q, :, m] = win[:128].T
            wc[q, :, m] = conv[:, 3 - 2 * m - q]
    k["a_in"], k["a_conv"] = wi.reshape(128, 2, 128), wc.reshape(128, 2, 128)
    k["a_z"], k["a_cb"] = win[128:].T, p("conv_b")[:, None]
    k["a_cr"] = p("conv_b")[None]
    k["a_xd"], k["a_dt"], k["a_dtb"] = xp[:4], p("dt_w").T, p("dt_b")[:, None]
    k["a_bc3"], k["a_b"] = np.tile(xp[4:].T, (1, 3)), xp[4:4 + ST].T
    k["a_alog"], k["a_d"], k["a_out"] = p("A_log"), p("D")[:, None], p("out_w").T
    return {n: np.ascontiguousarray(v) for n, v in k.items()}


def merge_layouts(i):
    p = lambda n: np.asarray(i["L3_conv_" + n])
    gw = np.stack([np.stack([p(f"{q}_gn_w"), p(f"{q}_gn_b")], 1) for q in ("spa", "spe")], 1)
    return {"m_gn": np.concatenate([gw, gw], 0), "m_att": np.tile(p("att_w"), (128, 1))}


def smoothing(n):
    k = np.exp(-0.5 * np.arange(-4, 5, dtype=np.float32) ** 2)
    k = k / k.sum()
    m = np.zeros((n, n))
    for r in range(n):
        for t in range(9):
            m[r, min(max(r + t - 4, 0), n - 1)] += k[t]
    return m


def of_two_images(m):
    out = np.zeros((2, 2, MD, 2, m.shape[1]))
    for i in range(2):
        out[:, i, :, i] = m.reshape(2, MD, -1)
    return out.reshape(4 * MD, 2, -1)


def shape_constants():
    k = {}
    a = 2 * np.pi * np.outer(np.arange(128), np.arange(128)) / 128
    co, si = np.cos(a), np.sin(a)
    k["c_h"] = np.concatenate([co, si], 1)
    cw, sw = co[:, :WF] / 128, si[:, :WF] / 128
    k["c_w"] = np.stack([np.concatenate([cw, -sw], 1), np.concatenate([-sw, -cw], 1)], 1)
    k["c_k"] = np.stack([np.concatenate([co, si], 1), np.concatenate([-si, co], 1)], 1)
    al = np.where((np.arange(WF) == 0) | (np.arange(WF) == W // 2), 1.0, 2.0)[:, None] / 128
    k["c_f"] = np.stack([al * co[:WF], -al * si[:WF]], 1)
    k["c_h32"] = np.concatenate([co[:, :MD], si[:, :MD]], 1)
    c2, s2 = co[:, :MD] / 128, si[:, :MD] / 128
    k["c_w32"] = np.stack([np.concatenate([c2, -s2], 1), np.concatenate([-s2, -c2], 1)], 1)
    k["c_k32"] = np.stack([np.concatenate([co[:MD], -si[:MD]], 0), np.concatenate([si[:MD], co[:MD]], 0)], 1)
    k["c_m32"] = of_two_images(np.concatenate([al[:MD] * co[:MD], -al[:MD] * si[:MD]], 0))
    k["c_w2"] = k["c_w32"] * 128
    d = 2 * np.pi * np.add.outer(np.arange(M2), np.arange(M2)) / 128
    k["t_re"], k["t_im"] = np.tile(1 - np.sin(d), (128, 1, 1)), np.tile(np.cos(d), (128, 1, 1))
    s = 0.5 / HW
    k["half"] = np.stack([np.repeat([1, -1], 64), np.repeat([s, -s], 64)], 1)
    bc, bb = smoothing(C), smoothing(B)
    k["mixc"] = np.stack([np.concatenate([bc.T, bc.T], 1) * bb[r, q] for r in range(B) for q in range(B)], 1)
    rs, cs = smoothing(H) @ co[:, :MD], smoothing(H) @ si[:, :MD]
    k["c_k2"] = np.stack([np.concatenate([rs.T, cs.T], 0), np.concatenate([-cs.T, rs.T], 0)], 1)
    keep = np.abs(np.fft.fftfreq(W)) <= 0.25
    both = np.concatenate([rs.T, cs.T], 0) * keep
    k["c_m2"] = of_two_images(np.concatenate([both[:, :37], both[:, 96:]], 1))
    k["split_rows"] = np.stack([-np.repeat([0, 1, 1], 32), -np.repeat([0, 0, 1], 32)], 1)
    k["pick"] = np.tile(np.eye(32), (3, 1))
    k["groups16"] = np.kron(np.eye(8), np.full((16, 16), 1 / 16))
    k["groups8"] = np.kron(np.eye(16), np.full((8, 8), 1 / 8))
    sg = np.ones((128, 128))
    sg[64:, :64] = -1
    k["sign"] = sg
    k["before"] = np.tile(np.tril(np.ones((NE, NE)), -1), (B, 1, 1))
    k["ident"] = np.eye(128)
    dsel = np.zeros((NH, 32, NH, 32))
    for h in range(NH):
        dsel[h, HD, h, :] = 1
    k["dsel"] = dsel.reshape(128, 128)
    part = np.repeat([1, 2, 1, 2, 3, 1], HD)
    k["part_rows"] = np.stack([-(part >= 2).astype(np.float32), -(part >= 3).astype(np.float32)], 1)
    return {n: np.ascontiguousarray(v, dtype=np.float32) for n, v in k.items()}


SCRATCH = {
    "spec": (B * C, H, 2 * WF), "power": (B * C, H, WF), "gate": (B * C, H, WF), "xf": (B, C, H, W), "xs": (128, 2, 320),
    "kd": (B, 99, 1280, BF16), "vd": (B, 128, VC), "qp": (3, B, C, HW, BF16), "x1": (B, C, H, W), "st1": (B, C, 32, 6),
    "low1": (2 * MD, B * C, MD), "modes1": (2, B, C, MD, MD), "ab1": (C, 2, B), "y1": (B * C, H, W), "feats": (128, 2, HW),
    "fmean": (128, 2), "sel": (B, TOP, NE), "wts": (B, TOP), "out1": (B, C, H, W), "low2": (2 * MD, B * C, MD),
    "modes2": (2, B, C, M2 + 1, M2 + 1), "x2": (C, PADX + LX), "ys": (C, LX), "ye": (C, LX),
}


def layouts(i):
    k = {}
    for part in (layer0_layouts(i), layer1_layouts(i), layer2_layouts(i), spatial_layouts(i), spectral_layouts(i), merge_layouts(i),
                 shape_constants()):
        k.update(part)
    return k


def build(nc, t, out):
    for name, shape in SCRATCH.items():
        dt = F32
        if not isinstance(shape[-1], int):
            shape, dt = shape[:-1], shape[-1]
        t[name] = nc.dram_tensor(f"scratch_{name}", shape, dt, kind="Internal").ap()

    def of(names):
        return [t[n] for n in names.split()]

    spectrum(nc, *of("x c_h c_w spec power"))
    frequency_gate(nc, *of("power fg1 fg2 gate"))
    gated_inverse(nc, *of("x spec gate c_k c_f xf"))
    patch_convolutions(nc, *of("xf sr1 sr2 srb xs"))
    keys_and_values(nc, *of("xs ident ln wk bk part_rows wv dwv kd vd"))
    query_parts(nc, *of("xf wq bq qp"))
    attention(nc, *of("x qp kd vd ident dsel wp bp x1 st1"))
    low_spectrum(nc, "low1", *of("x1 c_h32 c_w32 low1"))
    fourier_mlp(nc, *of("low1 st1 groups8 gn1 sign afno1 afno2 afnob modes1 ab1"))
    low_inverse(nc, "inv1", t["modes1"], MD, *of("c_k32 c_m32"), t["y1"].rearrange("(b c) h w -> h b c w", b=B))
    with nc.sbuf_tensor("hr", [128, 2, HW], F32) as hr:
        with nc.sbuf_tensor("st2", [128, 2, 32, 6], F32) as st2:
            second_residual(nc, *of("x1 y1 ab1"), hr, st2)
            features(nc, hr, st2, *of("groups8 gn2 few feb feats fmean"))
        routing(nc, *of("fmean g1 bn1 ca1 ca1b ca2 ca2b g2 bn2 g3 g3b before sel wts"))
        experts(nc, hr, *of("feats sel wts ew eb sw sb out1"))
    low_spectrum(nc, "low2", *of("out1 c_h32 c_w2 low2"))
    hartley_modes(nc, *of("low2 t_re t_im half wm mixc modes2 x2"))
    low_inverse(nc, "inv2", t["modes2"], M2 + 1, *of("c_k2 c_m2"), t["x2"][:, PADX:].rearrange("c (b h w) -> h b c w", b=B, h=H))
    spatial_mamba(nc, *of("x2 a_in a_conv a_z a_cb a_cr a_xd a_dt a_dtb a_bc3 a_b a_alog a_d a_out split_rows pick ident ys"))
    spectral_mamba(nc, *of("x2 e_in e_conv e_xd e_dt e_bc e_row e_d e_alog e_out ident ye"))
    merge_branches(nc, *of("ys ye x2 groups16 m_gn m_att"), out)


def kernel(**inputs):
    import concourse.bacc as bacc
    from concourse.bass_utils import run_bass_kernel_spmd

    nc = bacc.Bacc("TRN2", target_bir_lowering=False, num_devices=1)
    arrays, t = {}, {}
    for name, a in {"x": np.ascontiguousarray(inputs["x"]), **layouts(inputs)}.items():
        arrays[f"in_{name}_dram"] = a
        t[name] = nc.dram_tensor(f"in_{name}_dram", a.shape, mybir.dt.from_np(a.dtype), kind="ExternalInput").ap()
    out = nc.dram_tensor("out_0_dram", (B, C, H, W), F32, kind="ExternalOutput").ap()
    build(nc, t, out)
    r = run_bass_kernel_spmd(nc, [arrays], core_ids=[0])
    return r.results[0]["out_0_dram"]
```
